# Optimizing a Trainium2 kernel written in Bass

```python
import numpy as np
import jax
import jax.numpy as jnp

def _softmax(x, axis=-1):
    return jax.nn.softmax(x, axis=axis)

def _gelu(x):
    return jax.nn.gelu(x, approximate=True)

def _silu(x):
    return jax.nn.silu(x)

def _sigmoid(x):
    return jax.nn.sigmoid(x)

def _layernorm(x, axis=-1, eps=1e-05):
    m = jnp.mean(x, axis=axis, keepdims=True)
    v = jnp.var(x, axis=axis, keepdims=True)
    return (x - m) / jnp.sqrt(v + eps)

def _scatter_add(tgt, idx, src, axis=0):
    return tgt.at[idx].add(src)

def _segment_sum(src, seg, n):
    return jax.ops.segment_sum(src, seg, n)
kernel_name = 'mk_hybrid_d2_jaxref_r8_0025a0'

def setup_inputs(seed: int=0):
    np.random.seed(seed)
    _w = jnp.asarray

    def _L0_attn_a_setup():
        import jax, jax.numpy as jnp
        import numpy as np
        EPS = 1e-06
        NUM_HEADS = 16

        def _phi(x):
            return jax.nn.elu(x) + 1.0
        key = jax.random.key(seed)
        ks = jax.random.split(key, 5)
        B, S, D = (2, 256, 128)
        scale = 1.0 / np.sqrt(D)
        return {'x': jax.random.normal(ks[0], (B, S, D), dtype=jnp.float32), 'Wq': jax.random.normal(ks[1], (D, D), dtype=jnp.float32) * scale, 'bq': jnp.zeros((D,), dtype=jnp.float32), 'Wk': jax.random.normal(ks[2], (D, D), dtype=jnp.float32) * scale, 'bk': jnp.zeros((D,), dtype=jnp.float32), 'Wv': jax.random.normal(ks[3], (D, D), dtype=jnp.float32) * scale, 'bv': jnp.zeros((D,), dtype=jnp.float32), 'Wo': jax.random.normal(ks[4], (D, D), dtype=jnp.float32) * scale, 'bo': jnp.zeros((D,), dtype=jnp.float32)}
    _L0_attn_a_in = _L0_attn_a_setup()

    def _L0_attn_b_setup():
        import jax, jax.numpy as jnp
        import numpy as np
        import math
        N_HEAD = 16
        V_HEAD = 32
        NOPE = 32
        ROPE_D = 64
        KEEP = 32
        EPS = 1e-06

        def _freqs(T, dim=ROPE_D, theta=10000.0):
            f = 1.0 / theta ** (jnp.arange(0, dim, 2, dtype=jnp.float32) / dim)
            t = jnp.arange(T, dtype=jnp.float32)
            a = jnp.outer(t, f)
            return (jnp.cos(a), jnp.sin(a))

        def _rope(x, cos, sin):
            S = x.shape[-2]
            c = cos[:S][None, None]
            s = sin[:S][None, None]
            x1, x2 = jnp.split(x, 2, axis=-1)
            return jnp.concatenate([x1 * c - x2 * s, x1 * s + x2 * c], axis=-1)

        def _rms(x, g, eps=EPS):
            return x * jax.lax.rsqrt(jnp.mean(x * x, axis=-1, keepdims=True) + eps) * g

        def _attn(q, k, v, causal):
            scale = 1.0 / math.sqrt(q.shape[-1])
            s = jnp.einsum('bhqd,bhkd->bhqk', q, k) * scale
            if causal:
                Tq, Tk = (s.shape[-2], s.shape[-1])
                mask = jnp.tril(jnp.ones((Tq, Tk), dtype=bool))
                s = jnp.where(mask, s, jnp.finfo(s.dtype).min)
            return jnp.einsum('bhqk,bhkd->bhqd', jax.nn.softmax(s, axis=-1), v)

        def _forward(x, w_cq, g_qnorm, w_dq_nope, w_dq_rope, w_ckv, g_kvnorm, w_dk_nope, w_dv, w_krope, w_imp, w_selk, w_selv, w_wink, w_winv, w_gate, w_proj):
            B, T, C = x.shape
            cos, sin = _freqs(T)
            nq = _rms(x @ w_cq, g_qnorm)
            q_nope = (nq @ w_dq_nope).reshape(B, T, N_HEAD, NOPE).transpose(0, 2, 1, 3)
            q_rope = (nq @ w_dq_rope).reshape(B, T, N_HEAD, ROPE_D).transpose(0, 2, 1, 3)
            q_rope = _rope(q_rope, cos, sin)
            q = jnp.concatenate([q_nope, q_rope], axis=-1)
            gate = jax.nn.softmax((x @ w_gate).mean(axis=1), axis=-1)
            ckv = _rms(x @ w_ckv, g_kvnorm)
            k_nope = (ckv @ w_dk_nope).reshape(B, T, N_HEAD, NOPE).transpose(0, 2, 1, 3)
            v1 = (ckv @ w_dv).reshape(B, T, N_HEAD, V_HEAD).transpose(0, 2, 1, 3)
            k_rope = (x @ w_krope).reshape(B, T, 1, ROPE_D).transpose(0, 2, 1, 3) / N_HEAD
            k_rope = _rope(k_rope, cos, sin)
            k1 = jnp.concatenate([k_nope, jnp.broadcast_to(k_rope, (B, N_HEAD, T, ROPE_D))], axis=-1)
            scores = (x @ w_imp)[..., 0]
            _, idx = jax.lax.top_k(scores, KEEP)
            idx = jnp.sort(idx, axis=1)
            sel = jnp.take_along_axis(x, idx[:, :, None], axis=1)
            ks = (sel @ w_selk).reshape(B, KEEP, N_HEAD, NOPE + ROPE_D).transpose(0, 2, 1, 3)
            vs = (sel @ w_selv).reshape(B, KEEP, N_HEAD, V_HEAD).transpose(0, 2, 1, 3)
            ks = jnp.concatenate([ks[..., :NOPE], _rope(ks[..., NOPE:], cos, sin)], axis=-1)
            kw = (x @ w_wink).reshape(B, T, N_HEAD, NOPE + ROPE_D).transpose(0, 2, 1, 3)
            vw = (x @ w_winv).reshape(B, T, N_HEAD, V_HEAD).transpose(0, 2, 1, 3)
            kw = jnp.concatenate([kw[..., :NOPE], _rope(kw[..., NOPE:], cos, sin)], axis=-1)
            a1 = _attn(q, k1, v1, causal=True)
            a2 = _attn(q, ks, vs, causal=False)
            a3 = _attn(q, kw, vw, causal=True)
            g = gate[:, :, None, None, None]
            out = g[:, 0] * a1 + g[:, 1] * a2 + g[:, 2] * a3
            out = out.transpose(0, 2, 1, 3).reshape(B, T, N_HEAD * V_HEAD)
            return out @ w_proj
        key = jax.random.key(seed)
        ks = jax.random.split(key, 20)
        B, T, C = (2, 128, 128)
        q_lora, kv_lora = (96, 32)
        std = 0.02

        def w(k, shape):
            return jax.random.normal(k, shape, dtype=jnp.float32) * std
        return {'x': jax.random.normal(ks[0], (B, T, C), dtype=jnp.float32), 'w_cq': w(ks[1], (C, q_lora)), 'g_qnorm': jnp.ones((q_lora,), jnp.float32), 'w_dq_nope': w(ks[2], (q_lora, N_HEAD * NOPE)), 'w_dq_rope': w(ks[3], (q_lora, N_HEAD * ROPE_D)), 'w_ckv': w(ks[4], (C, kv_lora)), 'g_kvnorm': jnp.ones((kv_lora,), jnp.float32), 'w_dk_nope': w(ks[5], (kv_lora, N_HEAD * NOPE)), 'w_dv': w(ks[6], (kv_lora, N_HEAD * V_HEAD)), 'w_krope': w(ks[7], (C, ROPE_D)), 'w_imp': w(ks[8], (C, 1)), 'w_selk': w(ks[9], (C, N_HEAD * (NOPE + ROPE_D))), 'w_selv': w(ks[10], (C, N_HEAD * V_HEAD)), 'w_wink': w(ks[11], (C, N_HEAD * (NOPE + ROPE_D))), 'w_winv': w(ks[12], (C, N_HEAD * V_HEAD)), 'w_gate': w(ks[13], (C, 3)), 'w_proj': w(ks[14], (N_HEAD * V_HEAD, C))}
    _L0_attn_b_in = _L0_attn_b_setup()

    def _L0_ffn_setup():
        import jax, jax.numpy as jnp
        import numpy as np
        DIM = 128
        HEADS = 16
        HD = DIM // HEADS
        M = 32
        E = 4
        K = 2
        HID = 256
        MID = 256
        LB = 0.01
        EPS = 1.1920929e-07

        def _rms(x, w):
            return x * jax.lax.rsqrt(jnp.mean(x * x, axis=-1, keepdims=True) + EPS) * w

        def _gelu(x):
            return jax.nn.gelu(x, approximate=False)
        key = jax.random.key(seed)
        ks = jax.random.split(key, 20)
        d = DIM
        w = lambda k, s: jax.random.normal(k, s, jnp.float32) * 0.02
        return {'x': jax.random.normal(ks[0], (4, 128, d), jnp.float32), 'n1_w': jnp.ones((d,), jnp.float32), 'n2_w': jnp.ones((d,), jnp.float32), 'wq': w(ks[1], (d, d)), 'wk': w(ks[2], (d, d)), 'wv': w(ks[3], (d, d)), 'wo': w(ks[4], (d, d)), 'qn_w': jnp.ones((HD,), jnp.float32), 'kn_w': jnp.ones((HD,), jnp.float32), 'gate_w': w(ks[5], (E, d)), 'e0_up': w(ks[6], (HID, d)), 'e0_down': w(ks[7], (d, HID)), 'e1_w1': w(ks[8], (HID, d)), 'e1_w2': w(ks[9], (HID, d)), 'e1_down': w(ks[10], (d, HID)), 'e2_l1': w(ks[11], (MID, d)), 'e2_l2': w(ks[12], (HID, MID)), 'e2_l3': w(ks[13], (MID, HID)), 'e2_l4': w(ks[14], (d, MID)), 'e3_down': w(ks[15], (d, d)), 'e3_up': w(ks[16], (HID, d)), 'e3_out': w(ks[17], (d, HID))}
    _L0_ffn_in = _L0_ffn_setup()

    def _L1_attn_a_setup():
        import jax, jax.numpy as jnp
        import numpy as np
        DIM = 128
        HEAD_DIM = 64
        CHUNK = 128
        B, T = (4, 512)

        def _reference_tuple_inner(x, Wq, bq, Wk, bk, Wv, bv, Wbeta, bbeta, Walpha, balpha):
            Bsz, Tlen, D = x.shape
            d = HEAD_DIM
            H = D // d
            C = CHUNK
            scale = d ** (-0.5)
            q = ((x @ Wq.T + bq) * scale).reshape(Bsz, Tlen, H, d)
            k = ((x @ Wk.T + bk) * scale).reshape(Bsz, Tlen, H, d)
            v = (x @ Wv.T + bv).reshape(Bsz, Tlen, H, d)
            alpha_logits = jnp.clip((x @ Walpha.T + balpha).reshape(Bsz, Tlen, H, d), -10.0, 10.0)
            log_alpha = jax.nn.log_sigmoid(alpha_logits)
            alpha_val = jax.nn.sigmoid(alpha_logits)
            beta = jax.nn.softplus(x @ Wbeta.T + bbeta).reshape(Bsz, Tlen, H, d)
            pad = -Tlen % C
            if pad:
                pw = ((0, 0), (0, pad), (0, 0), (0, 0))
                q, k, v = (jnp.pad(q, pw), jnp.pad(k, pw), jnp.pad(v, pw))
                log_alpha, beta = (jnp.pad(log_alpha, pw), jnp.pad(beta, pw))
            N = q.shape[1] // C
            cshape = (Bsz, N, C, H, d)
            q, k, v = (q.reshape(cshape), k.reshape(cshape), v.reshape(cshape))
            log_alpha, beta = (log_alpha.reshape(cshape), beta.reshape(cshape))
            ccum = jnp.cumsum(log_alpha, axis=2)
            m = ccum.mean(axis=-1)
            decay_logits_mean = m[:, :, :, None, :] - m[:, :, None, :, :]
            tril = jnp.tril(jnp.ones((C, C), jnp.float32))[None, None, :, :, None]
            decay_logits_mean = jnp.where(tril == 0, -1000000000.0, decay_logits_mean)
            decay = jnp.exp(decay_logits_mean)
            attn = jnp.einsum('bnihd,bnjhd->bnhij', q, k)
            attn = attn * decay.transpose(0, 1, 4, 2, 3)
            y_intra = jnp.einsum('bnhij,bnjhd->bnihd', attn, v * beta)
            asum = jnp.exp(log_alpha.sum(axis=2).mean(axis=-1))
            curve = jnp.exp(m)
            bmean = beta.mean(axis=-1)

            def to_scan(a):
                return jnp.moveaxis(a, 1, 0)
            xs = (to_scan(q), to_scan(y_intra), to_scan(curve), to_scan(asum), to_scan(k), to_scan(v), to_scan(bmean))
            state0 = jnp.zeros((Bsz, H, d, d), jnp.float32)

            def step(state, inputs):
                qi, yi, ci, ai, ki, vi, bmi = inputs
                mem = jnp.einsum('bchq,bhqk->bchk', qi, state)
                y = yi + mem * ci[..., None]
                state = state * ai[:, :, None, None]
                delta = jnp.einsum('bchk,bchv,bch->bhkv', ki, vi, bmi)
                return (state + delta, y)
            state, ys = jax.lax.scan(step, state0, xs)
            y = jnp.moveaxis(ys, 0, 1).reshape(Bsz, N * C, D)
            if pad:
                y = y[:, :Tlen, :]
            return (y, state, alpha_val)
        key = jax.random.key(seed)
        ks = jax.random.split(key, 8)
        s = 1.0 / np.sqrt(DIM)
        inp = {'x': jax.random.normal(ks[0], (B, T, DIM), jnp.float32), 'Wq': jax.random.normal(ks[1], (DIM, DIM), jnp.float32) * s, 'bq': jnp.zeros((DIM,), jnp.float32), 'Wk': jax.random.normal(ks[2], (DIM, DIM), jnp.float32) * s, 'bk': jnp.zeros((DIM,), jnp.float32), 'Wv': jax.random.normal(ks[3], (DIM, DIM), jnp.float32) * s, 'bv': jnp.zeros((DIM,), jnp.float32), 'Wbeta': jax.random.normal(ks[4], (DIM, DIM), jnp.float32) * s, 'bbeta': jnp.zeros((DIM,), jnp.float32), 'Walpha': jax.random.normal(ks[5], (DIM, DIM), jnp.float32) * s, 'balpha': jnp.full((DIM,), 2.0, jnp.float32)}
        return inp
    _L1_attn_a_in = _L1_attn_a_setup()

    def _L1_attn_b_setup():
        import jax, jax.numpy as jnp
        import numpy as np
        DIM = 128
        HEADS = 16
        DIM_HEAD = 64
        SOFTCAP = 50.0
        key = jax.random.key(seed)
        k1, k2, k3, k4 = jax.random.split(key, 4)
        b, n = (2, 256)
        dim_inner = HEADS * DIM_HEAD
        x = jax.random.normal(k1, (b, n, DIM), dtype=jnp.float32)
        w_qkv = jax.random.normal(k2, (DIM, 3 * dim_inner), dtype=jnp.float32) * 0.02
        w_gates = jax.random.normal(k3, (DIM, HEADS), dtype=jnp.float32) * 0.02
        w_out = jax.random.normal(k4, (dim_inner, DIM), dtype=jnp.float32) * 0.02
        return {'x': x, 'w_qkv': w_qkv, 'w_gates': w_gates, 'w_out': w_out}
    _L1_attn_b_in = _L1_attn_b_setup()

    def _L1_ffn_setup():
        import jax, jax.numpy as jnp
        import numpy as np
        BLOCK_SIZE = 32
        FP6_E2M3_MAX = 7.5

        def _build_fp6_e2m3_grid():
            vals = set()
            for bits in range(64):
                s = bits >> 5 & 1
                e = bits >> 3 & 3
                m = bits & 7
                v = m / 8.0 if e == 0 else (1.0 + m / 8.0) * 2.0 ** (e - 1)
                vals.add(-v if s else v)
            return np.array(sorted(vals), dtype=np.float32)
        _GRID = jnp.asarray(_build_fp6_e2m3_grid())

        def _nearest_on_grid(x, grid):
            idx = jnp.clip(jnp.searchsorted(grid, x), 0, grid.shape[0] - 1)
            idx_lo = jnp.maximum(idx - 1, 0)
            v_hi = grid[idx]
            v_lo = grid[idx_lo]
            return jnp.where(jnp.abs(x - v_lo) <= jnp.abs(x - v_hi), v_lo, v_hi)

        def _mx_quantize(t, eps=1e-30):
            rows, K = t.shape
            blocks = t.reshape(rows, K // BLOCK_SIZE, BLOCK_SIZE)
            scales = jnp.maximum(jnp.max(jnp.abs(blocks), axis=-1) / FP6_E2M3_MAX, eps)
            q = _nearest_on_grid(blocks / scales[..., None], _GRID)
            return (q, scales)
        key = jax.random.key(seed)
        k1, k2, k3 = jax.random.split(key, 3)
        x = jax.random.normal(k1, (8, 1024, 128), dtype=jnp.float32)
        weight = jax.random.normal(k2, (128, 128), dtype=jnp.float32) * 0.02
        bias = jax.random.normal(k3, (128,), dtype=jnp.float32) * 0.02
        return {'x': x, 'weight': weight, 'bias': bias}
    _L1_ffn_in = _L1_ffn_setup()
    _d = {'L0_attn_a_x': _L0_attn_a_in['x'], 'L0_attn_a_Wq': _L0_attn_a_in['Wq'], 'L0_attn_a_bq': _L0_attn_a_in['bq'], 'L0_attn_a_Wk': _L0_attn_a_in['Wk'], 'L0_attn_a_bk': _L0_attn_a_in['bk'], 'L0_attn_a_Wv': _L0_attn_a_in['Wv'], 'L0_attn_a_bv': _L0_attn_a_in['bv'], 'L0_attn_a_Wo': _L0_attn_a_in['Wo'], 'L0_attn_a_bo': _L0_attn_a_in['bo'], 'L0_attn_b_w_cq': _L0_attn_b_in['w_cq'], 'L0_attn_b_g_qnorm': _L0_attn_b_in['g_qnorm'], 'L0_attn_b_w_dq_nope': _L0_attn_b_in['w_dq_nope'], 'L0_attn_b_w_dq_rope': _L0_attn_b_in['w_dq_rope'], 'L0_attn_b_w_ckv': _L0_attn_b_in['w_ckv'], 'L0_attn_b_g_kvnorm': _L0_attn_b_in['g_kvnorm'], 'L0_attn_b_w_dk_nope': _L0_attn_b_in['w_dk_nope'], 'L0_attn_b_w_dv': _L0_attn_b_in['w_dv'], 'L0_attn_b_w_krope': _L0_attn_b_in['w_krope'], 'L0_attn_b_w_imp': _L0_attn_b_in['w_imp'], 'L0_attn_b_w_selk': _L0_attn_b_in['w_selk'], 'L0_attn_b_w_selv': _L0_attn_b_in['w_selv'], 'L0_attn_b_w_wink': _L0_attn_b_in['w_wink'], 'L0_attn_b_w_winv': _L0_attn_b_in['w_winv'], 'L0_attn_b_w_gate': _L0_attn_b_in['w_gate'], 'L0_attn_b_w_proj': _L0_attn_b_in['w_proj'], 'L0_ffn_n1_w': _L0_ffn_in['n1_w'], 'L0_ffn_n2_w': _L0_ffn_in['n2_w'], 'L0_ffn_wq': _L0_ffn_in['wq'], 'L0_ffn_wk': _L0_ffn_in['wk'], 'L0_ffn_wv': _L0_ffn_in['wv'], 'L0_ffn_wo': _L0_ffn_in['wo'], 'L0_ffn_qn_w': _L0_ffn_in['qn_w'], 'L0_ffn_kn_w': _L0_ffn_in['kn_w'], 'L0_ffn_gate_w': _L0_ffn_in['gate_w'], 'L0_ffn_e0_up': _L0_ffn_in['e0_up'], 'L0_ffn_e0_down': _L0_ffn_in['e0_down'], 'L0_ffn_e1_w1': _L0_ffn_in['e1_w1'], 'L0_ffn_e1_w2': _L0_ffn_in['e1_w2'], 'L0_ffn_e1_down': _L0_ffn_in['e1_down'], 'L0_ffn_e2_l1': _L0_ffn_in['e2_l1'], 'L0_ffn_e2_l2': _L0_ffn_in['e2_l2'], 'L0_ffn_e2_l3': _L0_ffn_in['e2_l3'], 'L0_ffn_e2_l4': _L0_ffn_in['e2_l4'], 'L0_ffn_e3_down': _L0_ffn_in['e3_down'], 'L0_ffn_e3_up': _L0_ffn_in['e3_up'], 'L0_ffn_e3_out': _L0_ffn_in['e3_out'], 'L1_attn_a_Wq': _L1_attn_a_in['Wq'], 'L1_attn_a_bq': _L1_attn_a_in['bq'], 'L1_attn_a_Wk': _L1_attn_a_in['Wk'], 'L1_attn_a_bk': _L1_attn_a_in['bk'], 'L1_attn_a_Wv': _L1_attn_a_in['Wv'], 'L1_attn_a_bv': _L1_attn_a_in['bv'], 'L1_attn_a_Wbeta': _L1_attn_a_in['Wbeta'], 'L1_attn_a_bbeta': _L1_attn_a_in['bbeta'], 'L1_attn_a_Walpha': _L1_attn_a_in['Walpha'], 'L1_attn_a_balpha': _L1_attn_a_in['balpha'], 'L1_attn_b_w_qkv': _L1_attn_b_in['w_qkv'], 'L1_attn_b_w_gates': _L1_attn_b_in['w_gates'], 'L1_attn_b_w_out': _L1_attn_b_in['w_out'], 'L1_ffn_weight': _L1_ffn_in['weight'], 'L1_ffn_bias': _L1_ffn_in['bias']}
    _x0 = _d['L0_attn_a_x']
    _d['L0_attn_a_x'] = jax.random.normal(jax.random.fold_in(jax.random.key(seed), 1), (4, 512, 128), dtype=_x0.dtype)
    del _x0
    return _d

def reference(L0_attn_a_x, L0_attn_a_Wq, L0_attn_a_bq, L0_attn_a_Wk, L0_attn_a_bk, L0_attn_a_Wv, L0_attn_a_bv, L0_attn_a_Wo, L0_attn_a_bo, L0_attn_b_w_cq, L0_attn_b_g_qnorm, L0_attn_b_w_dq_nope, L0_attn_b_w_dq_rope, L0_attn_b_w_ckv, L0_attn_b_g_kvnorm, L0_attn_b_w_dk_nope, L0_attn_b_w_dv, L0_attn_b_w_krope, L0_attn_b_w_imp, L0_attn_b_w_selk, L0_attn_b_w_selv, L0_attn_b_w_wink, L0_attn_b_w_winv, L0_attn_b_w_gate, L0_attn_b_w_proj, L0_ffn_n1_w, L0_ffn_n2_w, L0_ffn_wq, L0_ffn_wk, L0_ffn_wv, L0_ffn_wo, L0_ffn_qn_w, L0_ffn_kn_w, L0_ffn_gate_w, L0_ffn_e0_up, L0_ffn_e0_down, L0_ffn_e1_w1, L0_ffn_e1_w2, L0_ffn_e1_down, L0_ffn_e2_l1, L0_ffn_e2_l2, L0_ffn_e2_l3, L0_ffn_e2_l4, L0_ffn_e3_down, L0_ffn_e3_up, L0_ffn_e3_out, L1_attn_a_Wq, L1_attn_a_bq, L1_attn_a_Wk, L1_attn_a_bk, L1_attn_a_Wv, L1_attn_a_bv, L1_attn_a_Wbeta, L1_attn_a_bbeta, L1_attn_a_Walpha, L1_attn_a_balpha, L1_attn_b_w_qkv, L1_attn_b_w_gates, L1_attn_b_w_out, L1_ffn_weight, L1_ffn_bias):

    def _L0_attn_a_ref(x, Wq, bq, Wk, bk, Wv, bv, Wo, bo):
        import jax, jax.numpy as jnp
        import numpy as np
        EPS = 1e-06
        NUM_HEADS = 16

        def _phi(x):
            return jax.nn.elu(x) + 1.0
        B, S, D = x.shape
        H = NUM_HEADS
        hd = D // H
        q = (x @ Wq.T + bq).reshape(B, S, H, hd).transpose(0, 2, 1, 3)
        k = (x @ Wk.T + bk).reshape(B, S, H, hd).transpose(0, 2, 1, 3)
        v = (x @ Wv.T + bv).reshape(B, S, H, hd).transpose(0, 2, 1, 3)
        q = _phi(q)
        k = _phi(k)
        kv_cum = jnp.cumsum(k[..., :, None] * v[..., None, :], axis=2)
        k_cum = jnp.cumsum(k, axis=2)
        num = jnp.einsum('bhsd,bhsde->bhse', q, kv_cum)
        den = jnp.einsum('bhsd,bhsd->bhs', q, k_cum)
        out = num / (den[..., None] + EPS)
        out = out.transpose(0, 2, 1, 3).reshape(B, S, D)
        return out @ Wo.T + bo

    def _L0_attn_b_ref(x, w_cq, g_qnorm, w_dq_nope, w_dq_rope, w_ckv, g_kvnorm, w_dk_nope, w_dv, w_krope, w_imp, w_selk, w_selv, w_wink, w_winv, w_gate, w_proj):
        import jax, jax.numpy as jnp
        import numpy as np
        import math
        N_HEAD = 16
        V_HEAD = 32
        NOPE = 32
        ROPE_D = 64
        KEEP = 32
        EPS = 1e-06

        def _freqs(T, dim=ROPE_D, theta=10000.0):
            f = 1.0 / theta ** (jnp.arange(0, dim, 2, dtype=jnp.float32) / dim)
            t = jnp.arange(T, dtype=jnp.float32)
            a = jnp.outer(t, f)
            return (jnp.cos(a), jnp.sin(a))

        def _rope(x, cos, sin):
            S = x.shape[-2]
            c = cos[:S][None, None]
            s = sin[:S][None, None]
            x1, x2 = jnp.split(x, 2, axis=-1)
            return jnp.concatenate([x1 * c - x2 * s, x1 * s + x2 * c], axis=-1)

        def _rms(x, g, eps=EPS):
            return x * jax.lax.rsqrt(jnp.mean(x * x, axis=-1, keepdims=True) + eps) * g

        def _attn(q, k, v, causal):
            scale = 1.0 / math.sqrt(q.shape[-1])
            s = jnp.einsum('bhqd,bhkd->bhqk', q, k) * scale
            if causal:
                Tq, Tk = (s.shape[-2], s.shape[-1])
                mask = jnp.tril(jnp.ones((Tq, Tk), dtype=bool))
                s = jnp.where(mask, s, jnp.finfo(s.dtype).min)
            return jnp.einsum('bhqk,bhkd->bhqd', jax.nn.softmax(s, axis=-1), v)

        def _forward(x, w_cq, g_qnorm, w_dq_nope, w_dq_rope, w_ckv, g_kvnorm, w_dk_nope, w_dv, w_krope, w_imp, w_selk, w_selv, w_wink, w_winv, w_gate, w_proj):
            B, T, C = x.shape
            cos, sin = _freqs(T)
            nq = _rms(x @ w_cq, g_qnorm)
            q_nope = (nq @ w_dq_nope).reshape(B, T, N_HEAD, NOPE).transpose(0, 2, 1, 3)
            q_rope = (nq @ w_dq_rope).reshape(B, T, N_HEAD, ROPE_D).transpose(0, 2, 1, 3)
            q_rope = _rope(q_rope, cos, sin)
            q = jnp.concatenate([q_nope, q_rope], axis=-1)
            gate = jax.nn.softmax((x @ w_gate).mean(axis=1), axis=-1)
            ckv = _rms(x @ w_ckv, g_kvnorm)
            k_nope = (ckv @ w_dk_nope).reshape(B, T, N_HEAD, NOPE).transpose(0, 2, 1, 3)
            v1 = (ckv @ w_dv).reshape(B, T, N_HEAD, V_HEAD).transpose(0, 2, 1, 3)
            k_rope = (x @ w_krope).reshape(B, T, 1, ROPE_D).transpose(0, 2, 1, 3) / N_HEAD
            k_rope = _rope(k_rope, cos, sin)
            k1 = jnp.concatenate([k_nope, jnp.broadcast_to(k_rope, (B, N_HEAD, T, ROPE_D))], axis=-1)
            scores = (x @ w_imp)[..., 0]
            _, idx = jax.lax.top_k(scores, KEEP)
            idx = jnp.sort(idx, axis=1)
            sel = jnp.take_along_axis(x, idx[:, :, None], axis=1)
            ks = (sel @ w_selk).reshape(B, KEEP, N_HEAD, NOPE + ROPE_D).transpose(0, 2, 1, 3)
            vs = (sel @ w_selv).reshape(B, KEEP, N_HEAD, V_HEAD).transpose(0, 2, 1, 3)
            ks = jnp.concatenate([ks[..., :NOPE], _rope(ks[..., NOPE:], cos, sin)], axis=-1)
            kw = (x @ w_wink).reshape(B, T, N_HEAD, NOPE + ROPE_D).transpose(0, 2, 1, 3)
            vw = (x @ w_winv).reshape(B, T, N_HEAD, V_HEAD).transpose(0, 2, 1, 3)
            kw = jnp.concatenate([kw[..., :NOPE], _rope(kw[..., NOPE:], cos, sin)], axis=-1)
            a1 = _attn(q, k1, v1, causal=True)
            a2 = _attn(q, ks, vs, causal=False)
            a3 = _attn(q, kw, vw, causal=True)
            g = gate[:, :, None, None, None]
            out = g[:, 0] * a1 + g[:, 1] * a2 + g[:, 2] * a3
            out = out.transpose(0, 2, 1, 3).reshape(B, T, N_HEAD * V_HEAD)
            return out @ w_proj
        return _forward(x, w_cq, g_qnorm, w_dq_nope, w_dq_rope, w_ckv, g_kvnorm, w_dk_nope, w_dv, w_krope, w_imp, w_selk, w_selv, w_wink, w_winv, w_gate, w_proj)

    def _L0_ffn_ref(x, n1_w, n2_w, wq, wk, wv, wo, qn_w, kn_w, gate_w, e0_up, e0_down, e1_w1, e1_w2, e1_down, e2_l1, e2_l2, e2_l3, e2_l4, e3_down, e3_up, e3_out):
        import jax, jax.numpy as jnp
        import numpy as np
        DIM = 128
        HEADS = 16
        HD = DIM // HEADS
        M = 32
        E = 4
        K = 2
        HID = 256
        MID = 256
        LB = 0.01
        EPS = 1.1920929e-07

        def _rms(x, w):
            return x * jax.lax.rsqrt(jnp.mean(x * x, axis=-1, keepdims=True) + EPS) * w

        def _gelu(x):
            return jax.nn.gelu(x, approximate=False)
        B, T, C = x.shape
        h = _rms(x, n1_w)
        heads = lambda w_: (h @ w_.T).reshape(B, T, HEADS, HD).transpose(0, 2, 1, 3)
        q = _rms(heads(wq), qn_w)
        k = _rms(heads(wk), kn_w)
        v = heads(wv)
        scores = jnp.einsum('bhqd,bhkd->bhqk', q, k) * HD ** (-0.5)
        causal = jnp.tril(jnp.ones((T, T), bool))
        scores = jnp.where(causal[None, None], scores, -jnp.inf)
        attn = jax.nn.softmax(scores, axis=-1)
        ao = jnp.einsum('bhqk,bhkd->bhqd', attn, v).transpose(0, 2, 1, 3).reshape(B, T, C) @ wo.T
        ao = ao.at[:, :, :M].set(0.0)
        x = x + ao
        xf = _rms(x, n2_w).reshape(-1, C)
        N = xf.shape[0]
        logits = jnp.nan_to_num(xf @ gate_w.T)
        probs = jax.nn.softmax(logits, axis=-1)
        topv, topi = jax.lax.top_k(probs, K)
        topv = topv / (topv.sum(-1, keepdims=True) + 1e-08)
        wts = jnp.zeros((N, E), x.dtype).at[jnp.arange(N)[:, None], topi].add(topv)
        o0 = _gelu(xf @ e0_up.T) @ e0_down.T
        o1 = jax.nn.silu(xf @ e1_w1.T) * (xf @ e1_w2.T) @ e1_down.T
        o2 = _gelu(_gelu(_gelu(xf @ e2_l1.T) @ e2_l2.T) @ e2_l3.T) @ e2_l4.T
        o3 = _gelu(_gelu(xf @ e3_down.T) @ e3_up.T) @ e3_out.T
        moe = wts[:, 0:1] * o0 + wts[:, 1:2] * o1 + wts[:, 2:3] * o2 + wts[:, 3:4] * o3
        moe = moe.reshape(B, T, C).at[:, :, :M].set(0.0)
        return x + moe

    def _L1_attn_a_ref(x, Wq, bq, Wk, bk, Wv, bv, Wbeta, bbeta, Walpha, balpha):
        import jax, jax.numpy as jnp
        import numpy as np
        DIM = 128
        HEAD_DIM = 64
        CHUNK = 128
        B, T = (4, 512)

        def _reference_tuple_inner(x, Wq, bq, Wk, bk, Wv, bv, Wbeta, bbeta, Walpha, balpha):
            Bsz, Tlen, D = x.shape
            d = HEAD_DIM
            H = D // d
            C = CHUNK
            scale = d ** (-0.5)
            q = ((x @ Wq.T + bq) * scale).reshape(Bsz, Tlen, H, d)
            k = ((x @ Wk.T + bk) * scale).reshape(Bsz, Tlen, H, d)
            v = (x @ Wv.T + bv).reshape(Bsz, Tlen, H, d)
            alpha_logits = jnp.clip((x @ Walpha.T + balpha).reshape(Bsz, Tlen, H, d), -10.0, 10.0)
            log_alpha = jax.nn.log_sigmoid(alpha_logits)
            alpha_val = jax.nn.sigmoid(alpha_logits)
            beta = jax.nn.softplus(x @ Wbeta.T + bbeta).reshape(Bsz, Tlen, H, d)
            pad = -Tlen % C
            if pad:
                pw = ((0, 0), (0, pad), (0, 0), (0, 0))
                q, k, v = (jnp.pad(q, pw), jnp.pad(k, pw), jnp.pad(v, pw))
                log_alpha, beta = (jnp.pad(log_alpha, pw), jnp.pad(beta, pw))
            N = q.shape[1] // C
            cshape = (Bsz, N, C, H, d)
            q, k, v = (q.reshape(cshape), k.reshape(cshape), v.reshape(cshape))
            log_alpha, beta = (log_alpha.reshape(cshape), beta.reshape(cshape))
            ccum = jnp.cumsum(log_alpha, axis=2)
            m = ccum.mean(axis=-1)
            decay_logits_mean = m[:, :, :, None, :] - m[:, :, None, :, :]
            tril = jnp.tril(jnp.ones((C, C), jnp.float32))[None, None, :, :, None]
            decay_logits_mean = jnp.where(tril == 0, -1000000000.0, decay_logits_mean)
            decay = jnp.exp(decay_logits_mean)
            attn = jnp.einsum('bnihd,bnjhd->bnhij', q, k)
            attn = attn * decay.transpose(0, 1, 4, 2, 3)
            y_intra = jnp.einsum('bnhij,bnjhd->bnihd', attn, v * beta)
            asum = jnp.exp(log_alpha.sum(axis=2).mean(axis=-1))
            curve = jnp.exp(m)
            bmean = beta.mean(axis=-1)

            def to_scan(a):
                return jnp.moveaxis(a, 1, 0)
            xs = (to_scan(q), to_scan(y_intra), to_scan(curve), to_scan(asum), to_scan(k), to_scan(v), to_scan(bmean))
            state0 = jnp.zeros((Bsz, H, d, d), jnp.float32)

            def step(state, inputs):
                qi, yi, ci, ai, ki, vi, bmi = inputs
                mem = jnp.einsum('bchq,bhqk->bchk', qi, state)
                y = yi + mem * ci[..., None]
                state = state * ai[:, :, None, None]
                delta = jnp.einsum('bchk,bchv,bch->bhkv', ki, vi, bmi)
                return (state + delta, y)
            state, ys = jax.lax.scan(step, state0, xs)
            y = jnp.moveaxis(ys, 0, 1).reshape(Bsz, N * C, D)
            if pad:
                y = y[:, :Tlen, :]
            return (y, state, alpha_val)
        return _reference_tuple_inner(x, Wq, bq, Wk, bk, Wv, bv, Wbeta, bbeta, Walpha, balpha)[0]

    def _L1_attn_b_ref(x, w_qkv, w_gates, w_out):
        import jax, jax.numpy as jnp
        import numpy as np
        DIM = 128
        HEADS = 16
        DIM_HEAD = 64
        SOFTCAP = 50.0
        b, n, _ = x.shape
        scale = DIM_HEAD ** (-0.5)
        qkv = jnp.einsum('bnf,fe->bne', x, w_qkv).reshape(b, n, 3, HEADS, DIM_HEAD)
        qkv = jnp.moveaxis(qkv, 2, 0)
        q, k, v = jnp.moveaxis(qkv, 3, 2)
        q = q * scale
        sim = jnp.einsum('bhid,bhjd->bhij', q, k)
        sim = SOFTCAP * jnp.tanh(sim / SOFTCAP)
        mask_value = -jnp.finfo(sim.dtype).max
        causal_mask = jnp.triu(jnp.ones((n, n), dtype=bool), 1)
        sim = jnp.where(causal_mask, mask_value, sim)
        attn = jax.nn.softmax(sim, axis=-1)
        out = jnp.einsum('bhij,bhjd->bhid', attn, v)
        gates = jax.nn.sigmoid(jnp.einsum('bnf,fh->bhn', x, w_gates))[..., None]
        out = out * gates
        out = jnp.transpose(out, (0, 2, 1, 3)).reshape(b, n, HEADS * DIM_HEAD)
        return jnp.einsum('bne,ef->bnf', out, w_out)

    def _L1_ffn_ref(x, weight, bias):
        import jax, jax.numpy as jnp
        import numpy as np
        BLOCK_SIZE = 32
        FP6_E2M3_MAX = 7.5

        def _build_fp6_e2m3_grid():
            vals = set()
            for bits in range(64):
                s = bits >> 5 & 1
                e = bits >> 3 & 3
                m = bits & 7
                v = m / 8.0 if e == 0 else (1.0 + m / 8.0) * 2.0 ** (e - 1)
                vals.add(-v if s else v)
            return np.array(sorted(vals), dtype=np.float32)
        _GRID = jnp.asarray(_build_fp6_e2m3_grid())

        def _nearest_on_grid(x, grid):
            idx = jnp.clip(jnp.searchsorted(grid, x), 0, grid.shape[0] - 1)
            idx_lo = jnp.maximum(idx - 1, 0)
            v_hi = grid[idx]
            v_lo = grid[idx_lo]
            return jnp.where(jnp.abs(x - v_lo) <= jnp.abs(x - v_hi), v_lo, v_hi)

        def _mx_quantize(t, eps=1e-30):
            rows, K = t.shape
            blocks = t.reshape(rows, K // BLOCK_SIZE, BLOCK_SIZE)
            scales = jnp.maximum(jnp.max(jnp.abs(blocks), axis=-1) / FP6_E2M3_MAX, eps)
            q = _nearest_on_grid(blocks / scales[..., None], _GRID)
            return (q, scales)
        batch_shape = x.shape[:-1]
        in_features = x.shape[-1]
        x2 = x.astype(jnp.float32).reshape(-1, in_features)
        w2 = weight.astype(jnp.float32)
        xq, xs = _mx_quantize(x2)
        wq, ws = _mx_quantize(w2)
        xd = (xq * xs[..., None]).reshape(x2.shape)
        wd = (wq * ws[..., None]).reshape(w2.shape)
        out = xd @ wd.T + bias
        return out.reshape(*batch_shape, -1)
    x = L0_attn_a_x
    x = x + _L0_attn_a_ref(_layernorm(x, axis=-1), L0_attn_a_Wq, L0_attn_a_bq, L0_attn_a_Wk, L0_attn_a_bk, L0_attn_a_Wv, L0_attn_a_bv, L0_attn_a_Wo, L0_attn_a_bo)
    x = x + _L0_ffn_ref(_layernorm(x, axis=-1), L0_ffn_n1_w, L0_ffn_n2_w, L0_ffn_wq, L0_ffn_wk, L0_ffn_wv, L0_ffn_wo, L0_ffn_qn_w, L0_ffn_kn_w, L0_ffn_gate_w, L0_ffn_e0_up, L0_ffn_e0_down, L0_ffn_e1_w1, L0_ffn_e1_w2, L0_ffn_e1_down, L0_ffn_e2_l1, L0_ffn_e2_l2, L0_ffn_e2_l3, L0_ffn_e2_l4, L0_ffn_e3_down, L0_ffn_e3_up, L0_ffn_e3_out)
    x = x + _L0_attn_b_ref(_layernorm(x, axis=-1), L0_attn_b_w_cq, L0_attn_b_g_qnorm, L0_attn_b_w_dq_nope, L0_attn_b_w_dq_rope, L0_attn_b_w_ckv, L0_attn_b_g_kvnorm, L0_attn_b_w_dk_nope, L0_attn_b_w_dv, L0_attn_b_w_krope, L0_attn_b_w_imp, L0_attn_b_w_selk, L0_attn_b_w_selv, L0_attn_b_w_wink, L0_attn_b_w_winv, L0_attn_b_w_gate, L0_attn_b_w_proj)
    x = x + _L0_ffn_ref(_layernorm(x, axis=-1), L0_ffn_n1_w, L0_ffn_n2_w, L0_ffn_wq, L0_ffn_wk, L0_ffn_wv, L0_ffn_wo, L0_ffn_qn_w, L0_ffn_kn_w, L0_ffn_gate_w, L0_ffn_e0_up, L0_ffn_e0_down, L0_ffn_e1_w1, L0_ffn_e1_w2, L0_ffn_e1_down, L0_ffn_e2_l1, L0_ffn_e2_l2, L0_ffn_e2_l3, L0_ffn_e2_l4, L0_ffn_e3_down, L0_ffn_e3_up, L0_ffn_e3_out)
    x = x + _L1_attn_a_ref(_layernorm(x, axis=-1), L1_attn_a_Wq, L1_attn_a_bq, L1_attn_a_Wk, L1_attn_a_bk, L1_attn_a_Wv, L1_attn_a_bv, L1_attn_a_Wbeta, L1_attn_a_bbeta, L1_attn_a_Walpha, L1_attn_a_balpha)
    x = x + _L1_ffn_ref(_layernorm(x, axis=-1), L1_ffn_weight, L1_ffn_bias)
    x = x + _L1_attn_b_ref(_layernorm(x, axis=-1), L1_attn_b_w_qkv, L1_attn_b_w_gates, L1_attn_b_w_out)
    x = x + _L1_ffn_ref(_layernorm(x, axis=-1), L1_ffn_weight, L1_ffn_bias)
    return x

_drawn_inputs = setup_inputs


def setup_inputs(seed=0):
    import zlib

    import numpy as np

    out = dict(_drawn_inputs(seed))
    spreads = {'L0_attn_a_bq': (0.0, 0.8),
     'L0_attn_a_bk': (0.0, 0.8),
     'L0_attn_a_bv': (0.0, 0.1),
     'L0_attn_a_bo': (0.0, 0.1),
     'L0_attn_b_g_qnorm': (1.0, 0.6),
     'L0_attn_b_g_kvnorm': (1.0, 0.6),
     'L0_ffn_n1_w': (1.0, 0.6),
     'L0_ffn_n2_w': (1.0, 0.6),
     'L0_ffn_qn_w': (1.0, 0.6),
     'L0_ffn_kn_w': (1.0, 0.6),
     'L1_attn_a_bq': (0.0, 2.0),
     'L1_attn_a_bk': (0.0, 2.0),
     'L1_attn_a_bv': (0.0, 2.0),
     'L1_attn_a_bbeta': (0.0, 2.0),
     'L1_attn_a_balpha': (2.0, 0.6)}
    factors = {'L0_attn_a_Wq': 2.748,
     'L0_attn_b_w_cq': 8.0,
     'L0_attn_b_w_dq_nope': 8.0,
     'L0_attn_b_w_dq_rope': 8.0,
     'L0_attn_b_w_ckv': 8.0,
     'L0_attn_b_w_dk_nope': 8.0,
     'L0_attn_b_w_dv': 8.0,
     'L0_attn_b_w_krope': 8.0,
     'L0_attn_b_w_imp': 8.0,
     'L0_attn_b_w_selk': 8.0,
     'L0_attn_b_w_selv': 8.0,
     'L0_attn_b_w_wink': 8.0,
     'L0_attn_b_w_winv': 8.0,
     'L0_attn_b_w_gate': 8.0,
     'L0_attn_b_w_proj': 8.0,
     'L0_ffn_wq': 8.0,
     'L0_ffn_wk': 8.0,
     'L0_ffn_wv': 5.102,
     'L0_ffn_wo': 5.145,
     'L0_ffn_gate_w': 8.0,
     'L0_ffn_e0_up': 5.137,
     'L0_ffn_e0_down': 5.059,
     'L0_ffn_e1_w1': 8.0,
     'L0_ffn_e1_w2': 8.0,
     'L0_ffn_e1_down': 8.0,
     'L0_ffn_e2_l1': 8.0,
     'L0_ffn_e2_l2': 8.0,
     'L0_ffn_e2_l3': 8.0,
     'L0_ffn_e2_l4': 8.0,
     'L0_ffn_e3_down': 8.0,
     'L0_ffn_e3_up': 8.0,
     'L0_ffn_e3_out': 8.0,
     'L1_attn_a_Walpha': 64.0,
     'L1_attn_b_w_qkv': 8.0,
     'L1_attn_b_w_gates': 8.0,
     'L1_attn_b_w_out': 8.0,
     'L1_ffn_bias': 16.227,
     'L1_attn_a_Wq': 2.726,
     'L1_attn_a_Wv': 2.921,
     'L1_attn_a_Wbeta': 5.689}
    for name, (base, spread) in spreads.items():
        noise = np.random.default_rng([zlib.crc32(name.encode()), seed]).standard_normal(out[name].shape)
        drawn = base * np.exp(spread * noise) if base else spread * noise
        out[name] = jnp.asarray(drawn.astype(out[name].dtype))
    for name, factor in factors.items():
        out[name] = (out[name] * factor).astype(out[name].dtype)
    return out
```

```python
from contextlib import ExitStack

import numpy as np

import concourse.bass as bass
from concourse import mybir

F32 = mybir.dt.float32
BF16 = mybir.dt.bfloat16
ALU = mybir.AluOpType
ACT = mybir.ActivationFunctionType
AX = mybir.AxisListType

P = 128
BATCH, SEQ, D = 4, 512, 128
NT = SEQ // P
NG = 4
NEG = -1.0e30
LN_EPS = 1e-5

WEIGHTS = [
    ("a_wqkv", 128, 384), ("a_wo", 128, NG * 128), ("a_brow", 1, 512),
    ("f_wqkv", 128, 384), ("f_wo", 128, NG * 128), ("f_n1", 128, 1), ("f_n2", 128, 1),
    ("f_qn", 128, 1), ("f_kn", 128, 1), ("f_gate", 128, 4),
    ("f_e0_up", 128, 256), ("f_e0_dn", 128, 256), ("f_e1_w1", 128, 256), ("f_e1_w2", 128, 256),
    ("f_e1_dn", 128, 256), ("f_e2_l1", 128, 256), ("f_e2_l2", 128, 512), ("f_e2_l3", 128, 512),
    ("f_e2_l4", 128, 256), ("f_e3_dn", 128, 128), ("f_e3_up", 128, 256), ("f_e3_out", 128, 256),
    ("m_cq", 128, 96), ("m_ckv", 128, 32), ("m_krope", 128, 128), ("m_imp", 128, 128),
    ("m_gate", 128, 3), ("m_gqkv", 128, 1), ("m_dv", 128, 512), ("m_selv", 128, 512),
    ("m_winv", 128, 512), ("m_proj", 128, NG * 128),
    ("g_wqk", 128, 256), ("g_wkvab", 128, 512), ("g_bcol", 128, 2), ("g_brow", 1, 512),
    ("s_wout", 128, 8 * 128),
    ("q_w", 128, 128), ("q_brow", 1, 128),
]
TABLES = [
    ("ident", 128, 128), ("mask_qk", 128, 128), ("mask_kq", 128, 128), ("upto", 128, 128),
    ("before", 128, 128), ("block", 128, 128), ("spread8", 128, 128), ("rope_c", 96, 512), ("rope_s", 96, 512),
    ("below", 128, 128), ("iota", 128, 32), ("lower4", 128, 16), ("aug8", 128, 1), ("aug3", 128, 3),
]


class Named:
    pass


def offsets(table):
    at, out = 0, {}
    for name, rows, cols in table:
        out[name] = (at, rows, cols)
        at += cols
    return out, at


W_AT, W_COLS = offsets(WEIGHTS)
T_AT, T_COLS = offsets(TABLES)
M_COLS = 7 * 384


def sems(nc, ctx, prefix, names):
    made = {n: ctx.enter_context(nc.semaphore(f"{prefix}_{n}")) for n in names.split()}
    return made, list(made.values())


def clear(nc, used):
    for s in used:
        nc.sync.sem_clear(s)
    nc.all_engine_barrier()


LN_SEMS = "ln_stats ln_aggr ln_var ln_std ln_rstd ln_y ln_turned ln_yt "


def ln_vector(dve, m, s):
    for t in range(NT):
        dve.bn_stats(m.stats[:, t, :], m.X[:, t, :]).then_inc(s["ln_stats"], 1)
    for t in range(NT):
        dve.wait_ge(s["ln_stats"], t + 1)
        dve.bn_aggr(m.mv[:, t, :], m.stats[:, t, :]).then_inc(s["ln_aggr"], 1)
    dve.wait_ge(s["ln_aggr"], NT)
    dve.tensor_scalar(m.var[:], m.mv[:, :, 1], LN_EPS, None, ALU.add).then_inc(s["ln_var"], 1)
    dve.wait_ge(s["ln_std"], 1)
    dve.reciprocal(m.rstd[:], m.std[:]).then_inc(s["ln_rstd"], 1)
    dve.wait_ge(s["ln_rstd"], 1)
    for t in range(NT):
        dve.tensor_scalar(m.Y[:, t, :], m.X[:, t, :], m.mv[:, t, 0:1], m.rstd[:, t:t + 1],
                          ALU.subtract, ALU.mult).then_inc(s["ln_y"], 1)


def ln_scalar(act, m, s):
    act.wait_ge(s["ln_var"], 1)
    act.activation(m.std[:], m.var[:], ACT.Sqrt).then_inc(s["ln_std"], 1)


def ln_tensor(pe, m, s, bank):
    for t in range(NT):
        pe.wait_ge(s["ln_y"], t + 1)
        pe.transpose(m.ps[bank][:, t * P:(t + 1) * P], m.Y[:, t, :], m.ident).then_inc(s["ln_turned"], 1)


def ln_copy(act, m, s, bank):
    act.wait_ge(s["ln_turned"], NT)
    act.copy(m.YT[:], m.ps[bank][:]).then_inc(s["ln_yt"], 1)


def linear_attention(nc, m):
    def weights_of(g, j):
        return (m.PT, m.hid)[g % 2][:, j, :]

    with ExitStack() as ctx:
        s, used = sems(nc, ctx, "lin", LN_SEMS + "proj low exps high phi vcopy turned laid "
                       "scores masked state_sum state numden numden_out spread den_eps rden normed out_sum "
                       "residual")
        with nc.Block() as block:

            @block.tensor
            def _(pe):
                ln_tensor(pe, m, s, 0)
                pe.wait_ge(s["ln_yt"], 1)
                for t in range(NT):
                    pe.matmul(m.ps[1 + t][:, 0:384], m.YT[:, t * P:(t + 1) * P], m.w["a_wqkv"],
                              start=True, stop=False)
                    pe.matmul(m.ps[1 + t][:, 0:384], m.ones[0:1, 0:P], m.w["a_brow"][:, 0:384],
                              start=False, stop=True).then_inc(s["proj"], 1)
                pe.wait_ge(s["phi"], 8)
                turn_heads(pe, m, s)
                pe.wait_ge(s["laid"], 2 * NG)

                def scores(g):
                    for j in range(4):
                        for c in range(NT):
                            r = slice(c * P, (c + 1) * P)
                            mm = pe.matmul(m.ps[j][:, r], m.KTall[32 * j:32 * j + 8, g, r],
                                           m.QTall[32 * j:32 * j + 8, g, r], start=True, stop=True)
                        mm.then_inc(s["scores"], 1)

                def states(g):
                    for c in range(NT - 1):
                        if g or c:
                            pe.wait_ge(s["state"], 3 * g + c)
                        pe.matmul(m.ps[4][:, 0:P], tile4(m.Kp, c, g), tile4(m.Vp, c, g),
                                  start=(c == 0), stop=True, skip_group_check=True
                                  ).then_inc(s["state_sum"], 1)

                def values(g):
                    if g:
                        pe.wait_ge(s["numden_out"], g)
                    for c in range(1, NT):
                        r = slice(c * P, (c + 1) * P)
                        pe.wait_ge(s["state"], 3 * g + c)
                        pe.matmul(m.ps[5][:, r], m.S[:, g % 2, c - 1, :], m.QTall[:, g, r], start=(c == 1),
                                  stop=False, skip_group_check=True)
                    for j in range(4):
                        pe.wait_ge(s["masked"], 4 * g + j + 1)
                        q = slice(32 * j, 32 * j + 32)
                        for c in range(NT):
                            r = slice(c * P, (c + 1) * P)
                            mm = pe.matmul(m.ps[5][q, r], m.Vp[:, c, 4 * g + j, :], weights_of(g, j)[:, r],
                                           start=False, stop=True, skip_group_check=True)
                    mm.then_inc(s["numden"], 1)

                scores(0)
                states(0)
                for g in range(NG):
                    if g + 1 < NG:
                        pe.wait_ge(s["masked"], 4 * (g + 1))
                        scores(g + 1)
                        states(g + 1)
                    if g:
                        spread_den(pe, m, s, g - 1)
                    values(g)
                spread_den(pe, m, s, NG - 1)
                for t in range(NT):
                    pe.matmul(m.ps[7][:, t * P:(t + 1) * P], m.ones[0:1, 0:P],
                              m.w["a_brow"][:, 384:512], start=(t == 0), stop=False,
                              skip_group_check=True)
                project(pe, m, s, m.ps[7], m.w["a_wo"], started=True)

            @block.scalar
            def _(act):
                ln_scalar(act, m, s)
                ln_copy(act, m, s, 0)
                for t in range(NT):
                    act.wait_ge(s["high"], t + 1)
                    act.copy(m.Vp[:, t, :, 0:8], heads8(m.ps[1 + t][:, 256:384])).then_inc(s["vcopy"], 1)
                    act.wait_ge(s["low"], t + 1)
                    act.activation(m.B1[:, t, :], m.B1[:, t, :], ACT.Exp).then_inc(s["exps"], 1)
                lay_heads(act, m, s)
                for g in range(NG):
                    take_numden(act, m, s, g)

            @block.vector
            def _(dve):
                ln_vector(dve, m, s)
                for t in range(NT):
                    dve.wait_ge(s["proj"], t + 1)
                    dve.tensor_scalar(m.B1[:, t, :], m.ps[1 + t][:, 0:256], 0.0, None,
                                      ALU.min).then_inc(s["low"], 1)
                    dve.tensor_scalar(m.B2[:, t, :], m.ps[1 + t][:, 0:256], 0.0, None,
                                      ALU.max).then_inc(s["high"], 1)
                    dve.wait_ge(s["exps"], t + 1)
                    dve.wait_ge(s["high"], t + 1)
                    for k, pad in enumerate((m.Qp, m.Kp)):
                        r = slice(P * k, P * k + P)
                        dve.tensor_tensor(pad[:, t, :, 0:8], heads8(m.B1[:, t, r]),
                                          heads8(m.B2[:, t, r]), ALU.add).then_inc(s["phi"], 1)

                def masks(g):
                    if g >= 2:
                        dve.wait_ge(s["numden"], g - 1)
                    for j in range(4):
                        dve.wait_ge(s["scores"], 4 * g + j + 1)
                        dve.tensor_tensor(weights_of(g, j).rearrange("p (c i) -> p c i", c=NT),
                                          m.ps[j][:].rearrange("p (c i) -> p c i", c=NT),
                                          m.t["upto"].unsqueeze(1).to_broadcast([P, NT, P]),
                                          ALU.mult).then_inc(s["masked"], 1)
                    for c in range(NT - 1):
                        dve.wait_ge(s["state_sum"], 3 * g + c + 1)
                        dve.tensor_tensor(m.S[:, g % 2, c, :], m.ps[4][:, 0:P], m.t["block"],
                                          ALU.mult).then_inc(s["state"], 1)

                def norm(g):
                    dve.wait_ge(s["spread"], g + 1)
                    dve.tensor_scalar(m.R[:], m.ps[6][:], 1e-6, None, ALU.add).then_inc(s["den_eps"], 1)
                    dve.wait_ge(s["den_eps"], g + 1)
                    dve.reciprocal(m.R[:], m.R[:]).then_inc(s["rden"], 1)
                    dve.wait_ge(s["rden"], g + 1)
                    dve.tensor_tensor(m.Aall[:, g, :], m.Aall[:, g, :], m.R[:], ALU.mult
                                      ).then_inc(s["normed"], 1)

                masks(0)
                for g in range(NG):
                    if g + 1 < NG:
                        masks(g + 1)
                    if g:
                        norm(g - 1)
                norm(NG - 1)
                dve.wait_ge(s["out_sum"], 1)
                dve.tensor_tensor(flat(m.X), flat(m.X), m.ps[7][:], ALU.add).then_inc(s["residual"], 1)
        clear(nc, used)


def flat(x):
    return x[:].rearrange("p t d -> p (t d)")


def heads8(x):
    return x.rearrange("p (h d) -> p h d", d=8)


def tile4(padded, t, g):
    return padded[:, t, 4 * g:4 * g + 4, :].rearrange("p h d -> p (h d)")


def turn_heads(pe, m, s):
    for g in range(NG):
        for k, pad in enumerate((m.Qp, m.Kp)):
            n = 2 * g + k
            if n >= 2:
                pe.wait_ge(s["laid"], n - 1)
            for t in range(NT):
                mm = pe.transpose(m.ps[6 + n % 2][:, t * P:(t + 1) * P],
                                  tile4(pad, t, g), m.ident)
            mm.then_inc(s["turned"], 1)


def lay_heads(act, m, s, q_scale=1.0, k_scale=1.0, k_bias=0.0):
    for g in range(NG):
        for k, (all_heads, scale, bias) in enumerate(((m.QTall, q_scale, 0.0),
                                                      (m.KTall, k_scale, k_bias))):
            n = 2 * g + k
            act.wait_ge(s["turned"], n + 1)
            act.activation(all_heads[:, g, :], m.ps[6 + n % 2][:], ACT.Identity,
                           scale=scale, bias=bias).then_inc(s["laid"], 1)


def take_numden(act, m, s, g):
    act.wait_ge(s["numden"], g + 1)
    act.copy(m.Aall[:, g, :], m.ps[5][:]).then_inc(s["numden_out"], 1)


def spread_den(pe, m, s, g):
    pe.wait_ge(s["numden_out"], g + 1)
    if g:
        pe.wait_ge(s["normed"], g)
    pe.matmul(m.ps[6][:], m.t["spread8"], m.Aall[:, g, :], start=True, stop=True
              ).then_inc(s["spread"], 1)


def project(pe, m, s, bank, weights, started=False):
    for g in range(NG):
        pe.wait_ge(s["normed"], g + 1)
        for t in range(NT):
            mm = pe.matmul(bank[:, t * P:(t + 1) * P], m.Aall[:, g, t * P:(t + 1) * P],
                           weights[:, g * P:(g + 1) * P], start=(g == 0 and t == 0 and not started),
                           stop=(g == NG - 1), skip_group_check=True)
    mm.then_inc(s["out_sum"], 1)


WIDTH = [SEQ - t * P for t in range(NT)]
UNITS = [[(0, 0)], [(1, 0), (3, 384)], [(2, 0)]]
UNIT_AT = [0, 512, 1024]
KEYS_AT = [0, 512, 1024, 512 + 384]
HEAD_COLS = 1280


def unit_cols(u):
    return sum(WIDTH[kt] for kt, _ in UNITS[u])


def score_max(pe, m, q, k, bank_of, before, done):
    for i in range(NT):
        before(i)
        bank = m.ps[bank_of(i)]
        pe.matmul(bank[:, 0:(i + 1) * P], q[:, i * P:(i + 1) * P], k[:, 0:(i + 1) * P],
                  start=True, stop=False, skip_group_check=True)
        pe.matmul(bank[:, i * P:(i + 1) * P], m.identb[:], m.mask_qk[:], start=False, stop=True,
                  skip_group_check=True).then_inc(done, 1)


def score_unit(pe, m, q, k, u, bank, done):
    for n, (kt, at) in enumerate(UNITS[u]):
        pe.matmul(bank[:, at:at + WIDTH[kt]], k[:, kt * P:(kt + 1) * P], q[:, kt * P:SEQ],
                  start=(n == 0), stop=False, skip_group_check=True)
        mm = pe.matmul(bank[:, at:at + P], m.identb[:], m.mask_kq[:], start=False, stop=True,
                       skip_group_check=True)
    mm.then_inc(done, 1)


def weigh_values(pe, m, probs, values, rows, den_rows, num, den, ones):
    for kt in range(NT):
        p = probs[:, KEYS_AT[kt]:KEYS_AT[kt] + WIDTH[kt]]
        pe.matmul(num[rows, kt * P:SEQ], values(kt), p, start=(kt == 0), stop=(kt == NT - 1),
                  skip_group_check=True)
        mm = pe.matmul(den[den_rows, kt * P:SEQ], ones, p, start=(kt == 0), stop=(kt == NT - 1),
                       skip_group_check=True)
    return mm


def take_swapped(dve, to, bank, done):
    dve.tensor_copy(to[0:64, :], bank[64:P, :])
    dve.tensor_copy(to[64:P, :], bank[0:64, :]).then_inc(done, 1)


RMS_SEMS = "sq_sum sq_mean sq_std sq_rstd h_ready h_turned h_laid "
FFN_EPS = 1.1920929e-07


def rms_scalar_sum(act, m, s):
    for t in range(NT):
        act.activation(m.B1[:, t, 0:P], m.Y[:, t, :], ACT.Square, accum_out=m.sq[:, t:t + 1]
                       ).then_inc(s["sq_sum"], 1)


def rms_scalar_root(act, m, s):
    act.wait_ge(s["sq_mean"], 1)
    act.activation(m.std[:], m.var[:], ACT.Sqrt).then_inc(s["sq_std"], 1)


def rms_vector(dve, m, s):
    dve.wait_ge(s["sq_sum"], NT)
    dve.tensor_scalar(m.var[:], m.sq[:], 1.0 / D, FFN_EPS, ALU.mult, ALU.add).then_inc(s["sq_mean"], 1)
    dve.wait_ge(s["sq_std"], 1)
    dve.reciprocal(m.rstd[:], m.std[:]).then_inc(s["sq_rstd"], 1)
    dve.wait_ge(s["sq_rstd"], 1)
    for t in range(NT):
        dve.tensor_scalar(m.H[:, t, :], m.Y[:, t, :], m.rstd[:, t:t + 1], None, ALU.mult
                          ).then_inc(s["h_ready"], 1)


def rms_tensor(pe, m, s, bank):
    for t in range(NT):
        pe.wait_ge(s["h_ready"], t + 1)
        pe.transpose(m.ps[bank][:, t * P:(t + 1) * P], m.H[:, t, :], m.ident).then_inc(s["h_turned"], 1)


def rms_lay(act, m, s, bank, weight):
    act.wait_ge(s["h_turned"], NT)
    act.activation(m.YT[:], m.ps[bank][:], ACT.Copy, scale=weight).then_inc(s["h_laid"], 1)


def ffn_attention(nc, m):
    def keys(n):
        return m.hid[:, n, :] if n < 15 else m.PT[:, 0, :]

    def small_keys(n):
        return m.KB[:, n % 4, :] if n // 4 % 2 == 0 else (m.K1B, m.KWB)[n % 4 // 2][:, n % 2, :]

    def own_rows(n):
        return m.t["block"][:, 32 * (n % 4):32 * (n % 4) + 1]

    scale = 8 ** -0.5
    with ExitStack() as ctx:
        s, used = sems(nc, ctx, "fat", LN_SEMS + RMS_SEMS + "proj squared vcopy head_sum head_mean "
                       "head_std head_rstd phi turned laid q_small k_small keys max_scores maxed max_turned augmented "
                       "scores probs numden numden_out spread rden normed out_sum residual")
        with nc.Block() as block:

            @block.tensor
            def _(pe):
                rms_tensor(pe, m, s, 0)
                pe.wait_ge(s["h_laid"], 1)
                for t in range(NT):
                    pe.matmul(m.ps[1 + t][:, 0:384], m.YT[:, t * P:(t + 1) * P], m.w["f_wqkv"],
                              start=True, stop=True).then_inc(s["proj"], 1)
                pe.wait_ge(s["phi"], 8)
                turn_heads(pe, m, s)

                def rows(n):
                    return slice(32 * (n % 4), 32 * (n % 4) + 32)

                def first(n):
                    pe.wait_ge(s["q_small"], n // 4 + 1)
                    pe.wait_ge(s["k_small"], n + 1)

                    def before(i):
                        if 4 * n + i >= 2:
                            pe.wait_ge(s["maxed"], 4 * n + i - 1)
                    score_max(pe, m, m.QB[:, n // 4, :], small_keys(n), lambda i: i % 2, before,
                              s["max_scores"])

                def turn_maxes(g):
                    pe.wait_ge(s["maxed"], 16 * (g + 1))
                    if g:
                        pe.wait_ge(s["augmented"], g)
                    else:
                        pe.wait_ge(s["laid"], 2 * NG)
                    for t in range(NT):
                        mm = pe.transpose(m.ps[7][:, t * P:(t + 1) * P], m.NM[:, g % 2, t, :], m.ident)
                    mm.then_inc(s["max_turned"], 1)

                def second(n):
                    pe.wait_ge(s["augmented"], n // 4 + 1)
                    pe.wait_ge(s["keys"], n + 1)
                    for u in range(3):
                        if n:
                            pe.wait_ge(s["probs"], 3 * n + u - 2)
                        score_unit(pe, m, m.QTall[:, n // 4, :], keys(n), u, m.ps[2 + u], s["scores"])

                def values(n):
                    pe.wait_ge(s["probs"], 3 * n + 3)
                    if n % 4 == 0 and n:
                        pe.wait_ge(s["numden_out"], n // 4)
                    for kt in range(NT):
                        mm = pe.matmul(m.ps[5][rows(n), kt * P:SEQ], m.Vp[:, kt, n, :],
                                       m.probs[:, n % 3, KEYS_AT[kt]:KEYS_AT[kt] + WIDTH[kt]],
                                       start=(kt == 0), stop=(kt == NT - 1), skip_group_check=True)
                    if n % 4 == 3:
                        mm.then_inc(s["numden"], 1)

                for n in range(4):
                    first(n)
                turn_maxes(0)
                first(4)
                for n in range(17):
                    if n < 16:
                        second(n)
                    if n % 4 == 3 and n < 15:
                        turn_maxes(n // 4 + 1)
                    if n + 5 < 16:
                        first(n + 5)
                    if n > 1 and n % 4 == 1:
                        spread_den(pe, m, s, n // 4 - 1)
                    if n:
                        values(n - 1)
                spread_den(pe, m, s, NG - 1)
                project(pe, m, s, m.ps[0], m.w["f_wo"])

            @block.scalar
            def _(act):
                ln_scalar(act, m, s)
                act.wait_ge(s["ln_y"], NT)
                rms_scalar_sum(act, m, s)
                rms_scalar_root(act, m, s)
                rms_lay(act, m, s, 0, m.w["f_n1"])
                for t in range(NT):
                    act.wait_ge(s["proj"], t + 1)
                    act.activation(m.B2[:, t, :], m.ps[1 + t][:, 0:256], ACT.Square
                                   ).then_inc(s["squared"], 1)
                    act.copy(m.Vp[:, t, :, 0:8], heads8(m.ps[1 + t][:, 256:384])).then_inc(s["vcopy"], 1)
                act.wait_ge(s["head_mean"], 1)
                act.activation(m.hstd[:], m.hmean[:], ACT.Sqrt).then_inc(s["head_std"], 1)
                lay_heads(act, m, s, m.w["f_qn"], m.w["f_kn"], m.t["aug8"])
                act.wait_ge(s["laid"], 2)
                for n in range(4):
                    act.activation(keys(n), m.KTall[:, 0, :], ACT.Copy, scale=own_rows(n)
                                   ).then_inc(s["keys"], 1)
                for n in range(16):
                    for u in range(3):
                        act.wait_ge(s["scores"], 3 * n + u + 1)
                        act.activation(m.probs[:, n % 3, UNIT_AT[u]:UNIT_AT[u] + unit_cols(u)],
                                       m.ps[2 + u][:, 0:unit_cols(u)], ACT.Exp, scale=scale
                                       ).then_inc(s["probs"], 1)
                    if n and n % 4 == 0:
                        take_numden(act, m, s, n // 4 - 1)
                take_numden(act, m, s, NG - 1)

            @block.vector
            def _(dve):
                dve.memset(m.NM[:, :, :, 96:97], 0.0)
                ln_vector(dve, m, s)
                rms_vector(dve, m, s)
                for t in range(NT):
                    dve.wait_ge(s["squared"], t + 1)
                    dve.tensor_reduce(m.hsum[:, t, :], heads8(m.B2[:, t, :]), AX.X, ALU.add
                                      ).then_inc(s["head_sum"], 1)
                dve.wait_ge(s["head_sum"], NT)
                dve.tensor_scalar(m.hmean[:], flat(m.hsum), 0.125, FFN_EPS, ALU.mult, ALU.add
                                  ).then_inc(s["head_mean"], 1)
                dve.wait_ge(s["head_std"], 1)
                dve.reciprocal(flat(m.hsum), m.hstd[:]).then_inc(s["head_rstd"], 1)
                dve.wait_ge(s["head_rstd"], 1)
                dve.wait_ge(s["vcopy"], NT)
                for t in range(NT):
                    for k, pad in enumerate((m.Qp, m.Kp)):
                        dve.tensor_tensor(pad[:, t, :, 0:8], heads8(m.ps[1 + t][:, P * k:P * k + P]),
                                          m.hsum[:, t, 16 * k:16 * k + 16].unsqueeze(2)
                                          .to_broadcast([P, 16, 8]), ALU.mult).then_inc(s["phi"], 1)

                def largest(n):
                    g = n // 4
                    for i in range(NT):
                        dve.wait_ge(s["max_scores"], 4 * n + i + 1)
                        dve.tensor_reduce(m.NM[:, g % 2, i, 32 * (n % 4) + 8:32 * (n % 4) + 9],
                                          m.ps[i % 2][:, 0:(i + 1) * P], AX.X, ALU.max,
                                          negate=True).then_inc(s["maxed"], 1)

                def augment(g):
                    dve.wait_ge(s["q_small"], g + 1)
                    dve.wait_ge(s["max_turned"], g + 1)
                    dve.tensor_tensor(m.QTall[:, g, :], m.QTall[:, g, :], m.ps[7][:], ALU.add
                                      ).then_inc(s["augmented"], 1)

                def norm(g):
                    dve.wait_ge(s["spread"], g + 1)
                    dve.reciprocal(m.R[:], m.ps[6][:]).then_inc(s["rden"], 1)
                    dve.wait_ge(s["rden"], g + 1)
                    dve.tensor_tensor(m.Aall[:, g, :], m.Aall[:, g, :], m.R[:], ALU.mult
                                      ).then_inc(s["normed"], 1)

                for n in range(4):
                    largest(n)
                augment(0)
                largest(4)
                for n in range(17):
                    if n % 4 == 3 and n < 15:
                        augment(n // 4 + 1)
                    if n + 5 < 16:
                        largest(n + 5)
                    if n > 1 and n % 4 == 1:
                        norm(n // 4 - 1)
                norm(NG - 1)
                dve.wait_ge(s["out_sum"], 1)
                dve.tensor_tensor(m.Y[:, :, 32:P], m.Y[:, :, 32:P],
                                  m.ps[0][:].rearrange("p (t d) -> p t d", t=NT)[:, :, 32:P],
                                  ALU.add).then_inc(s["residual"], 1)

            @block.gpsimd
            def _(pool):
                for g in range(NG):
                    pool.wait_ge(s["laid"], 2 * g + 1)
                    pool.tensor_copy(m.QB[:, g, :], m.QTall[:, g, :]).then_inc(s["q_small"], 1)
                    pool.wait_ge(s["laid"], 2 * g + 2)
                    if g >= 2:
                        pool.wait_ge(s["max_scores"], 16 * (g - 1))
                    for n in range(4 * g, 4 * g + 4):
                        pool.tensor_scalar(small_keys(n), m.KTall[:, g, :], own_rows(n), None, ALU.mult
                                           ).then_inc(s["k_small"], 1)
                    if g:
                        pool.wait_ge(s["keys"], 4 * g)
                        for n in range(4 * g, 4 * g + 4):
                            pool.tensor_scalar(keys(n), m.KTall[:, g, :], own_rows(n), None, ALU.mult
                                               ).then_inc(s["keys"], 1)
        clear(nc, used)


HIDDEN = [
    ("e0_0", (), "f_e0_up", 0, ACT.Gelu), ("e0_1", (), "f_e0_up", 128, ACT.Gelu),
    ("e2a_0", (), "f_e2_l1", 0, ACT.Gelu), ("e2a_1", (), "f_e2_l1", 128, ACT.Gelu),
    ("e3a", (), "f_e3_dn", 0, ACT.Gelu),
    ("e2b_0", ("e2a_0", "e2a_1"), "f_e2_l2", 0, ACT.Gelu),
    ("e2b_1", ("e2a_0", "e2a_1"), "f_e2_l2", 128, ACT.Gelu),
    ("e3b_0", ("e3a",), "f_e3_up", 0, ACT.Gelu), ("e3b_1", ("e3a",), "f_e3_up", 128, ACT.Gelu),
    ("e2c_0", ("e2b_0", "e2b_1"), "f_e2_l3", 0, ACT.Gelu),
    ("e2c_1", ("e2b_0", "e2b_1"), "f_e2_l3", 128, ACT.Gelu),
    ("e1v_0", (), "f_e1_w2", 0, ACT.Copy), ("e1v_1", (), "f_e1_w2", 128, ACT.Copy),
    ("e1g_0", (), "f_e1_w1", 0, ACT.Silu), ("e1g_1", (), "f_e1_w1", 128, ACT.Silu),
]
TILE = {h[0]: n for n, h in enumerate(HIDDEN)}
EXPERT_OUT = [(6, 0, ("e0_0", "e0_1"), "f_e0_dn"), (11, 3, ("e3b_0", "e3b_1"), "f_e3_out"),
              (13, 2, ("e2c_0", "e2c_1"), "f_e2_l4"), (14, 1, ("e1g_0", "e1g_1"), "f_e1_dn")]
FLOAT_MAX = float(np.finfo(np.float32).max)


def experts(nc, m):
    with ExitStack() as ctx:
        s, used = sems(nc, ctx, "moe", RMS_SEMS + "gate_sum logits gmax gshift gexp gsum grec probs gt "
                       "eq eqlow rank_terms rank kept top topsum topeps toprec weights hidden_sum hidden gated out_sum "
                       "mixed residual")
        with nc.Block() as block:

            @block.tensor
            def _(pe):
                rms_tensor(pe, m, s, 0)
                pe.wait_ge(s["h_laid"], 1)
                for t in range(NT):
                    mm = pe.matmul(m.ps[7][:, 4 * t:4 * t + 4], m.YT[:, t * P:(t + 1) * P],
                                   m.w["f_gate"], start=True, stop=True)
                mm.then_inc(s["gate_sum"], 1)
                outs = list(EXPERT_OUT)
                done = 0
                for n, (name, sources, w, at, func) in enumerate(HIDDEN):
                    if n >= 6:
                        pe.wait_ge(s["hidden"], n - 5)
                    for k, src in enumerate(sources or (None,)):
                        if src:
                            pe.wait_ge(s["hidden"], TILE[src] + 1)
                        rhs = m.hid[:, TILE[src], :] if src else m.YT[:]
                        mm = pe.matmul(m.ps[n % 6][:], m.w[w][:, 256 * k + at:256 * k + at + P], rhs,
                                       start=(k == 0), stop=(k == max(len(sources), 1) - 1))
                    mm.then_inc(s["hidden_sum"], 1)
                    while outs and outs[0][0] == n:
                        _, e, (a, b), w = outs.pop(0)
                        pe.wait_ge(s["hidden"], max(TILE[a], TILE[b]) + 1)
                        if e == 1:
                            pe.wait_ge(s["gated"], 2)
                        if done == 0:
                            pe.wait_ge(s["logits"], 1)
                        if done >= 2:
                            pe.wait_ge(s["mixed"], 4 * (done - 1))
                        for t in range(NT):
                            r = slice(t * P, (t + 1) * P)
                            pe.matmul(m.ps[6 + done % 2][:, r], m.hid[:, TILE[a], r], m.w[w][:, 0:P],
                                      start=(t == 0), stop=False, skip_group_check=True)
                            mm = pe.matmul(m.ps[6 + done % 2][:, r], m.hid[:, TILE[b], r],
                                           m.w[w][:, P:256], start=False, stop=True,
                                           skip_group_check=True)
                        mm.then_inc(s["out_sum"], 1)
                        done += 1

            @block.scalar
            def _(act):
                rms_scalar_sum(act, m, s)
                rms_scalar_root(act, m, s)
                rms_lay(act, m, s, 0, m.w["f_n2"])
                act.wait_ge(s["gshift"], 1)
                act.activation(m.g16b[:], m.g16[:], ACT.Exp).then_inc(s["gexp"], 1)
                for n, (name, sources, w, at, func) in enumerate(HIDDEN):
                    act.wait_ge(s["hidden_sum"], n + 1)
                    act.activation(m.hid[:, n, :], m.ps[n % 6][:], func).then_inc(s["hidden"], 1)

            @block.vector
            def _(dve):
                rms_vector(dve, m, s)
                te = lambda x: x[:].rearrange("p (t e) -> p t e", e=4)
                over = lambda x: x.unsqueeze(2).to_broadcast([P, NT, 4])
                dve.wait_ge(s["gate_sum"], 1)
                dve.tensor_scalar(m.g16[:], m.ps[7][:, 0:16], FLOAT_MAX, -FLOAT_MAX, ALU.min, ALU.max
                                  ).then_inc(s["logits"], 1)
                dve.wait_ge(s["logits"], 1)
                dve.tensor_reduce(m.g4[:], te(m.g16), AX.X, ALU.max).then_inc(s["gmax"], 1)
                dve.wait_ge(s["gmax"], 1)
                dve.tensor_tensor(te(m.g16), te(m.g16), over(m.g4[:]), ALU.subtract
                                  ).then_inc(s["gshift"], 1)
                dve.wait_ge(s["gexp"], 1)
                dve.tensor_reduce(m.g4[:], te(m.g16b), AX.X, ALU.add).then_inc(s["gsum"], 1)
                dve.wait_ge(s["gsum"], 1)
                dve.reciprocal(m.g4b[:], m.g4[:]).then_inc(s["grec"], 1)
                dve.wait_ge(s["grec"], 1)
                dve.tensor_tensor(te(m.g16), te(m.g16b), over(m.g4b[:]), ALU.mult
                                  ).then_inc(s["probs"], 1)
                dve.wait_ge(s["probs"], 1)
                others = te(m.g16).unsqueeze(2).to_broadcast([P, NT, 4, 4])
                own = te(m.g16).unsqueeze(3).to_broadcast([P, NT, 4, 4])
                t44 = lambda x: x[:].rearrange("p (t e f) -> p t e f", t=NT, e=4)
                dve.tensor_tensor(t44(m.g64), others, own, ALU.is_gt).then_inc(s["gt"], 1)
                dve.tensor_tensor(t44(m.g64b), others, own, ALU.is_equal).then_inc(s["eq"], 1)
                dve.wait_ge(s["eq"], 1)
                low = m.t["lower4"].unsqueeze(1).to_broadcast([P, NT, 16])
                t16 = lambda x: x[:].rearrange("p (t e) -> p t e", t=NT)
                dve.tensor_tensor(t16(m.g64b), t16(m.g64b), low, ALU.mult).then_inc(s["eqlow"], 1)
                dve.wait_ge(s["eqlow"], 1)
                dve.wait_ge(s["gt"], 1)
                dve.tensor_tensor(m.g64[:], m.g64[:], m.g64b[:], ALU.add).then_inc(s["rank_terms"], 1)
                dve.wait_ge(s["rank_terms"], 1)
                dve.tensor_reduce(m.g16b[:], m.g64[:].rearrange("p (n f) -> p n f", f=4), AX.X,
                                  ALU.add).then_inc(s["rank"], 1)
                dve.wait_ge(s["rank"], 1)
                dve.scalar_tensor_tensor(m.top[:], m.g16b[:], 1.5, m.g16[:], ALU.is_lt, ALU.mult
                                         ).then_inc(s["kept"], 1)
                dve.wait_ge(s["kept"], 1)
                dve.tensor_reduce(m.g4[:], te(m.top), AX.X, ALU.add).then_inc(s["topsum"], 1)
                dve.wait_ge(s["topsum"], 1)
                dve.tensor_scalar(m.g4[:], m.g4[:], 1e-8, None, ALU.add).then_inc(s["topeps"], 1)
                dve.wait_ge(s["topeps"], 1)
                dve.reciprocal(m.g4b[:], m.g4[:]).then_inc(s["toprec"], 1)
                dve.wait_ge(s["toprec"], 1)
                dve.tensor_tensor(te(m.top), te(m.top), over(m.g4b[:]), ALU.mult
                                  ).then_inc(s["weights"], 1)
                dve.wait_ge(s["weights"], 1)
                for n, (_, e, _, _) in enumerate(EXPERT_OUT):
                    if e == 1:
                        for k in range(2):
                            dve.wait_ge(s["hidden"], TILE["e1g_1"] + 1)
                            dve.tensor_tensor(m.hid[:, TILE["e1g_0"] + k, :],
                                              m.hid[:, TILE["e1g_0"] + k, :],
                                              m.hid[:, TILE["e1v_0"] + k, :], ALU.mult
                                              ).then_inc(s["gated"], 1)
                    dve.wait_ge(s["out_sum"], n + 1)
                    for t in range(NT):
                        w = m.top[:, 4 * t + e:4 * t + e + 1]
                        o = m.ps[6 + n % 2][:, t * P + 32:(t + 1) * P]
                        if n:
                            dve.wait_ge(s["mixed"], 4 * (n - 1) + t + 1)
                        dve.scalar_tensor_tensor(m.Y[:, t, 32:P], o, w, m.Y[:, t, 32:P], ALU.mult,
                                                 ALU.add).then_inc(s["mixed"], 1)
                dve.wait_ge(s["mixed"], 16)
                dve.tensor_tensor(flat(m.X), flat(m.X), flat(m.Y), ALU.add).then_inc(s["residual"], 1)
        clear(nc, used)


MLA_EPS = 1e-6
KEEP = 32
LATENT, SELECTED, WINDOW = 0, 1, 2
W_Q, W_WIN, W_SEL, W_LATENT = 0, 2, 4, 6
JOBS = [(g, x, j) for g in range(NG)
        for x, j in [(LATENT, j) for j in range(4)] + [(WINDOW, j) for j in range(4)] + [(SELECTED, 0)]]
PER_GROUP = 9


def preparations():
    order, upto = [("q", 0, j) for j in range(4)] + [JOBS[0], JOBS[1]], []
    for k in range(len(JOBS)):
        if k + 2 < len(JOBS):
            order.append(JOBS[k + 2])
        g, local = divmod(k, PER_GROUP)
        if local < 4 and g + 1 < NG:
            order.append(("q", g + 1, local))
        upto.append(len(order))
    return order, upto


PREPS, PREPS_UPTO = preparations()
PREP_AT = {item: n for n, item in enumerate(PREPS)}
FIRST_PREPS = 6
JOB_UNITS = [1 if x == SELECTED else 3 for _, x, _ in JOBS]
UNITS_BEFORE = [sum(JOB_UNITS[:k]) for k in range(len(JOBS) + 1)]
MAXES = [1 if x == SELECTED else NT for _, x, _ in JOBS]
MAXES_BEFORE = [sum(MAXES[:k]) for k in range(len(JOBS) + 1)]
def ends_kind(k):
    g, x, j = JOBS[k]
    return x == SELECTED or j == 3


KINDS_BEFORE = [sum(ends_kind(i) for i in range(k)) for k in range(len(JOBS) + 1)]


def mla_prepare(nc, m):
    with ExitStack() as ctx:
        s, used = sems(nc, ctx, "mpre", LN_SEMS + "chain latent squares means roots normed turned laid "
                       "krope gate_sum gates_in gate_mean gmax gexp gates v1 vw imp imp_read before_sum "
                       "kept onehot picked picked_laid vs vs_read v1_read vw_read")
        with nc.Block() as block:

            @block.tensor
            def _(pe):
                ln_tensor(pe, m, s, 0)
                pe.wait_ge(s["ln_yt"], 1)
                cq = W_AT["m_cq"][0]
                for t in range(NT):
                    pe.matmul(m.ps[1][:, t * P:(t + 1) * P], m.YT[:, t * P:(t + 1) * P],
                              m.w_all[:, cq:cq + P], start=True, stop=True).then_inc(s["latent"], 1)
                pe.matmul(m.ps[2][:], m.w["m_imp"], m.YT[:], start=True, stop=True).then_inc(s["imp"], 1)
                for k in range(2):
                    mm = pe.matmul(m.ps[3 + k][0:64, :], m.w["m_krope"][:, 64 * k:64 * k + 64], m.YT[:],
                                   start=True, stop=True)
                mm.then_inc(s["krope"], 1)
                for t in range(NT):
                    mm = pe.matmul(m.ps[5][:, 4 * t:4 * t + 3], m.YT[:, t * P:(t + 1) * P],
                                   m.w["m_gate"], start=True, stop=True)
                mm.then_inc(s["gate_sum"], 1)
                pe.wait_ge(s["gates_in"], 1)
                for t in range(NT):
                    mm = pe.matmul(m.ps[6][:, 0:3], m.ones[:], m.small[:, 4 * t:4 * t + 3],
                                   start=(t == 0), stop=(t == NT - 1))
                mm.then_inc(s["gate_mean"], 1)
                for t in range(NT):
                    pe.wait_ge(s["normed"], 2 * t + 2)
                    mm = pe.transpose(m.ps[7][:, t * P:(t + 1) * P], m.H[:, t, :], m.ident)
                mm.then_inc(s["turned"], 1)
                pe.wait_ge(s["kept"], 1)
                pe.matmul(m.ps[6][:, 8:12], m.t["before"], m.small[:, 20:24], start=True, stop=False,
                          skip_group_check=True)
                for t in range(1, NT):
                    mm = pe.matmul(m.ps[6][:, 8 + t:12], m.ones[:], m.small[:, 20:24 - t],
                                   start=False, stop=True, skip_group_check=True)
                mm.then_inc(s["before_sum"], 1)
                pe.wait_ge(s["onehot"], 4)
                for t in range(NT):
                    mm = pe.matmul(m.ps[5][:, 0:P], m.Y[:, t, :], m.onehot[:, t, :],
                                   start=(t == 0), stop=(t == NT - 1))
                mm.then_inc(s["picked"], 1)
                pe.wait_ge(s["laid"], 1)
                for n in range(2 * NT):
                    t, wide = n % NT, n // NT
                    if n == 0:
                        pe.wait_ge(s["v1_read"], 1)
                    if n >= 2:
                        pe.wait_ge(s["vw_read"], n - 1)
                    src = (m.YT if wide else m.NCT)[:, t * P:(t + 1) * P]
                    pe.matmul(m.ps[3 + n % 2][:], src, m.w["m_winv" if wide else "m_dv"],
                              start=True, stop=True).then_inc(s["v1"], 1)
                pe.wait_ge(s["picked_laid"], 1)
                pe.matmul(m.ps[0][:], m.SELT, m.w["m_selv"], start=True, stop=True
                          ).then_inc(s["vs"], 1)

            @block.scalar
            def _(act):
                ln_scalar(act, m, s)
                ln_copy(act, m, s, 0)
                act.wait_ge(s["latent"], NT)
                for t in range(NT):
                    act.activation(m.B1[:, t, 0:96], m.ps[1][:, t * P:t * P + 96], ACT.Square,
                                   accum_out=m.small[:, 24 + t:25 + t]).then_inc(s["squares"], 1)
                    act.activation(m.B1[:, t, 96:P], m.ps[1][:, t * P + 96:(t + 1) * P], ACT.Square,
                                   accum_out=m.small[:, 28 + t:29 + t]).then_inc(s["squares"], 1)
                act.wait_ge(s["means"], 1)
                act.activation(m.small[:, 40:48], m.small[:, 32:40], ACT.Sqrt).then_inc(s["roots"], 1)
                act.wait_ge(s["turned"], 1)
                act.activation(m.NCT, m.ps[7][:], ACT.Copy, scale=m.w["m_gqkv"]).then_inc(s["laid"], 1)
                act.wait_ge(s["gmax"], 1)
                act.activation(m.small[:, 52:55], m.small[:, 48:51], ACT.Exp,
                               bias=m.small[:, 51:52]).then_inc(s["gexp"], 1)
                act.wait_ge(s["picked"], 1)
                act.copy(m.SELT, m.ps[5][:, 0:P]).then_inc(s["picked_laid"], 1)
                act.wait_ge(s["gates"], 1)
                for n in range(2 * NT):
                    t, wide = n % NT, n // NT
                    act.wait_ge(s["v1"], n + 1)
                    act.activation((m.VW if wide else m.V1)[:, t, :, :].rearrange("p h d -> p (h d)"),
                                   m.ps[3 + n % 2][:], ACT.Copy,
                                   scale=m.gates[:, 2 * wide:2 * wide + 1]).then_inc(s["vw_read"], 1)

            @block.vector
            def _(dve):
                count = [0]

                def link(ins):
                    count[0] += 1
                    ins.then_inc(s["chain"], 1)
                    dve.wait_ge(s["chain"], count[0])

                dve.memset(m.NM[:, :, :, 8:P:32], 0.0)
                ln_vector(dve, m, s)
                dve.wait_ge(s["squares"], 8)
                link(dve.tensor_scalar(m.small[:, 32:36], m.small[:, 24:28], 1.0 / 96, MLA_EPS,
                                       ALU.mult, ALU.add))
                dve.tensor_scalar(m.small[:, 36:40], m.small[:, 28:32], 1.0 / 32, MLA_EPS,
                                  ALU.mult, ALU.add).then_inc(s["means"], 1)
                dve.wait_ge(s["roots"], 1)
                link(dve.reciprocal(m.small[:, 56:64], m.small[:, 40:48]))
                for t in range(NT):
                    dve.tensor_scalar(m.H[:, t, 0:96], m.ps[1][:, t * P:t * P + 96],
                                      m.small[:, 56 + t:57 + t], None, ALU.mult).then_inc(s["normed"], 1)
                    dve.tensor_scalar(m.H[:, t, 96:P], m.ps[1][:, t * P + 96:(t + 1) * P],
                                      m.small[:, 60 + t:61 + t], None, ALU.mult).then_inc(s["normed"], 1)
                dve.wait_ge(s["gate_sum"], 1)
                dve.tensor_copy(m.small[:, 0:16].rearrange("p (t e) -> p t e", e=4)[:, :, 0:3],
                                m.ps[5][:, 0:16].rearrange("p (t e) -> p t e", e=4)[:, :, 0:3]
                                ).then_inc(s["gates_in"], 1)
                dve.wait_ge(s["gate_mean"], 1)
                link(dve.tensor_scalar(m.small[:, 48:51], m.ps[6][:, 0:3], 1.0 / SEQ, None, ALU.mult))
                dve.tensor_reduce(m.small[:, 51:52], m.small[:, 48:51], AX.X, ALU.max, negate=True
                                  ).then_inc(s["gmax"], 1)
                dve.wait_ge(s["gexp"], 1)
                link(dve.tensor_reduce(m.small[:, 55:56], m.small[:, 52:55], AX.X, ALU.add))
                link(dve.reciprocal(m.small[:, 16:17], m.small[:, 55:56]))
                dve.tensor_scalar(m.gates[:], m.small[:, 52:55], m.small[:, 16:17], None, ALU.mult
                                  ).then_inc(s["gates"], 1)
                dve.wait_ge(s["krope"], 1)
                link(dve.scalar_tensor_tensor(m.R[0:64, :], m.ps[3][0:64, :], 1.0 / 16,
                                              m.t["rope_c"][0:64, :], ALU.mult, ALU.mult))
                link(dve.scalar_tensor_tensor(m.A[0:64, :], m.ps[4][0:64, :], 1.0 / 16,
                                              m.t["rope_s"][0:64, :], ALU.mult, ALU.mult))
                for k in range(2):
                    ins = dve.tensor_tensor(m.K1[0:64, k, :], m.R[0:64, :], m.A[0:64, :], ALU.add)
                    dve_bf = dve.tensor_tensor(m.K1B[0:64, k, :], m.R[0:64, :], m.A[0:64, :], ALU.add)
                dve_bf.then_inc(s["v1_read"], 1)
                dve.wait_ge(s["imp"], 1)
                link(dve.tensor_copy(m.imp, m.ps[2][:]))
                for t in range(NT):
                    link(dve.tensor_tensor(m.H2, m.imp[:, t * P:(t + 1) * P], m.ident, ALU.mult))
                    link(dve.tensor_reduce(m.own[:, t:t + 1], m.H2, AX.X, ALU.add))
                for t in range(NT):
                    link(dve.tensor_scalar(m.R[:], m.imp, m.own[:, t:t + 1], None, ALU.is_gt))
                    link(dve.tensor_reduce(m.own[:, 4 + t:5 + t], m.R[:], AX.X, ALU.add))
                    if t:
                        link(dve.tensor_scalar(m.R[:, 0:t * P], m.imp[:, 0:t * P], m.own[:, t:t + 1], None,
                                               ALU.is_equal))
                    r = slice(t * P, (t + 1) * P)
                    link(dve.scalar_tensor_tensor(m.R[:, r], m.imp[:, r], m.own[:, t:t + 1],
                                                  m.t["below"], ALU.is_equal, ALU.mult))
                    link(dve.tensor_reduce(m.own[:, 8 + t:9 + t], m.R[:, 0:(t + 1) * P], AX.X, ALU.add))
                link(dve.tensor_tensor(m.own[:, 12:16], m.own[:, 4:8], m.own[:, 8:12], ALU.add))
                dve.tensor_scalar(m.small[:, 20:24], m.own[:, 12:16], KEEP - 0.5, None, ALU.is_lt
                                  ).then_inc(s["kept"], 1)
                dve.wait_ge(s["before_sum"], 1)
                link(dve.tensor_copy(m.own[:, 16:20], m.ps[6][:, 8:12]))
                for t in range(NT):
                    dve.tensor_scalar(m.onehot[:, t, :].rearrange("p (r k) -> p r k", k=KEEP),
                                      m.t["iota"].unsqueeze(1).to_broadcast([P, 4, KEEP]),
                                      m.own[:, 16 + t:17 + t], m.small[:, 20 + t:21 + t],
                                      ALU.is_equal, ALU.mult).then_inc(s["onehot"], 1)
                dve.wait_ge(s["vs"], 1)
                dve.scalar_tensor_tensor(
                    m.VS, m.ps[0][:].rearrange("p (g n) -> p g n", g=NG), m.gates[:, 1:2],
                    m.t["block"][:, 0:P].unsqueeze(1).to_broadcast([P, NG, P]), ALU.mult, ALU.mult
                    ).then_inc(s["vs_read"], 1)
        clear(nc, used)


def mla_heads(nc, m, mw):
    scale = 96 ** -0.5
    with ExitStack() as ctx:
        s, used = sems(nc, ctx, "mla", "weights_even weights_odd prep plain roped added small max_scores maxed "
                       "max_turned augmented scores probs numden num_out den_out rden part normed out_sum residual")

        def landed(g):
            return (s["weights_even"], s["weights_odd"])[g % 2]

        def wt(g, part, j):
            at = 384 * part + 96 * j
            return m.mw[:, g % 2, at:at + 96]

        def q_tile(g, j):
            return m.Q[:, (g % 2) * 4 + j, :]

        def k_tile(k):
            _, x, j = JOBS[k]
            return (m.K1 if x == LATENT else m.KW)[0:97, j % 2, :]

        with nc.Block() as block:

            @block.sync
            def _(sp):
                for g in range(NG):
                    if g >= 2:
                        sp.wait_ge(s["prep"], PREP_AT[(g - 2, SELECTED, 0)] + 1)
                    sp.dma_start(m.mw[:, g % 2, :], mw[g]).then_inc(landed(g), 16)

            @block.tensor
            def _(pe):
                def prepare(p):
                    kind, a, b = PREPS[p]
                    g = a if kind == "q" else kind
                    pe.wait_ge(landed(g), 16 * (g // 2 + 1))
                    if p:
                        pe.wait_ge(s["roped"], p)
                    A, B = m.ps[6], m.ps[7]
                    if kind != "q" and a == LATENT:
                        mm = pe.matmul(A[0:96, :], wt(g, W_LATENT, b), m.NCT, start=True, stop=True)
                    elif kind != "q" and a == SELECTED:
                        for k, bank in enumerate((A, B)):
                            for j in range(4):
                                mm = pe.matmul(bank[0:96, KEEP * j:KEEP * j + KEEP], wt(g, W_SEL + k, j),
                                               m.SELT[:, 0:KEEP], start=True, stop=True)
                    else:
                        part, src, j = (W_Q, m.NCT, b) if kind == "q" else (W_WIN, m.YT[:], b)
                        for k, bank in enumerate((A, B)):
                            mm = pe.matmul(bank[0:96, :], wt(g, part + k, j), src, start=True,
                                           stop=True)
                    mm.then_inc(s["prep"], 1)

                def first(k):
                    g, x, j = JOBS[k]
                    pe.wait_ge(s["small"], PREP_AT[JOBS[k]] + 1)
                    if k:
                        pe.wait_ge(s["augmented"], MAXED_ROWS[k])
                    if x == SELECTED:
                        for t in range(NT):
                            for h in range(4):
                                c = t * P + KEEP * h
                                mm = pe.matmul(m.ps[0][:, c:c + KEEP],
                                               m.QB[0:96, 4 * (g % 2) + h, t * P:(t + 1) * P],
                                               m.KSB[0:96, KEEP * h:KEEP * h + KEEP],
                                               start=True, stop=True)
                        mm.then_inc(s["max_scores"], 1)
                    else:
                        def before(i):
                            if i >= 2:
                                pe.wait_ge(s["maxed"], MAXES_BEFORE[k] + i - 1)
                        score_max(pe, m, m.QB[0:96, 4 * (g % 2) + j, :],
                                  (m.K1B if x == LATENT else m.KWB)[0:96, j % 2, :],
                                  lambda i: i % 2, before, s["max_scores"])

                def turn_max(k, h):
                    for t in range(NT):
                        mm = pe.transpose(m.ps[0][:, t * P:(t + 1) * P], m.NMm[:, h, t, :], m.ident)
                    mm.then_inc(s["max_turned"], 1)

                def turn_maxes(k):
                    pe.wait_ge(s["maxed"], MAXES_BEFORE[k + 1])
                    for h in range(4 if JOBS[k][1] == SELECTED else 1):
                        if h:
                            pe.wait_ge(s["augmented"], MAXED_ROWS[k] + h)
                        turn_max(k, h)

                def second(k):
                    g, x, j = JOBS[k]
                    pe.wait_ge(s["augmented"], MAXED_ROWS[k + 1])
                    for u in range(JOB_UNITS[k]):
                        n = UNITS_BEFORE[k] + u
                        if n >= 2:
                            pe.wait_ge(s["probs"], n - 1)
                        if x == SELECTED:
                            for h in range(4):
                                mm = pe.matmul(m.ps[2 + n % 2][32 * h:32 * h + 32, :],
                                               m.KS[0:97, KEEP * h:KEEP * h + KEEP],
                                               q_tile(g, h)[0:97, :], start=True, stop=True)
                            mm.then_inc(s["scores"], 1)
                        else:
                            score_unit(pe, m, q_tile(g, j)[0:97, :], k_tile(k), u, m.ps[2 + n % 2],
                                       s["scores"])

                def values(k):
                    g, x, j = JOBS[k]
                    pe.wait_ge(s["probs"], UNITS_BEFORE[k + 1])
                    if (x == SELECTED or j == 0) and KINDS_BEFORE[k]:
                        pe.wait_ge(s["num_out"], KINDS_BEFORE[k])
                        pe.wait_ge(s["den_out"], KINDS_BEFORE[k])
                    if x == SELECTED:
                        pe.matmul(m.ps[4][:], m.VS[:, g, :], m.probs[:, k % 3, 0:SEQ], start=True,
                                  stop=True)
                        for to, at in ((0, 64), (64, 0)):
                            mm = pe.matmul(m.ps[5][to:to + 64, :], m.t["block"][:, at:at + 64],
                                           m.probs[:, k % 3, 0:SEQ], start=True, stop=True)
                    else:
                        v = m.V1 if x == LATENT else m.VW
                        mm = weigh_values(pe, m, m.probs[:, k % 3, :], lambda kt: v[:, kt, 4 * g + j, :],
                                          slice(32 * j, 32 * j + 32),
                                          slice(32 * ((j + 2) % 4), 32 * ((j + 2) % 4) + 32),
                                          m.ps[4], m.ps[5], m.ones[:, 0:32])
                    if ends_kind(k):
                        mm.then_inc(s["numden"], 1)

                for p in range(FIRST_PREPS):
                    prepare(p)
                first(0)
                turn_maxes(0)
                done = FIRST_PREPS
                for k in range(len(JOBS) + 1):
                    if k < len(JOBS):
                        second(k)
                    if k + 1 < len(JOBS):
                        first(k + 1)
                    if k:
                        values(k - 1)
                    if k + 1 < len(JOBS):
                        turn_maxes(k + 1)
                    if k < len(JOBS):
                        while done < PREPS_UPTO[k]:
                            prepare(done)
                            done += 1
                pe.wait_ge(s["normed"], 3 * NG)
                for g in range(NG):
                    for t in range(NT):
                        mm = pe.matmul(m.ps[0][:, t * P:(t + 1) * P], m.Aall[:, g, t * P:(t + 1) * P],
                                       m.w["m_proj"][:, g * P:(g + 1) * P], start=(g == 0 and t == 0),
                                       stop=(g == NG - 1), skip_group_check=True)
                mm.then_inc(s["out_sum"], 1)

            @block.scalar
            def _(act):
                def augment(k):
                    g, x, j = JOBS[k]
                    for h in range(4 if x == SELECTED else 1):
                        act.wait_ge(s["max_turned"], MAXED_ROWS[k] + h + 1)
                        act.copy(q_tile(g, h if x == SELECTED else j)[96:97, :], m.ps[0][96:97, :]
                                 ).then_inc(s["augmented"], 1)

                def take_num(k):
                    n = KINDS_BEFORE[k]
                    act.wait_ge(s["numden"], n + 1)
                    if n:
                        act.wait_ge(s["normed"], n)
                    act.copy(m.A[:], m.ps[4][:]).then_inc(s["num_out"], 1)

                augment(0)
                for k in range(len(JOBS)):
                    for u in range(JOB_UNITS[k]):
                        n = UNITS_BEFORE[k] + u
                        cols = SEQ if JOBS[k][1] == SELECTED else unit_cols(u)
                        act.wait_ge(s["scores"], n + 1)
                        act.activation(m.probs[:, k % 3, UNIT_AT[u]:UNIT_AT[u] + cols],
                                       m.ps[2 + n % 2][:, 0:cols], ACT.Exp, scale=scale
                                       ).then_inc(s["probs"], 1)
                    if k and ends_kind(k - 1):
                        take_num(k - 1)
                    if k + 1 < len(JOBS):
                        augment(k + 1)
                take_num(len(JOBS) - 1)

            @block.vector
            def _(dve):
                def rope(p):
                    kind, a, b = PREPS[p]
                    dve.wait_ge(s["prep"], p + 1)
                    if kind != "q" and a == LATENT:
                        dve.tensor_copy(m.K1[64:96, b % 2, :], m.ps[6][64:96, :]).then_inc(s["roped"], 1)
                        return
                    n = SWAPS_BEFORE[p]
                    if kind != "q" and a == SELECTED:
                        heads = lambda x: x.rearrange("p (h k) -> p h k", k=KEEP)
                        A, B = heads(m.ps[6][0:96, 0:P]), heads(m.ps[7][0:96, 0:P])
                        C, S = (m.t[c][:, 0:KEEP].unsqueeze(1).to_broadcast([96, 4, KEEP])
                                for c in ("rope_c", "rope_s"))
                        to, tmp = heads(m.KS[0:96, :]), heads(m.R2[n % 2][0:96, 0:P])
                    else:
                        A, B, C, S = m.ps[6][0:96, :], m.ps[7][0:96, :], m.t["rope_c"], m.t["rope_s"]
                        to = q_tile(a, b)[0:96, :] if kind == "q" else m.KW[0:96, b % 2, :]
                        tmp = m.R2[n % 2][0:96, :]
                    dve.tensor_tensor(to, A, C, ALU.mult).then_inc(s["plain"], 1)
                    if n >= 2:
                        dve.wait_ge(s["added"], n - 1)
                    dve.tensor_tensor(tmp, B, S, ALU.mult).then_inc(s["roped"], 1)

                def largest(k):
                    g, x, j = JOBS[k]
                    if x == SELECTED:
                        dve.wait_ge(s["max_scores"], MAXES_BEFORE[k] + 1)
                        dve.tensor_reduce(m.NMm[:, :, :, 96:97].rearrange("p h t o -> p t (h o)"),
                                          m.ps[0][:].rearrange("p (t h k) -> p t h k", t=NT, h=4),
                                          AX.X, ALU.max, negate=True).then_inc(s["maxed"], 1)
                        return
                    for i in range(NT):
                        dve.wait_ge(s["max_scores"], MAXES_BEFORE[k] + i + 1)
                        dve.tensor_reduce(m.NMm[:, 0, i, 96:97], m.ps[i % 2][:, 0:(i + 1) * P], AX.X,
                                          ALU.max, negate=True).then_inc(s["maxed"], 1)

                def take_den(k):
                    n = KINDS_BEFORE[k]
                    dve.wait_ge(s["numden"], n + 1)
                    take_swapped(dve, m.R, m.ps[5], s["den_out"])

                def norm(k):
                    g, x, j = JOBS[k]
                    n = KINDS_BEFORE[k]
                    dve.wait_ge(s["den_out"], n + 1)
                    dve.reciprocal(m.R[:], m.R[:]).then_inc(s["rden"], 1)
                    dve.wait_ge(s["rden"], n + 1)
                    dve.wait_ge(s["num_out"], n + 1)
                    if x == LATENT:
                        dve.tensor_tensor(m.Aall[:, g, :], m.A[:], m.R[:], ALU.mult
                                          ).then_inc(s["normed"], 1)
                        return
                    dve.tensor_tensor(m.A[:], m.A[:], m.R[:], ALU.mult).then_inc(s["part"], 1)
                    dve.wait_ge(s["part"], n - g)
                    dve.wait_ge(s["normed"], n)
                    dve.tensor_tensor(m.Aall[:, g, :], m.Aall[:, g, :], m.A[:], ALU.add
                                      ).then_inc(s["normed"], 1)

                for p in range(FIRST_PREPS):
                    rope(p)
                largest(0)
                done = FIRST_PREPS
                for k in range(len(JOBS)):
                    if k + 1 < len(JOBS):
                        largest(k + 1)
                    if k and ends_kind(k - 1):
                        take_den(k - 1)
                    while done < PREPS_UPTO[k]:
                        rope(done)
                        done += 1
                    if k and ends_kind(k - 1):
                        norm(k - 1)
                take_den(len(JOBS) - 1)
                norm(len(JOBS) - 1)
                dve.wait_ge(s["out_sum"], 1)
                dve.tensor_tensor(flat(m.X), flat(m.X), m.ps[0][:], ALU.add).then_inc(s["residual"], 1)

            @block.gpsimd
            def _(pool):
                for p, (kind, a, b) in enumerate(PREPS):
                    pool.wait_ge(s["roped"], p + 1)
                    if p:
                        pool.wait_ge(s["small"], p)
                    if kind == "q":
                        to, src = m.QB[0:96, 4 * (a % 2) + b, :], q_tile(a, b)[0:96, :]
                    elif a == LATENT:
                        to, src = m.K1B[64:96, b % 2, :], m.K1[64:96, b % 2, :]
                    elif a == WINDOW:
                        to, src = m.KWB[0:96, b % 2, :], m.KW[0:96, b % 2, :]
                    else:
                        to, src = m.KSB[0:96, :], m.KS[0:96, :]
                    if kind == "q" or a != LATENT:
                        n = SWAPS_BEFORE[p]
                        tmp = m.R2[n % 2][0:96, 0:src.shape[-1]]
                        pool.wait_ge(s["plain"], n + 1)
                        pool.tensor_tensor(src, src, tmp, ALU.add).then_inc(s["added"], 1)
                        pool.wait_ge(s["added"], n + 1)
                    pool.tensor_copy(to, src).then_inc(s["small"], 1)
        clear(nc, used)


MAXED_ROWS = [sum(4 if x == SELECTED else 1 for _, x, _ in JOBS[:k]) for k in range(len(JOBS) + 1)]
SWAPS_BEFORE = [sum(not (q[0] != "q" and q[1] == LATENT) for q in PREPS[:p]) for p in range(len(PREPS))]


def gated_attention(nc, m):
    b = Named()
    b.qT, b.kT = m.Q[:, 0, :], m.Q[:, 1, :]
    b.k, b.v, b.vbeta, b.vmean = (m.Q[:, 2 + n, :].rearrange("p (t c) -> p t c", t=NT) for n in range(4))
    b.logits, b.abs = m.B1, m.B2
    b.beta, b.logalpha = (m.PT[:, n, :].rearrange("p (t c) -> p t c", t=NT) for n in range(2))
    b.rep = m.hid[:, 0:2, :].rearrange("p n c -> p (n c)").rearrange("p (n c) -> p n c", n=8)
    b.decay, b.attn = m.hid[:, 2:4, :], m.hid[:, 4:6, :]
    b.state = m.PT[:, 2, 0:256].rearrange("p (c v) -> p c v", c=NT)
    scale = 64 ** -0.5
    with ExitStack() as ctx:
        s, used = sems(nc, ctx, "gla", LN_SEMS + "bcol heads heads_laid proj clipped copied absed exps logs "
                       "chain alpha_mean cum cum_laid curves rep decay_sum decay scores attn vbeta vmean "
                       "delta state intra_sum mem_sum residual")
        with nc.Block() as block:

            @block.tensor
            def _(pe):
                ln_tensor(pe, m, s, 0)
                pe.wait_ge(s["ln_yt"], 1)
                for t in range(NT):
                    pe.matmul(m.ps[3 + t][:], m.YT[:, t * P:(t + 1) * P], m.w["g_wkvab"],
                              start=True, stop=False)
                    pe.matmul(m.ps[3 + t][:], m.ones[0:1, 0:P], m.w["g_brow"], start=False, stop=True
                              ).then_inc(s["proj"], 1)
                for k in range(2):
                    pe.matmul(m.ps[1 + k][:], m.w["g_wqk"][:, k * P:(k + 1) * P], m.YT[:],
                              start=True, stop=True).then_inc(s["heads"], 1)
                pe.wait_ge(s["heads_laid"], 2)
                for h in range(2):
                    for c in range(NT):
                        r = slice(c * P, (c + 1) * P)
                        mm = pe.matmul(m.ps[1 + h][:, r], b.kT[64 * h:64 * h + 64, r],
                                       b.qT[64 * h:64 * h + 64, r], start=True, stop=True)
                    mm.then_inc(s["scores"], 1)
                pe.wait_ge(s["alpha_mean"], 1)
                pe.matmul(m.ps[7][:, 0:8], m.t["upto"], m.own[:, 0:8], start=True, stop=True)
                pe.matmul(m.ps[7][:, 8:16], m.ones[:], m.own[:, 0:8], start=True, stop=True
                          ).then_inc(s["cum"], 1)
                pe.wait_ge(s["rep"], 1)
                pe.wait_ge(s["copied"], 2 * NT)
                for h in range(2):
                    for c in range(NT):
                        r = slice(c * P, (c + 1) * P)
                        pe.matmul(m.ps[3 + h][:, r], b.rep[:, 2 * c + h, :], m.t["upto"],
                                  start=(c == 0), stop=False, skip_group_check=True)
                        mm = pe.matmul(m.ps[3 + h][:, r], m.identb[:], m.mask_kq[:], start=False,
                                       stop=True, skip_group_check=True)
                    mm.then_inc(s["decay_sum"], 1)
                pe.wait_ge(s["vmean"], 1)
                for c in range(NT - 1):
                    mm = pe.matmul(m.ps[5][:, c * P:(c + 1) * P], b.k[:, c, :], b.vmean[:, c, :],
                                   start=True, stop=True)
                mm.then_inc(s["delta"], 1)
                pe.wait_ge(s["vbeta"], 1)
                pe.wait_ge(s["attn"], 2)
                for c in range(NT):
                    for h in range(2):
                        mm = pe.matmul(m.ps[6][:, c * P + 64 * h:c * P + 64 * h + 64],
                                       b.attn[:, h, c * P:(c + 1) * P],
                                       b.vbeta[:, c, 64 * h:64 * h + 64], start=True, stop=True)
                mm.then_inc(s["intra_sum"], 1)
                for c in range(1, NT):
                    pe.wait_ge(s["state"], 2 * c)
                    for h in range(2):
                        q = slice(64 * h, 64 * h + 64)
                        mm = pe.matmul(m.ps[7 * h][:, c * P + 64 * h:c * P + 64 * h + 64],
                                       b.qT[q, c * P:(c + 1) * P], b.state[q, c, :],
                                       start=True, stop=True)
                mm.then_inc(s["mem_sum"], 1)

            @block.scalar
            def _(act):
                ln_scalar(act, m, s)
                ln_copy(act, m, s, 0)
                for t in range(NT):
                    act.wait_ge(s["clipped"], 2 * t + 2)
                    act.activation(b.k[:, t, :], m.ps[3 + t][:, 0:P], ACT.Copy, scale=scale
                                   ).then_inc(s["copied"], 1)
                    act.copy(b.v[:, t, :], m.ps[3 + t][:, P:256]).then_inc(s["copied"], 1)
                act.wait_ge(s["bcol"], 1)
                for k, to in enumerate((b.qT, b.kT)):
                    act.wait_ge(s["heads"], k + 1)
                    act.activation(to, m.ps[1 + k][:], ACT.Identity, scale=scale,
                                   bias=m.small[:, k:k + 1]).then_inc(s["heads_laid"], 1)
                act.activation(b.abs, b.logits, ACT.Abs).then_inc(s["absed"], 1)
                act.wait_ge(s["absed"], 1)
                act.activation(b.abs, b.abs, ACT.Exp, scale=-1.0).then_inc(s["exps"], 1)
                act.wait_ge(s["exps"], 1)
                act.activation(b.abs, b.abs, ACT.Ln, bias=1.0).then_inc(s["logs"], 1)
                act.wait_ge(s["cum_laid"], 1)
                act.activation(m.small[:, 32:48], m.small[:, 16:32], ACT.Exp).then_inc(s["curves"], 1)
                for h in range(2):
                    act.wait_ge(s["decay_sum"], h + 1)
                    for c in range(NT):
                        n = 2 * c + h
                        act.activation(b.decay[:, h, c * P:(c + 1) * P],
                                       m.ps[3 + h][:, c * P:(c + 1) * P], ACT.Exp,
                                       bias=m.small[:, 48 + n:49 + n]).then_inc(s["decay"], 1)

            @block.vector
            def _(dve):
                count = [0]

                def link(ins):
                    count[0] += 1
                    ins.then_inc(s["chain"], 1)
                    dve.wait_ge(s["chain"], count[0])

                dve.tensor_scalar(m.small[:, 0:2], m.w["g_bcol"], scale, None, ALU.mult
                                  ).then_inc(s["bcol"], 1)
                ln_vector(dve, m, s)
                for t in range(NT):
                    dve.wait_ge(s["proj"], t + 1)
                    dve.tensor_copy(b.logits[:, t, 0:P], m.ps[3 + t][:, 256:384]).then_inc(s["clipped"], 1)
                    dve.tensor_scalar(b.logits[:, t, P:256], m.ps[3 + t][:, 384:512], -10.0, 10.0,
                                      ALU.max, ALU.min).then_inc(s["clipped"], 1)
                dve.wait_ge(s["logs"], 1)
                link(dve.scalar_tensor_tensor(b.logalpha, b.logits[:, :, P:256], 0.0, b.abs[:, :, P:256],
                                              ALU.min, ALU.subtract))
                per_head = lambda x: x.rearrange("p t (h d) -> p t h d", h=2)
                sums = lambda x: x.rearrange("p (t h) -> p t h", h=2)
                link(dve.tensor_reduce(sums(m.own[:, 8:16]), per_head(b.logalpha), AX.X, ALU.add))
                dve.tensor_scalar(m.own[:, 0:8], m.own[:, 8:16], 1.0 / 64, None, ALU.mult
                                  ).then_inc(s["alpha_mean"], 1)
                dve.wait_ge(s["alpha_mean"], 1)
                dve.tensor_copy(b.rep, m.own[:, 0:8].unsqueeze(2).to_broadcast([P, 8, P])
                                ).then_inc(s["rep"], 1)
                link(dve.scalar_tensor_tensor(b.beta, b.logits[:, :, 0:P], 0.0, b.abs[:, :, 0:P],
                                              ALU.max, ALU.add))
                dve.wait_ge(s["cum"], 1)
                link(dve.tensor_copy(m.small[:, 16:32], m.ps[7][:, 0:16]))
                dve.tensor_scalar(m.small[:, 48:56], m.small[:, 16:24], -1.0, None, ALU.mult
                                  ).then_inc(s["cum_laid"], 1)
                link(dve.tensor_reduce(sums(m.own[:, 8:16]), per_head(b.beta), AX.X, ALU.add))
                link(dve.tensor_scalar(m.small[:, 8:16], m.own[:, 8:16], 1.0 / 64, None, ALU.mult))
                dve.wait_ge(s["copied"], 2 * NT)
                dve.tensor_tensor(per_head(b.vmean), per_head(b.v),
                                  sums(m.small[:, 8:16]).unsqueeze(3).to_broadcast([P, NT, 2, 64]),
                                  ALU.mult).then_inc(s["vmean"], 1)
                dve.tensor_tensor(b.vbeta, b.v, b.beta, ALU.mult).then_inc(s["vbeta"], 1)
                for h in range(2):
                    dve.wait_ge(s["decay"], NT * (h + 1))
                    dve.wait_ge(s["scores"], h + 1)
                    dve.tensor_tensor(b.attn[:, h, :], m.ps[1 + h][:], b.decay[:, h, :], ALU.mult
                                      ).then_inc(s["attn"], 1)
                dve.wait_ge(s["delta"], 1)
                dve.wait_ge(s["curves"], 1)
                for c in range(NT - 1):
                    for h in range(2):
                        q = slice(64 * h, 64 * h + 64)
                        new = m.ps[5][q, c * P + 64 * h:c * P + 64 * h + 64]
                        n = 2 * c + h
                        if c == 0:
                            dve.tensor_copy(b.state[q, 1, :], new).then_inc(s["state"], 1)
                        else:
                            dve.wait_ge(s["state"], n - 1)
                            dve.scalar_tensor_tensor(b.state[q, c + 1, :], b.state[q, c, :],
                                                     m.small[q, 40 + n:41 + n], new, ALU.mult, ALU.add
                                                     ).then_inc(s["state"], 1)
                dve.wait_ge(s["intra_sum"], 1)
                link(dve.tensor_tensor(flat(m.X), flat(m.X), m.ps[6][:], ALU.add))
                dve.wait_ge(s["mem_sum"], 1)
                for c in range(1, NT):
                    for h in range(2):
                        n, q = 2 * c + h, slice(64 * h, 64 * h + 64)
                        dve.scalar_tensor_tensor(m.X[:, c, q],
                                                 m.ps[7 * h][:, c * P + 64 * h:c * P + 64 * h + 64],
                                                 m.small[:, 32 + n:33 + n], m.X[:, c, q], ALU.mult,
                                                 ALU.add).then_inc(s["residual"], 1)
        clear(nc, used)


ROUND = 12582912.0


def quantize(dve, link, src, dst, tmp, scales, columns):
    n = columns // 32
    blocks = lambda x: x.rearrange("p (n k) -> p n k", k=32)
    over = lambda x: x.unsqueeze(2).to_broadcast([P, n, 32])
    value, step, a, c = (t[:, 0:columns] for t in tmp)
    scale, inverse = scales[:, 0:n], scales[:, 16:16 + n]
    link(dve.tensor_reduce(scale, blocks(src), AX.X, ALU.max, apply_absolute_value=True))
    link(dve.tensor_scalar(scale, scale, 1.0 / 7.5, 1e-30, ALU.mult, ALU.max))
    link(dve.reciprocal(inverse, scale))
    link(dve.tensor_tensor(blocks(value), blocks(src), over(inverse), ALU.mult))
    link(dve.scalar_tensor_tensor(c, value, -1.0, value, ALU.mult, ALU.max))
    link(dve.tensor_scalar(step, c, 2.0, None, ALU.is_ge))
    link(dve.tensor_scalar(a, c, 4.0, None, ALU.is_ge))
    link(dve.scalar_tensor_tensor(step, a, 2.0, step, ALU.mult, ALU.add))
    link(dve.tensor_scalar(step, step, 0.125, 0.125, ALU.mult, ALU.add))
    link(dve.scalar_tensor_tensor(a, step, ROUND, value, ALU.mult, ALU.add))
    link(dve.scalar_tensor_tensor(a, step, -ROUND, a, ALU.mult, ALU.add))
    link(dve.tensor_tensor(c, a, value, ALU.subtract))
    link(dve.scalar_tensor_tensor(c, step, 0.5, c, ALU.mult, ALU.is_le))
    link(dve.tensor_tensor(c, c, step, ALU.mult))
    link(dve.tensor_tensor(a, a, c, ALU.subtract))
    return dve.tensor_tensor(blocks(dst), blocks(a), over(scale), ALU.mult)


def quantize_weight(nc, m):
    with ExitStack() as ctx:
        s, used = sems(nc, ctx, "qw", "chain ready turned laid")
        with nc.Block() as block:

            @block.vector
            def _(dve):
                count = [0]

                def link(ins):
                    count[0] += 1
                    ins.then_inc(s["chain"], 1)
                    dve.wait_ge(s["chain"], count[0])

                quantize(dve, link, m.w["q_w"], m.R[:, 0:P], [m.hid[:, n, :] for n in range(4)],
                         m.small, P).then_inc(s["ready"], 1)

            @block.tensor
            def _(pe):
                pe.wait_ge(s["ready"], 1)
                pe.transpose(m.ps[0][:, 0:P], m.R[:, 0:P], m.ident).then_inc(s["turned"], 1)

            @block.scalar
            def _(act):
                act.wait_ge(s["turned"], 1)
                act.copy(m.WQT[:], m.ps[0][:, 0:P]).then_inc(s["laid"], 1)
        clear(nc, used)


def quantized_linear(nc, m):
    with ExitStack() as ctx:
        s, used = sems(nc, ctx, "fp6", LN_SEMS + "chain ready turned laid out_sum residual")
        with nc.Block() as block:

            @block.vector
            def _(dve):
                count = [0]

                def link(ins):
                    count[0] += 1
                    ins.then_inc(s["chain"], 1)
                    dve.wait_ge(s["chain"], count[0])

                ln_vector(dve, m, s)
                dve.wait_ge(s["ln_y"], NT)
                quantize(dve, link, flat(m.Y), flat(m.H), [m.hid[:, n, :] for n in range(4)], m.small,
                         SEQ).then_inc(s["ready"], 1)
                dve.wait_ge(s["out_sum"], 1)
                dve.tensor_tensor(flat(m.X), flat(m.X), m.ps[1][:], ALU.add).then_inc(s["residual"], 1)

            @block.tensor
            def _(pe):
                pe.wait_ge(s["ready"], 1)
                for t in range(NT):
                    mm = pe.transpose(m.ps[0][:, t * P:(t + 1) * P], m.H[:, t, :], m.ident)
                mm.then_inc(s["turned"], 1)
                pe.wait_ge(s["laid"], 1)
                for t in range(NT):
                    r = slice(t * P, (t + 1) * P)
                    pe.matmul(m.ps[1][:, r], m.YT[:, r], m.WQT[:], start=(t == 0), stop=False,
                              skip_group_check=True)
                    mm = pe.matmul(m.ps[1][:, r], m.ones[0:1, 0:P], m.w["q_brow"], start=False, stop=True,
                                   skip_group_check=True)
                mm.then_inc(s["out_sum"], 1)

            @block.scalar
            def _(act):
                ln_scalar(act, m, s)
                act.wait_ge(s["turned"], 1)
                act.copy(m.YT[:], m.ps[0][:]).then_inc(s["laid"], 1)
        clear(nc, used)


SOFTCAP = 50.0
CAP_BANKS = [2, 3, 6, 7]


def capped_attention(nc, m, sw):
    b = Named()
    b.w = m.hid[:, 0:8, :]
    b.q = [m.B1[:, t:t + 2, :].rearrange("p t c -> p (t c)") for t in (0, 2)]
    b.k = m.hid[:, 8:12, :]
    b.v = [m.PT[:, n, :].rearrange("p (t c) -> p t c", t=NT) for n in range(2)]
    b.gate = [m.PT[:, 2 + n, :] for n in range(2)]
    scale = 64 ** -0.5
    with ExitStack() as ctx:
        s, used = sems(nc, ctx, "cap", LN_SEMS + "weights qk qk_laid zeros vg v_laid gate_laid scores tanhs probs "
                       "masked numden num_out den_out den rden normed out_sum residual")
        with nc.Block() as block:

            @block.sync
            def _(sp):
                sp.dma_start(m.big[:, 0:8 * 512], sw).then_inc(s["weights"], 16)

            @block.tensor
            def _(pe):
                ln_tensor(pe, m, s, 2)
                pe.wait_ge(s["ln_yt"], 1)
                pe.wait_ge(s["weights"], 16)

                def project_qk(g):
                    if g:
                        pe.wait_ge(s["v_laid"], g)
                        pe.wait_ge(s["gate_laid"], g)
                    for k in range(2):
                        mm = pe.matmul(m.ps[k][:], b.w[:, g, k * P:(k + 1) * P], m.YT[:], start=True,
                                       stop=True)
                    mm.then_inc(s["qk"], 1)

                def project_vg(g):
                    pe.wait_ge(s["qk_laid"], 3 * g + 3)
                    for t in range(NT):
                        pe.matmul(m.ps[0][:, t * P:(t + 1) * P], m.YT[:, t * P:(t + 1) * P],
                                  b.w[:, g, 256:384], start=True, stop=True)
                    pe.matmul(m.ps[1][:], b.w[:, g, 384:512], m.YT[:], start=True, stop=True
                              ).then_inc(s["vg"], 1)

                def scores(n):
                    g = n // 2
                    for u in range(3):
                        if 3 * n + u >= 4:
                            pe.wait_ge(s["tanhs"], 3 * n + u - 3)
                        bank = m.ps[CAP_BANKS[(3 * n + u) % 4]]
                        for kt, at in UNITS[u]:
                            mm = pe.matmul(bank[:, at:at + WIDTH[kt]], b.k[:, n % 4, kt * P:(kt + 1) * P],
                                           b.q[g % 2][:, kt * P:SEQ], start=True, stop=True)
                        mm.then_inc(s["scores"], 1)

                def values(n):
                    g, j = divmod(n, 2)
                    pe.wait_ge(s["masked"], 2 * n + 2)
                    if j == 0 and g:
                        pe.wait_ge(s["num_out"], g)
                        pe.wait_ge(s["den_out"], g)
                    cols, others = slice(64 * j, 64 * j + 64), slice(64 - 64 * j, P - 64 * j)
                    mm = weigh_values(pe, m, m.probs[:, n % 3, :], lambda kt: b.v[g % 2][:, kt, cols],
                                      cols, others, m.ps[4], m.ps[5], m.ones[:, 0:64])
                    if j:
                        mm.then_inc(s["numden"], 1)

                project_qk(0)
                pe.wait_ge(s["zeros"], 2)
                project_vg(0)
                for n in range(18):
                    if n < 16:
                        scores(n)
                    if n >= 2:
                        values(n - 2)
                    if n % 2 == 0 and n // 2 + 1 < 8:
                        project_qk(n // 2 + 1)
                    if n % 2 == 1 and n // 2 + 1 < 8:
                        project_vg(n // 2 + 1)
                for g in range(8):
                    pe.wait_ge(s["normed"], g + 1)
                    for t in range(NT):
                        mm = pe.matmul(m.ps[2][:, t * P:(t + 1) * P], m.Q[:, g, t * P:(t + 1) * P],
                                       m.w["s_wout"][:, g * P:(g + 1) * P], start=(g == 0 and t == 0),
                                       stop=(g == 7), skip_group_check=True)
                mm.then_inc(s["out_sum"], 1)

            @block.scalar
            def _(act):
                ln_scalar(act, m, s)
                ln_copy(act, m, s, 2)

                def gate(g):
                    act.wait_ge(s["vg"], g + 1)
                    if g >= 2:
                        act.wait_ge(s["den"], g - 1)
                    act.activation(b.gate[g % 2], m.ps[1][:], ACT.Exp, scale=-1.0
                                   ).then_inc(s["gate_laid"], 1)

                def exps(n):
                    act.wait_ge(s["tanhs"], 3 * n + 3)
                    act.activation(m.probs[:, n % 3, :], m.probs[:, n % 3, :], ACT.Exp, scale=SOFTCAP
                                   ).then_inc(s["probs"], 1)

                def take_num(g):
                    act.wait_ge(s["numden"], g + 1)
                    act.copy(m.Q[:, g, :], m.ps[4][:]).then_inc(s["num_out"], 1)

                for n in range(16):
                    if n % 2 == 0:
                        gate(n // 2)
                    for u in range(3):
                        act.wait_ge(s["scores"], 3 * n + u + 1)
                        act.activation(m.probs[:, n % 3, UNIT_AT[u]:UNIT_AT[u] + unit_cols(u)],
                                       m.ps[CAP_BANKS[(3 * n + u) % 4]][:, 0:unit_cols(u)], ACT.Tanh,
                                       scale=scale / SOFTCAP).then_inc(s["tanhs"], 1)
                    if n:
                        exps(n - 1)
                    if n >= 3 and n % 2:
                        take_num(n // 2 - 1)
                exps(15)
                take_num(7)

            @block.vector
            def _(dve):
                ln_vector(dve, m, s)

                def lay_qk(g):
                    dve.wait_ge(s["qk"], g + 1)
                    dve.tensor_copy(b.q[g % 2], m.ps[0][:]).then_inc(s["qk_laid"], 1)
                    for j in range(2):
                        r = slice(64 * j, 64 * j + 64)
                        dve.tensor_copy(b.k[r, 2 * (g % 2) + j, :], m.ps[1][r, :]).then_inc(s["qk_laid"], 1)

                def lay_v(g):
                    dve.wait_ge(s["vg"], g + 1)
                    dve.tensor_copy(b.v[g % 2].rearrange("p t c -> p (t c)"), m.ps[0][:]
                                    ).then_inc(s["v_laid"], 1)

                def mask(n):
                    dve.wait_ge(s["probs"], n + 1)
                    p = m.probs[:, n % 3, :]
                    three = m.probs_wide[:, n % 3, 0:3, 0:P]
                    upto = m.t["upto"]
                    dve.tensor_tensor(three, three, upto.unsqueeze(1).to_broadcast([P, 3, P]), ALU.mult
                                      ).then_inc(s["masked"], 1)
                    last = p[:, KEYS_AT[3]:KEYS_AT[3] + P]
                    dve.tensor_tensor(last, last, upto, ALU.mult).then_inc(s["masked"], 1)

                def norm(g):
                    dve.wait_ge(s["numden"], g + 1)
                    take_swapped(dve, m.R, m.ps[5], s["den_out"])
                    dve.wait_ge(s["gate_laid"], g + 1)
                    dve.wait_ge(s["den_out"], g + 1)
                    dve.scalar_tensor_tensor(m.A[:], b.gate[g % 2], 1.0, m.R[:], ALU.add, ALU.mult
                                             ).then_inc(s["den"], 1)
                    dve.wait_ge(s["den"], g + 1)
                    dve.reciprocal(m.A[:], m.A[:]).then_inc(s["rden"], 1)
                    dve.wait_ge(s["rden"], g + 1)
                    dve.wait_ge(s["num_out"], g + 1)
                    dve.tensor_tensor(m.Q[:, g, :], m.Q[:, g, :], m.A[:], ALU.mult).then_inc(s["normed"], 1)

                lay_qk(0)
                lay_v(0)
                for n in range(18):
                    if 1 <= n <= 16:
                        mask(n - 1)
                    if n % 2 == 0 and n // 2 + 1 < 8:
                        lay_qk(n // 2 + 1)
                    if n % 2 == 1 and n // 2 + 1 < 8:
                        lay_v(n // 2 + 1)
                    if n >= 3 and n % 2:
                        norm(n // 2 - 1)
                dve.wait_ge(s["out_sum"], 1)
                dve.tensor_tensor(flat(m.X), flat(m.X), m.ps[2][:], ALU.add).then_inc(s["residual"], 1)

            @block.gpsimd
            def _(pool):
                for j in range(2):
                    pool.memset(m.hid[64 - 64 * j:P - 64 * j, 8 + j:12:2, :], 0.0
                                ).then_inc(s["zeros"], 1)
                    pool.wait_ge(s["zeros"], j + 1)
        clear(nc, used)


def ffn(nc, m, mw, sw):
    ffn_attention(nc, m)
    experts(nc, m)


def mla(nc, m, mw, sw):
    mla_prepare(nc, m)
    mla_heads(nc, m, mw)


LAYERS = {0: lambda nc, m, mw, sw: linear_attention(nc, m), 1: ffn, 2: mla, 3: ffn,
          4: lambda nc, m, mw, sw: gated_attention(nc, m),
          5: lambda nc, m, mw, sw: quantized_linear(nc, m),
          6: lambda nc, m, mw, sw: capped_attention(nc, m, sw),
          7: lambda nc, m, mw, sw: quantized_linear(nc, m)}


def more_memory(sb, m, b12):
    m.H = sb("H", [P, NT, P])
    m.sq = sb("sq", [P, NT])
    m.hsum, m.hmean, m.hstd = sb("hsum", [P, NT, 32]), sb("hmean", [P, 128]), sb("hstd", [P, 128])
    m.QB = sb("QB", [P, 8, SEQ], BF16)
    m.KB = m.QB[:, NG:2 * NG, :]
    wide = sb("probs", [P, 3, 3, SEQ])
    m.probs_wide = wide
    m.probs = wide[:].rearrange("p h u c -> p h (u c)")[:, :, 0:HEAD_COLS]
    m.S = m.probs[:, 0, 0:768].rearrange("p (g c n) -> p g c n", g=2, c=3)
    m.Aall = sb("Aall", [P, NG, SEQ])
    m.g16, m.g16b, m.top = (sb(n, [P, 16]) for n in ("g16", "g16b", "top"))
    m.g64, m.g64b = (sb(n, [P, 64]) for n in ("g64", "g64b"))
    m.g4, m.g4b = (sb(n, [P, 4]) for n in ("g4", "g4b"))
    big = sb("big", [P, 15 * SEQ])
    m.big = big
    m.WQT = sb("WQT", [P, P])
    m.hid = big[:].rearrange("p (n c) -> p n c", c=SEQ)
    m.mw = big[:, 0:2 * M_COLS].rearrange("p (n c) -> p n c", c=M_COLS)
    m.K1, m.KW = (sb(n, [P, 2, SEQ]) for n in ("K1", "KW"))
    m.K1B, m.KWB = (sb(n, [P, 2, SEQ], BF16) for n in ("K1B", "KWB"))
    m.KS, m.KSB = sb("KS", [P, P]), sb("KSB", [P, P], BF16)
    m.V1 = b12[:].rearrange("p (t h d) -> p t h d", t=NT, h=16)
    m.VW = m.PT[:].rearrange("p j n -> p (j n)").rearrange("p (t h d) -> p t h d", t=NT, h=16)
    spare = 2 * M_COLS
    m.VS = big[:, spare:spare + 512].rearrange("p (g n) -> p g n", g=NG)
    m.NCT, m.imp, r2 = (big[:, spare + 512 * n:spare + 512 * n + 512] for n in (1, 2, 3))
    m.R2 = [r2, m.imp]
    m.NMm = sb("NMm", [P, 4, NT, P])
    m.NM = m.NMm[:, 0:2, :, :]
    m.small, m.own, m.gates = sb("small", [P, 64]), sb("own", [P, 20]), sb("gates", [P, 3])
    m.SELT = wide[:, 2, 2, HEAD_COLS - 1024:HEAD_COLS - 1024 + P]
    m.H2, m.onehot = m.A[:, 0:P], m.H


def program(nc, x, weights, tables, m_weights, s_weights, out, layers=range(8)):
    with ExitStack() as ctx:
        def sb(name, shape, dt=F32):
            return ctx.enter_context(nc.sbuf_tensor(name, shape, dt))

        m = Named()
        m.ps = [ctx.enter_context(nc.psum_tensor(f"bank{i}", [P, 512], F32)) for i in range(8)]
        m.w_all = sb("weights_sb", [P, W_COLS])
        m.t_all = sb("tables_sb", [P, T_COLS])
        m.w = {n: m.w_all[0:r, a:a + c] for n, (a, r, c) in W_AT.items()}
        m.t = {n: m.t_all[0:r, a:a + c] for n, (a, r, c) in T_AT.items()}
        m.ident = m.t["ident"]
        m.identb, m.mask_qk, m.mask_kq = (sb(n, [P, P], BF16) for n in ("identb", "maskqkb", "maskkqb"))
        m.ones = sb("ones", [P, P])
        m.X, m.Y = sb("X", [P, NT, P]), sb("Y", [P, NT, P])
        m.YT = sb("YT", [P, SEQ])
        m.stats, m.mv = sb("stats", [P, NT, 6]), sb("mv", [P, NT, 2])
        m.var, m.std, m.rstd = (sb(n, [P, NT]) for n in ("var", "std", "rstd"))
        m.Qp, m.Kp, m.Vp = (sb(n, [P, NT, 16, 32]) for n in ("Qp", "Kp", "Vp"))
        m.Q = sb("Q", [P, 2 * NG, SEQ])
        m.QTall, m.KTall = m.Q[:, 0:NG, :], m.Q[:, NG:2 * NG, :]
        b12 = sb("B12", [P, 2 * NT * 256])
        m.B1, m.B2 = (b12[:, 1024 * n:1024 * n + 1024].rearrange("p (t c) -> p t c", t=NT) for n in range(2))
        m.PT = sb("PT", [P, 4, SEQ])
        m.R, m.A = sb("R", [P, SEQ]), sb("A", [P, SEQ])
        more_memory(sb, m, b12)
        x_dram = x.rearrange("b (t p) d -> b p t d", p=P)
        out_dram = out.rearrange("b (t p) d -> b p t d", p=P)

        with ExitStack() as start:
            s, used = sems(nc, start, "load", "loaded set")
            with nc.Block() as block:

                @block.sync
                def _(sp):
                    sp.dma_start(m.w_all[:], weights).then_inc(s["loaded"], 16)
                    sp.dma_start(m.t_all[:], tables).then_inc(s["loaded"], 16)

                @block.vector
                def _(dve):
                    dve.memset(m.Qp[:], 0.0)
                    dve.memset(m.Kp[:], 0.0)
                    dve.memset(m.Vp[:, :, :, 0:8], 0.0)
                    dve.memset(m.Vp[:, :, :, 8:9], 1.0)
                    dve.memset(m.Vp[:, :, :, 9:32], 0.0)
                    dve.memset(m.NMm[:], 0.0)
                    dve.memset(m.K1[96:97, :, :], 1.0)
                    dve.memset(m.KW[96:97, :, :], 1.0)
                    dve.memset(m.KS[96:97, :], 1.0)
                    dve.memset(m.ones[:], 1.0).then_inc(s["set"], 1)
                    dve.wait_ge(s["loaded"], 32)
                    dve.tensor_copy(m.identb[:], m.t["ident"])
                    dve.tensor_copy(m.mask_qk[:], m.t["mask_qk"])
                    dve.tensor_copy(m.mask_kq[:], m.t["mask_kq"]).then_inc(s["set"], 1)
            clear(nc, used)
        if 5 in layers or 7 in layers:
            quantize_weight(nc, m)

        with nc.Fori(0, BATCH) as b:
            with ExitStack() as move:
                s, used = sems(nc, move, "in", "x_in")
                with nc.Block() as block:

                    @block.sync
                    def _(sp):
                        sp.dma_start(m.X[:], x_dram[bass.ds(b, 1)].rearrange("o p t d -> p (o t) d")
                                     ).then_inc(s["x_in"], 16)
                        sp.wait_ge(s["x_in"], 16)
                clear(nc, used)
            for layer in layers:
                LAYERS[layer](nc, m, m_weights, s_weights)
            with ExitStack() as move:
                s, used = sems(nc, move, "out", "x_out")
                with nc.Block() as block:

                    @block.sync
                    def _(sp):
                        sp.dma_start(out_dram[bass.ds(b, 1)].rearrange("o p t d -> p (o t) d"), m.X[:]
                                     ).then_inc(s["x_out"], 16)
                        sp.wait_ge(s["x_out"], 16)
                clear(nc, used)


def pack(table, parts):
    at, cols = offsets(table)
    packed = np.zeros((P, cols), np.float32)
    for name, part in parts.items():
        off, r, c = at[name]
        packed[0:r, off:off + c] = part.reshape(r, c)
    return packed


def head_rows(w):
    out = np.zeros((NG, P, w.shape[1]), np.float32)
    for g in range(NG):
        for j in range(4):
            out[g, 32 * j:32 * j + 8] = w[8 * (4 * g + j):8 * (4 * g + j) + 8]
    return out.transpose(1, 0, 2).reshape(P, -1)


def halves(w):
    return np.concatenate([w[:P], w[P:]], axis=1)


def rope_order(w, heads):
    w = w.reshape(w.shape[0], heads, 96)
    plain, x1, x2 = w[:, :, 0:32], w[:, :, 32:64], w[:, :, 64:96]
    return (np.concatenate([x1, x2, plain], axis=2), np.concatenate([x2, x1, plain], axis=2))


def swapped(w):
    return np.concatenate([w[:, 32:64], w[:, 0:32]], axis=1)


def column8(v):
    out = np.zeros((P, 1), np.float32)
    for j in range(4):
        out[32 * j:32 * j + 8, 0] = v
    return out


def tables():
    i = np.arange(P)
    k, q = i[:, None], i[None, :]
    angle = np.outer(np.arange(SEQ, dtype=np.float32),
                     (1.0 / np.float32(10000.0) ** (np.arange(0, 64, 2, dtype=np.float32) / np.float32(64)))
                     .astype(np.float32)).astype(np.float32)
    cos, sin = np.cos(angle).T, np.sin(angle).T
    one, zero = np.ones((32, SEQ), np.float32), np.zeros((32, SEQ), np.float32)
    e = np.arange(4)
    return pack(TABLES, {
        "ident": np.eye(P), "mask_qk": np.where(q > k, NEG, 0.0), "mask_kq": np.where(q < k, NEG, 0.0),
        "upto": k <= q, "before": k < q, "block": (k // 32) == (q // 32),
        "spread8": k == 32 * (q // 32) + 8,
        "rope_c": np.concatenate([cos, cos, one]), "rope_s": np.concatenate([-sin, sin, zero]),
        "below": q < k,
        "iota": np.tile(np.arange(32), (P, 1)),
        "lower4": np.tile((e[None, :] < e[:, None]).reshape(1, 16), (P, 1)),
        "aug8": i % 32 == 8, "aug3": i[:, None] - 96 == np.arange(3)[None, :],
    })


def kernel(**inputs):
    import concourse.bacc as bacc
    from concourse.bass_utils import run_bass_kernel_spmd

    nc = bacc.Bacc("TRN2", target_bir_lowering=False, num_devices=1)
    arrays, args = {}, []
    for name, a in host_arrays(**inputs).items():
        arrays[name] = np.ascontiguousarray(a)
        args.append(nc.dram_tensor(name, a.shape, F32, kind="ExternalInput").ap())
    args.append(nc.dram_tensor("out", (BATCH, SEQ, D), F32, kind="ExternalOutput").ap())
    program(nc, *args)
    return run_bass_kernel_spmd(nc, [arrays], core_ids=[0]).results[0]["out"]


def host_arrays(**inputs):
    v = {n: np.asarray(a) for n, a in inputs.items()}
    a = {n[len("L0_attn_a_"):]: x for n, x in v.items() if n.startswith("L0_attn_a_")}
    f = {n[len("L0_ffn_"):]: x for n, x in v.items() if n.startswith("L0_ffn_")}
    b = {n[len("L0_attn_b_"):]: x for n, x in v.items() if n.startswith("L0_attn_b_")}
    g = {n[len("L1_attn_a_"):]: x for n, x in v.items() if n.startswith("L1_attn_a_")}
    h = {n[len("L1_attn_b_"):]: x for n, x in v.items() if n.startswith("L1_attn_b_")}
    side = lambda *ws: np.concatenate(ws, axis=1)
    weights = pack(WEIGHTS, {
        "a_wqkv": side(a["Wq"].T, a["Wk"].T, a["Wv"].T), "a_wo": head_rows(a["Wo"].T),
        "a_brow": np.concatenate([a["bq"], a["bk"], a["bv"], a["bo"]]),
        "f_wqkv": side(f["wq"].T, f["wk"].T, f["wv"].T), "f_wo": head_rows(f["wo"].T),
        "f_n1": f["n1_w"], "f_n2": f["n2_w"], "f_qn": column8(f["qn_w"]), "f_kn": column8(f["kn_w"]),
        "f_gate": f["gate_w"].T, "f_e0_up": f["e0_up"].T, "f_e0_dn": halves(f["e0_down"].T),
        "f_e1_w1": f["e1_w1"].T, "f_e1_w2": f["e1_w2"].T, "f_e1_dn": halves(f["e1_down"].T),
        "f_e2_l1": f["e2_l1"].T, "f_e2_l2": halves(f["e2_l2"].T), "f_e2_l3": halves(f["e2_l3"].T),
        "f_e2_l4": halves(f["e2_l4"].T), "f_e3_dn": f["e3_down"].T, "f_e3_up": f["e3_up"].T,
        "f_e3_out": halves(f["e3_out"].T),
        "m_cq": b["w_cq"], "m_ckv": b["w_ckv"], "m_krope": side(b["w_krope"], swapped(b["w_krope"])),
        "m_imp": np.tile(b["w_imp"], (1, P)), "m_gate": b["w_gate"], "m_gqkv": np.concatenate([b["g_qnorm"], b["g_kvnorm"]]),
        "m_dv": np.concatenate([np.zeros((96, 512), np.float32), b["w_dv"]]), "m_selv": b["w_selv"], "m_winv": b["w_winv"],
        "m_proj": b["w_proj"].reshape(NG, P, D).transpose(1, 0, 2),
        "g_wqk": side(g["Wq"].T, g["Wk"].T),
        "g_wkvab": side(g["Wk"].T, g["Wv"].T, g["Wbeta"].T, g["Walpha"].T),
        "g_bcol": np.stack([g["bq"], g["bk"]], axis=1),
        "g_brow": np.concatenate([g["bk"], g["bv"], g["bbeta"], g["balpha"]]),
        "s_wout": h["w_out"].reshape(8, P, D).transpose(1, 0, 2),
        "q_w": v["L1_ffn_weight"], "q_brow": v["L1_ffn_bias"],
    })
    m_weights = np.zeros((NG, P, M_COLS), np.float32)
    nope = np.concatenate([b["w_dq_rope"].reshape(96, 16, 64), b["w_dq_nope"].reshape(96, 16, 32)], axis=2)
    nope_sw = np.concatenate([nope[:, :, 32:64], nope[:, :, 0:32], nope[:, :, 64:96]], axis=2)
    win, win_sw = rope_order(b["w_wink"], 16)
    sel, sel_sw = rope_order(b["w_selk"], 16)
    latent = np.zeros((P, 16, 96), np.float32)
    latent[96:P, :, 64:96] = b["w_dk_nope"].reshape(32, 16, 32)
    for grp in range(NG):
        hs = slice(4 * grp, 4 * grp + 4)
        for n, w in enumerate((nope, nope_sw, win, win_sw, sel, sel_sw, latent)):
            m_weights[grp, 0:w.shape[0], 384 * n:384 * n + 384] = w[:, hs].reshape(w.shape[0], 384)
    qkv = np.concatenate([h["w_qkv"].reshape(P, 3, 8, P),
                          np.repeat(h["w_gates"], 64, axis=1).reshape(P, 1, 8, P)], axis=1)
    s_weights = qkv.transpose(0, 2, 1, 3).reshape(P, 8 * 512)
    return {"x": v["L0_attn_a_x"], "weights": weights, "tables": tables(), "m_weights": m_weights,
            "s_weights": s_weights}
```

```python
from contextlib import ExitStack

import numpy as np

import concourse.bass as bass
from concourse import mybir

F32 = mybir.dt.float32
BF16 = mybir.dt.bfloat16
ALU = mybir.AluOpType
ACT = mybir.ActivationFunctionType
AX = mybir.AxisListType

P = 128
BATCH, SEQ, D = 4, 512, 128
NT = SEQ // P
NG = 4
NEG = -1.0e30
LN_EPS = 1e-5

WEIGHTS = [
    ("a_wqkv", 128, 384), ("a_wo", 128, NG * 128), ("a_brow", 1, 512),
    ("q_w", 128, 128), ("q_brow", 1, 128),
    ("f_wqkv", 128, 384), ("f_wo", 128, NG * 128), ("f_n1", 128, 1), ("f_n2", 128, 1),
    ("f_qn", 128, 1), ("f_kn", 128, 1), ("f_gate", 128, 4),
    ("f_e0_up", 128, 256), ("f_e0_dn", 128, 256), ("f_e1_w1", 128, 256), ("f_e1_w2", 128, 256),
    ("f_e1_dn", 128, 256), ("f_e2_l1", 128, 256), ("f_e2_l2", 128, 512), ("f_e2_l3", 128, 512),
    ("f_e2_l4", 128, 256), ("f_e3_dn", 128, 128), ("f_e3_up", 128, 256), ("f_e3_out", 128, 256),
    ("m_cq", 128, 96), ("m_ckv", 128, 32), ("m_krope", 128, 64), ("m_imp", 128, 128),
    ("m_gate", 128, 3), ("m_gqkv", 128, 1), ("m_dv", 128, 512), ("m_selv", 128, 512),
    ("m_winv", 128, 512), ("m_proj", 128, NG * 128),
    ("g_wqk", 128, 256), ("g_wkvab", 128, 512), ("g_bcol", 128, 2), ("g_brow", 1, 512),
    ("s_wout", 128, 8 * 128),
]
TABLES = [
    ("ident", 128, 128), ("mask_qk", 128, 128), ("mask_kq", 128, 128), ("upto", 128, 128),
    ("before", 128, 128), ("block", 128, 128), ("spread8", 128, 128), ("rope_c", 96, 512), ("rope_s", 64, 512),
    ("below", 128, 128), ("iota", 128, 32), ("lower4", 128, 16), ("aug8", 128, 1), ("aug3", 128, 3),
]


class Named:
    pass


def offsets(table):
    at, out = 0, {}
    for name, rows, cols in table:
        out[name] = (at, rows, cols)
        at += cols
    return out, at


W_AT, W_COLS = offsets(WEIGHTS)
T_AT, T_COLS = offsets(TABLES)
FIRST_COLS = W_AT["f_wqkv"][0]
M_COLS = 3 * 384 + 128


def sems(nc, ctx, prefix, names):
    made = {n: ctx.enter_context(nc.semaphore(f"{prefix}_{n}")) for n in names.split()}
    return made, list(made.values())


def retire(m, ctx, used):
    m.stale.close()
    m.stale, m.to_clear = ctx.pop_all(), used


def clear_stale(sp, m):
    for x in m.to_clear:
        sp.sem_clear(x)


def clear(nc, used):
    for s in used:
        nc.sync.sem_clear(s)
    nc.all_engine_barrier()


LN_SEMS = "ln_stats ln_aggr ln_var ln_std ln_rstd ln_y ln_turned ln_yt "


def ln_vector(dve, m, s):
    for t in range(NT):
        dve.bn_stats(m.stats[:, t, :], m.X[:, t, :]).then_inc(s["ln_stats"], 1)
    for t in range(NT):
        dve.wait_ge(s["ln_stats"], t + 1)
        dve.bn_aggr(m.mv[:, t, :], m.stats[:, t, :]).then_inc(s["ln_aggr"], 1)
    dve.wait_ge(s["ln_aggr"], NT)
    dve.tensor_scalar(m.var[:], m.mv[:, :, 1], LN_EPS, None, ALU.add).then_inc(s["ln_var"], 1)
    dve.wait_ge(s["ln_std"], 1)
    dve.reciprocal(m.rstd[:], m.std[:]).then_inc(s["ln_rstd"], 1)
    dve.wait_ge(s["ln_rstd"], 1)
    for t in range(NT):
        dve.tensor_scalar(m.Y[:, t, :], m.X[:, t, :], m.mv[:, t, 0:1], m.rstd[:, t:t + 1],
                          ALU.subtract, ALU.mult).then_inc(s["ln_y"], 1)


def ln_scalar(act, m, s):
    act.wait_ge(s["ln_var"], 1)
    act.activation(m.std[:], m.var[:], ACT.Sqrt).then_inc(s["ln_std"], 1)


def ln_tensor(pe, m, s, bank):
    for t in range(NT):
        pe.wait_ge(s["ln_y"], t + 1)
        pe.transpose(m.ps[bank][:, t * P:(t + 1) * P], m.Y[:, t, :], m.ident).then_inc(s["ln_turned"], 1)


def ln_copy(act, m, s, bank):
    act.wait_ge(s["ln_turned"], NT)
    act.copy(m.YT[:], m.ps[bank][:]).then_inc(s["ln_yt"], 1)


def linear_attention(nc, m, x_row):
    def weights_of(g, j):
        return (m.PT, m.hid)[g % 2][:, j, :]

    with ExitStack() as ctx:
        s, used = sems(nc, ctx, "lin", LN_SEMS + "proj low exps high phi vcopy turned laid "
                       "scores masked state_sum state numden numden_out spread den_eps rden normed out_sum "
                       "residual x_in")
        with nc.Block() as block:

            @block.sync
            def _(sp):
                clear_stale(sp, m)
                sp.dma_start(m.X[:], x_row).then_inc(s["x_in"], 16)
                sp.wait_ge(m.other_weights, 16)

            @block.tensor
            def _(pe):
                for t in range(NT):
                    pe.matmul(m.ps[1 + t][:, 0:384], m.ones[0:1, 0:P], m.w["a_brow"][:, 0:384],
                              start=True, stop=False, skip_group_check=True)
                ln_tensor(pe, m, s, 0)
                pe.wait_ge(s["ln_yt"], 1)
                for t in range(NT):
                    pe.matmul(m.ps[1 + t][:, 0:384], m.YT[:, t * P:(t + 1) * P], m.w["a_wqkv"],
                              start=False, stop=True, skip_group_check=True).then_inc(s["proj"], 1)
                for g in range(NG):
                    turn_heads(pe, m, s, g)
                pe.wait_ge(s["laid"], 2 * NG)

                def scores(g):
                    for j in range(4):
                        for c in range(NT):
                            r = slice(c * P, (c + 1) * P)
                            mm = pe.matmul(m.ps[j][:, r], m.KTall[32 * j:32 * j + 8, g, r],
                                           m.QTall[32 * j:32 * j + 8, g, r], start=True, stop=True)
                        mm.then_inc(s["scores"], 1)

                def states(g):
                    if g:
                        pe.wait_ge(s["state"], g)
                    for c in range(NT - 1):
                        for at in range(c + 1):
                            mm = pe.matmul(m.ps[4][:, c * P:(c + 1) * P], tile4(m.Kp, at, g),
                                           tile4(m.Vp, at, g), start=(at == 0), stop=(at == c))
                    mm.then_inc(s["state_sum"], 1)

                def values(g):
                    if g:
                        pe.wait_ge(s["numden_out"], g)
                    for c in range(1, NT):
                        r = slice(c * P, (c + 1) * P)
                        if c == 1:
                            pe.wait_ge(s["state"], g + 1)
                        pe.matmul(m.ps[5][:, r], m.S[:, g % 2, c - 1, :], m.QTall[:, g, r], start=(c == 1),
                                  stop=False, skip_group_check=True)
                    for j in range(4):
                        pe.wait_ge(s["masked"], 4 * g + j + 1)
                        q = slice(32 * j, 32 * j + 32)
                        for c in range(NT):
                            r = slice(c * P, (c + 1) * P)
                            mm = pe.matmul(m.ps[5][q, r], m.Vp[:, c, 4 * g + j, :], weights_of(g, j)[:, r],
                                           start=False, stop=True, skip_group_check=True)
                    mm.then_inc(s["numden"], 1)

                states(0)
                scores(0)
                for g in range(NG):
                    if g + 1 < NG:
                        pe.wait_ge(s["masked"], 4 * (g + 1))
                        states(g + 1)
                        scores(g + 1)
                    if g:
                        spread_den(pe, m, s, g - 1)
                    values(g)
                spread_den(pe, m, s, NG - 1)
                for t in range(NT):
                    pe.matmul(m.ps[7][:, t * P:(t + 1) * P], m.ones[0:1, 0:P],
                              m.w["a_brow"][:, 384:512], start=(t == 0), stop=False,
                              skip_group_check=True)
                project(pe, m, s, m.ps[7], m.w["a_wo"], started=True)

            @block.scalar
            def _(act):
                ln_scalar(act, m, s)
                ln_copy(act, m, s, 0)
                for t in range(NT):
                    act.wait_ge(s["high"], t + 1)
                    act.copy(m.Vp[:, t, :, 0:8], heads8(m.ps[1 + t][:, 256:384])).then_inc(s["vcopy"], 1)
                    act.wait_ge(s["low"], t + 1)
                    act.activation(m.B1[:, t, :], m.B1[:, t, :], ACT.Exp).then_inc(s["exps"], 1)
                lay_heads(act, m, s)
                for g in range(NG):
                    take_numden(act, m, s, g)

            @block.vector
            def _(dve):
                dve.wait_ge(s["x_in"], 16)
                ln_vector(dve, m, s)
                for t in range(NT):
                    dve.wait_ge(s["proj"], t + 1)
                    dve.tensor_scalar(m.B1[:, t, :], m.ps[1 + t][:, 0:256], 0.0, None,
                                      ALU.min).then_inc(s["low"], 1)
                    dve.tensor_scalar(m.B2[:, t, :], m.ps[1 + t][:, 0:256], 0.0, None,
                                      ALU.max).then_inc(s["high"], 1)
                    dve.wait_ge(s["exps"], t + 1)
                    dve.wait_ge(s["high"], t + 1)
                    for k, pad in enumerate((m.Qp, m.Kp)):
                        r = slice(P * k, P * k + P)
                        dve.tensor_tensor(pad[:, t, :, 0:8], heads8(m.B1[:, t, r]),
                                          heads8(m.B2[:, t, r]), ALU.add).then_inc(s["phi"], 1)

                def masks(g):
                    if g >= 2:
                        dve.wait_ge(s["numden"], g - 1)
                    dve.wait_ge(s["state_sum"], g + 1)
                    dve.tensor_tensor(m.S[:, g % 2, :, :],
                                      m.ps[4][:, 0:3 * P].rearrange("p (c n) -> p c n", c=3),
                                      m.t["block"].unsqueeze(1).to_broadcast([P, 3, P]), ALU.mult
                                      ).then_inc(s["state"], 1)
                    for j in range(4):
                        dve.wait_ge(s["scores"], 4 * g + j + 1)
                        dve.tensor_tensor(weights_of(g, j).rearrange("p (c i) -> p c i", c=NT),
                                          m.ps[j][:].rearrange("p (c i) -> p c i", c=NT),
                                          m.t["upto"].unsqueeze(1).to_broadcast([P, NT, P]),
                                          ALU.mult).then_inc(s["masked"], 1)

                def norm(g):
                    dve.wait_ge(s["spread"], g + 1)
                    dve.tensor_scalar(m.R[:], m.ps[6][:], 1e-6, None, ALU.add).then_inc(s["den_eps"], 1)
                    dve.wait_ge(s["den_eps"], g + 1)
                    dve.reciprocal(m.R[:], m.R[:]).then_inc(s["rden"], 1)
                    dve.wait_ge(s["rden"], g + 1)
                    dve.tensor_tensor(m.Aall[:, g, :], m.Aall[:, g, :], m.R[:], ALU.mult
                                      ).then_inc(s["normed"], 1)

                masks(0)
                for g in range(NG):
                    if g + 1 < NG:
                        masks(g + 1)
                    if g:
                        norm(g - 1)
                norm(NG - 1)
                dve.wait_ge(s["out_sum"], 1)
                dve.tensor_tensor(flat(m.X), flat(m.X), m.ps[7][:], ALU.add).then_inc(s["residual"], 1)
        retire(m, ctx, used)


def flat(x):
    return x[:].rearrange("p t d -> p (t d)")


def heads8(x):
    return x.rearrange("p (h d) -> p h d", d=8)


def tile4(padded, t, g):
    return padded[:, t, 4 * g:4 * g + 4, :].rearrange("p h d -> p (h d)")


def turn_heads(pe, m, s, g, ready=(8, 8)):
    for k, pad in enumerate((m.Qp, m.Kp)):
        n = 2 * g + k
        if g == 0:
            pe.wait_ge(s["phi"], ready[k])
        if n >= 2:
            pe.wait_ge(s["laid"], n - 1)
        for t in range(NT):
            mm = pe.transpose(m.ps[6 + n % 2][:, t * P:(t + 1) * P], tile4(pad, t, g), m.ident)
        mm.then_inc(s["turned"], 1)


def lay_heads(act, m, s, q_scale=1.0, k_scale=1.0, k_bias=0.0, small=None):
    for g in range(NG):
        for k, (all_heads, scale, bias) in enumerate(((m.QTall, q_scale, 0.0),
                                                      (m.KTall, k_scale, k_bias))):
            n = 2 * g + k
            act.wait_ge(s["turned"], n + 1)
            if small is not None and n == 0:
                act.activation(small, m.ps[6][:], ACT.Identity, scale=scale).then_inc(s["q_small"], 1)
            act.activation(all_heads[:, g, :], m.ps[6 + n % 2][:], ACT.Identity,
                           scale=scale, bias=bias).then_inc(s["laid"], 1)


def take_numden(act, m, s, g):
    act.wait_ge(s["numden"], g + 1)
    act.copy(m.Aall[:, g, :], m.ps[5][:]).then_inc(s["numden_out"], 1)


def spread_den(pe, m, s, g):
    pe.wait_ge(s["numden_out"], g + 1)
    if g:
        pe.wait_ge(s["normed"], g)
    pe.matmul(m.ps[6][:], m.t["spread8"], m.Aall[:, g, :], start=True, stop=True
              ).then_inc(s["spread"], 1)


def project(pe, m, s, bank, weights, started=False):
    for g in range(NG):
        pe.wait_ge(s["normed"], g + 1)
        for t in range(NT):
            mm = pe.matmul(bank[:, t * P:(t + 1) * P], m.Aall[:, g, t * P:(t + 1) * P],
                           weights[:, g * P:(g + 1) * P], start=(g == 0 and t == 0 and not started),
                           stop=(g == NG - 1), skip_group_check=True)
    mm.then_inc(s["out_sum"], 1)


WIDTH = [SEQ - t * P for t in range(NT)]
UNITS = [[(0, 0)], [(1, 0), (3, 384)], [(2, 0)]]
UNIT_AT = [0, 512, 1024]
KEYS_AT = [0, 512, 1024, 512 + 384]
HEAD_COLS = 1280


def unit_cols(u):
    return sum(WIDTH[kt] for kt, _ in UNITS[u])


def score_max(pe, m, q, k, before, done, tiles=range(NT), places=range(NT)):
    for place in places:
        before(place)
        i = tiles[place]
        bank = m.ps[place % 2]
        pe.matmul(bank[:, 0:(i + 1) * P], q[:, i * P:(i + 1) * P], k[:, 0:(i + 1) * P],
                  start=True, stop=False, skip_group_check=True)
        pe.matmul(bank[:, i * P:(i + 1) * P], m.identb[:], m.mask_qk[:], start=False, stop=True,
                  skip_group_check=True).then_inc(done, 1)


def score_unit(pe, m, q, k, u, bank, done):
    for n, (kt, at) in enumerate(UNITS[u]):
        pe.matmul(bank[:, at:at + WIDTH[kt]], k[:, kt * P:(kt + 1) * P], q[:, kt * P:SEQ],
                  start=(n == 0), stop=False, skip_group_check=True)
        mm = pe.matmul(bank[:, at:at + P], m.identb[:], m.mask_kq[:], start=False, stop=True,
                       skip_group_check=True)
    mm.then_inc(done, 1)


def weigh_values(pe, probs, values, rows, den_rows, num, den, ones, tiles=range(NT)):
    for kt in tiles:
        p = probs[:, KEYS_AT[kt]:KEYS_AT[kt] + WIDTH[kt]]
        pe.matmul(num[rows, kt * P:SEQ], values(kt), p, start=(kt == 0), stop=(kt == NT - 1),
                  skip_group_check=True)
        mm = pe.matmul(den[den_rows, kt * P:SEQ], ones, p, start=(kt == 0), stop=(kt == NT - 1),
                       skip_group_check=True)
    return mm


def take_swapped(dve, to, bank, done):
    dve.tensor_copy(to[0:64, :], bank[64:P, :])
    dve.tensor_copy(to[64:P, :], bank[0:64, :]).then_inc(done, 1)


RMS_SEMS = "sq_sum sq_mean sq_std sq_rstd h_ready h_turned h_laid "
FFN_EPS = 1.1920929e-07


def rms_scalar_sum(act, m, s, after=None):
    for t in range(NT):
        if after:
            act.wait_ge(s[after], t + 1)
        act.activation(m.B1[:, t, 0:P], m.Y[:, t, :], ACT.Square, accum_out=m.sq[:, t:t + 1]
                       ).then_inc(s["sq_sum"], 1)


def rms_scalar_root(act, m, s):
    act.wait_ge(s["sq_mean"], 1)
    act.activation(m.std[:], m.var[:], ACT.Sqrt).then_inc(s["sq_std"], 1)


def rms_vector(dve, m, s):
    dve.wait_ge(s["sq_sum"], NT)
    dve.tensor_scalar(m.var[:], m.sq[:], 1.0 / D, FFN_EPS, ALU.mult, ALU.add).then_inc(s["sq_mean"], 1)
    dve.wait_ge(s["sq_std"], 1)
    dve.reciprocal(m.rstd[:], m.std[:]).then_inc(s["sq_rstd"], 1)
    dve.wait_ge(s["sq_rstd"], 1)
    for t in range(NT):
        dve.tensor_scalar(m.H[:, t, :], m.Y[:, t, :], m.rstd[:, t:t + 1], None, ALU.mult
                          ).then_inc(s["h_ready"], 1)


def rms_tensor(pe, m, s, bank):
    for t in range(NT):
        pe.wait_ge(s["h_ready"], t + 1)
        pe.transpose(m.ps[bank][:, t * P:(t + 1) * P], m.H[:, t, :], m.ident).then_inc(s["h_turned"], 1)


def rms_lay(act, m, s, bank, weight):
    act.wait_ge(s["h_turned"], NT)
    act.activation(m.YT[:], m.ps[bank][:], ACT.Copy, scale=weight).then_inc(s["h_laid"], 1)


def ffn_attention(nc, m):
    def keys(n):
        return m.hid[:, n, :] if n < 15 else m.PT[:, 0, :]

    def small_keys(n):
        return m.KB[:, n % 4, :] if n // 4 % 2 == 0 else (m.K1B, m.KWB)[n % 4 // 2][:, n % 2, :]

    def own_rows(n):
        return m.t["block"][:, 32 * (n % 4):32 * (n % 4) + 1]

    scale = 8 ** -0.5
    with ExitStack() as ctx:
        s, used = sems(nc, ctx, "fat", LN_SEMS + RMS_SEMS + "proj squared vcopy head_sum head_mean "
                       "head_std head_rstd phi turned laid q_small k_small keys max_scores maxed max_turned augmented "
                       "scores probs numden numden_out spread rden normed out_sum residual")
        with nc.Block() as block:

            @block.sync
            def _(sp):
                clear_stale(sp, m)

            @block.tensor
            def _(pe):
                rms_tensor(pe, m, s, 0)
                pe.wait_ge(s["h_laid"], 1)
                for t in range(NT):
                    pe.matmul(m.ps[1 + t][:, 0:384], m.YT[:, t * P:(t + 1) * P], m.w["f_wqkv"],
                              start=True, stop=True).then_inc(s["proj"], 1)
                def rows(n):
                    return slice(32 * (n % 4), 32 * (n % 4) + 32)

                def first(n):
                    pe.wait_ge(s["q_small"], n // 4 + 1)
                    pe.wait_ge(s["k_small"], n + 1)

                    def before(i):
                        if 4 * n + i >= 2:
                            pe.wait_ge(s["maxed"], 4 * n + i - 1)
                    score_max(pe, m, m.QB[:, n // 4, :], small_keys(n), before, s["max_scores"])

                def turn_maxes(g):
                    pe.wait_ge(s["maxed"], 16 * (g + 1))
                    if g:
                        pe.wait_ge(s["augmented"], g)
                    else:
                        pe.wait_ge(s["laid"], 2 * NG)
                    for t in range(NT):
                        mm = pe.matmul(m.ps[7][:, t * P:(t + 1) * P], m.NM[:, g % 2, t, :],
                                       m.identb[:], start=True, stop=True)
                    mm.then_inc(s["max_turned"], 1)

                def second(n):
                    pe.wait_ge(s["augmented"], n // 4 + 1)
                    pe.wait_ge(s["keys"], n + 1)
                    for u in range(3):
                        if n:
                            pe.wait_ge(s["probs"], 3 * n + u - 2)
                        score_unit(pe, m, m.QTall[:, n // 4, :], keys(n), u, m.ps[2 + u], s["scores"])

                def values(n):
                    pe.wait_ge(s["probs"], 3 * n + 3)
                    if n % 4 == 0 and n:
                        pe.wait_ge(s["numden_out"], n // 4)
                    for kt in range(NT):
                        mm = pe.matmul(m.ps[5][rows(n), kt * P:SEQ], m.Vp[:, kt, n, :],
                                       m.probs[:, n % 3, KEYS_AT[kt]:KEYS_AT[kt] + WIDTH[kt]],
                                       start=(kt == 0), stop=(kt == NT - 1), skip_group_check=True)
                    if n % 4 == 3:
                        mm.then_inc(s["numden"], 1)

                turn_heads(pe, m, s, 0, ready=(4, 8))
                for n in range(4):
                    if n:
                        turn_heads(pe, m, s, n)
                    first(n)
                turn_maxes(0)
                first(4)
                for n in range(17):
                    if n < 16:
                        second(n)
                    if n % 4 == 3 and n < 15:
                        turn_maxes(n // 4 + 1)
                    if n + 5 < 16:
                        first(n + 5)
                    if n > 1 and n % 4 == 1:
                        spread_den(pe, m, s, n // 4 - 1)
                    if n:
                        values(n - 1)
                spread_den(pe, m, s, NG - 1)
                project(pe, m, s, m.ps[0], m.w["f_wo"])

            @block.scalar
            def _(act):
                ln_scalar(act, m, s)
                rms_scalar_sum(act, m, s, after="ln_y")
                rms_scalar_root(act, m, s)
                rms_lay(act, m, s, 0, m.w["f_n1"])
                for t in range(NT):
                    act.wait_ge(s["proj"], t + 1)
                    act.activation(m.B2[:, t, :], m.ps[1 + t][:, 0:256], ACT.Square
                                   ).then_inc(s["squared"], 1)
                    act.copy(m.Vp[:, t, :, 0:8], heads8(m.ps[1 + t][:, 256:384])).then_inc(s["vcopy"], 1)
                act.wait_ge(s["head_mean"], 1)
                act.activation(m.hstd[:], m.hmean[:], ACT.Sqrt).then_inc(s["head_std"], 1)
                lay_heads(act, m, s, m.w["f_qn"], m.w["f_kn"], m.t["aug8"], small=m.QB[:, 0, :])
                act.wait_ge(s["laid"], 2)
                for n in range(4):
                    act.activation(keys(n), m.KTall[:, 0, :], ACT.Copy, scale=own_rows(n)
                                   ).then_inc(s["keys"], 1)
                for n in range(16):
                    for u in range(3):
                        act.wait_ge(s["scores"], 3 * n + u + 1)
                        act.activation(m.probs[:, n % 3, UNIT_AT[u]:UNIT_AT[u] + unit_cols(u)],
                                       m.ps[2 + u][:, 0:unit_cols(u)], ACT.Exp, scale=scale
                                       ).then_inc(s["probs"], 1)
                    if n and n % 4 == 0:
                        take_numden(act, m, s, n // 4 - 1)
                take_numden(act, m, s, NG - 1)

            @block.vector
            def _(dve):
                dve.memset(m.NM[:, :, :, 96:97], 0.0)
                ln_vector(dve, m, s)
                rms_vector(dve, m, s)
                for t in range(NT):
                    dve.wait_ge(s["squared"], t + 1)
                    dve.tensor_reduce(m.hsum[:, t, :], heads8(m.B2[:, t, :]), AX.X, ALU.add
                                      ).then_inc(s["head_sum"], 1)
                dve.wait_ge(s["head_sum"], NT)
                dve.tensor_scalar(m.hmean[:], flat(m.hsum), 0.125, FFN_EPS, ALU.mult, ALU.add
                                  ).then_inc(s["head_mean"], 1)
                dve.wait_ge(s["head_std"], 1)
                dve.wait_ge(s["vcopy"], NT)
                for k, pad in enumerate((m.Qp, m.Kp)):
                    heads = slice(16 * k, 16 * k + 16)
                    dve.reciprocal(m.hsum[:, :, heads],
                                   m.hstd[:].rearrange("p (t h) -> p t h", t=NT)[:, :, heads]
                                   ).then_inc(s["head_rstd"], 1)
                    dve.wait_ge(s["head_rstd"], k + 1)
                    for t in range(NT):
                        dve.tensor_tensor(pad[:, t, :, 0:8], heads8(m.ps[1 + t][:, P * k:P * k + P]),
                                          m.hsum[:, t, 16 * k:16 * k + 16].unsqueeze(2)
                                          .to_broadcast([P, 16, 8]), ALU.mult).then_inc(s["phi"], 1)

                def largest(n):
                    g = n // 4
                    for i in range(NT):
                        dve.wait_ge(s["max_scores"], 4 * n + i + 1)
                        dve.tensor_reduce(m.NM[:, g % 2, i, 32 * (n % 4) + 8:32 * (n % 4) + 9],
                                          m.ps[i % 2][:, 0:(i + 1) * P], AX.X, ALU.max,
                                          negate=True).then_inc(s["maxed"], 1)

                def augment(g):
                    dve.wait_ge(s["q_small"], g + 1)
                    dve.wait_ge(s["max_turned"], g + 1)
                    dve.tensor_tensor(m.QTall[:, g, :], m.QTall[:, g, :], m.ps[7][:], ALU.add
                                      ).then_inc(s["augmented"], 1)

                def norm(g):
                    dve.wait_ge(s["spread"], g + 1)
                    dve.reciprocal(m.R[:], m.ps[6][:]).then_inc(s["rden"], 1)
                    dve.wait_ge(s["rden"], g + 1)
                    dve.tensor_tensor(m.Aall[:, g, :], m.Aall[:, g, :], m.R[:], ALU.mult
                                      ).then_inc(s["normed"], 1)

                dve.wait_ge(s["laid"], 2)
                for n in range(4):
                    dve.tensor_scalar(small_keys(n), m.KTall[:, 0, :], own_rows(n), None, ALU.mult
                                      ).then_inc(s["k_small"], 1)
                for n in range(4):
                    largest(n)
                augment(0)
                largest(4)
                for n in range(17):
                    if n % 4 == 3 and n < 15:
                        augment(n // 4 + 1)
                    if n + 5 < 16:
                        largest(n + 5)
                    if 4 <= n + 4 < 16:
                        dve.wait_ge(s["keys"], n + 4)
                        dve.wait_ge(s["laid"], 2 * (n // 4) + 4)
                        dve.tensor_scalar(keys(n + 4), m.KTall[:, n // 4 + 1, :], own_rows(n + 4), None,
                                          ALU.mult).then_inc(s["keys"], 1)
                    if n > 1 and n % 4 == 1:
                        norm(n // 4 - 1)
                norm(NG - 1)
                dve.wait_ge(s["out_sum"], 1)
                dve.tensor_tensor(m.Y[:, :, 32:P], m.Y[:, :, 32:P],
                                  m.ps[0][:].rearrange("p (t d) -> p t d", t=NT)[:, :, 32:P],
                                  ALU.add).then_inc(s["residual"], 1)

            @block.gpsimd
            def _(pool):
                for g in range(NG):
                    if g:
                        pool.wait_ge(s["laid"], 2 * g + 1)
                        pool.wait_ge(s["q_small"], g)
                        pool.tensor_copy(m.QB[:, g, :], m.QTall[:, g, :]).then_inc(s["q_small"], 1)
                    pool.wait_ge(s["laid"], 2 * g + 2)
                    if g >= 2:
                        pool.wait_ge(s["max_scores"], 16 * (g - 1))
                    if g:
                        pool.wait_ge(s["k_small"], 4 * g)
                        for n in range(4 * g, 4 * g + 4):
                            pool.tensor_scalar(small_keys(n), m.KTall[:, g, :], own_rows(n), None,
                                               ALU.mult).then_inc(s["k_small"], 1)
        retire(m, ctx, used)


HIDDEN = [
    ("e1g_0", (), "f_e1_w1", 0, ACT.Silu), ("e1g_1", (), "f_e1_w1", 128, ACT.Silu),
    ("e1v_0", (), "f_e1_w2", 0, ACT.Copy), ("e1v_1", (), "f_e1_w2", 128, ACT.Copy),
    ("e0_0", (), "f_e0_up", 0, ACT.Gelu), ("e0_1", (), "f_e0_up", 128, ACT.Gelu),
    ("e2a_0", (), "f_e2_l1", 0, ACT.Gelu), ("e2a_1", (), "f_e2_l1", 128, ACT.Gelu),
    ("e3a", (), "f_e3_dn", 0, ACT.Gelu),
    ("e2b_0", ("e2a_0", "e2a_1"), "f_e2_l2", 0, ACT.Gelu),
    ("e2b_1", ("e2a_0", "e2a_1"), "f_e2_l2", 128, ACT.Gelu),
    ("e3b_0", ("e3a",), "f_e3_up", 0, ACT.Gelu), ("e3b_1", ("e3a",), "f_e3_up", 128, ACT.Gelu),
    ("e2c_0", ("e2b_0", "e2b_1"), "f_e2_l3", 0, ACT.Gelu),
    ("e2c_1", ("e2b_0", "e2b_1"), "f_e2_l3", 128, ACT.Gelu),
]
TILE = {h[0]: n for n, h in enumerate(HIDDEN)}
EXPERT_OUT = [(8, 1, ("e1g_0", "e1g_1"), "f_e1_dn"), (10, 0, ("e0_0", "e0_1"), "f_e0_dn"),
              (13, 3, ("e3b_0", "e3b_1"), "f_e3_out"), (14, 2, ("e2c_0", "e2c_1"), "f_e2_l4")]
FLOAT_MAX = float(np.finfo(np.float32).max)


def experts(nc, m):
    with ExitStack() as ctx:
        s, used = sems(nc, ctx, "moe", RMS_SEMS + "gate_sum logits gmax gshift gexp gsum grec probs gt "
                       "eq eqlow rank_terms rank kept topsum topeps toprec weights hidden_sum hidden gated out_sum "
                       "mixed residual")
        with nc.Block() as block:

            @block.sync
            def _(sp):
                clear_stale(sp, m)

            @block.tensor
            def _(pe):
                rms_tensor(pe, m, s, 0)
                pe.wait_ge(s["h_laid"], 1)
                for t in range(NT):
                    mm = pe.matmul(m.ps[7][:, 4 * t:4 * t + 4], m.YT[:, t * P:(t + 1) * P],
                                   m.w["f_gate"], start=True, stop=True)
                mm.then_inc(s["gate_sum"], 1)
                outs = list(EXPERT_OUT)
                done = 0
                for n, (name, sources, w, at, func) in enumerate(HIDDEN):
                    if n >= 6:
                        pe.wait_ge(s["hidden"], n - 5)
                    for k, src in enumerate(sources or (None,)):
                        if src:
                            pe.wait_ge(s["hidden"], TILE[src] + 1)
                        rhs = m.hid[:, TILE[src], :] if src else m.YT[:]
                        mm = pe.matmul(m.ps[n % 6][:], m.w[w][:, 256 * k + at:256 * k + at + P], rhs,
                                       start=(k == 0), stop=(k == max(len(sources), 1) - 1))
                    mm.then_inc(s["hidden_sum"], 1)
                    while outs and outs[0][0] == n:
                        _, e, (a, b), w = outs.pop(0)
                        pe.wait_ge(s["hidden"], max(TILE[a], TILE[b]) + 1)
                        if e == 1:
                            pe.wait_ge(s["gated"], 2)
                        if done == 0:
                            pe.wait_ge(s["logits"], 1)
                        if done >= 2:
                            pe.wait_ge(s["mixed"], 4 * (done - 1))
                        for t in range(NT):
                            r = slice(t * P, (t + 1) * P)
                            pe.matmul(m.ps[6 + done % 2][:, r], m.hid[:, TILE[a], r], m.w[w][:, 0:P],
                                      start=(t == 0), stop=False, skip_group_check=True)
                            mm = pe.matmul(m.ps[6 + done % 2][:, r], m.hid[:, TILE[b], r],
                                           m.w[w][:, P:256], start=False, stop=True,
                                           skip_group_check=True)
                        mm.then_inc(s["out_sum"], 1)
                        done += 1

            @block.scalar
            def _(act):
                rms_scalar_sum(act, m, s)
                rms_scalar_root(act, m, s)
                rms_lay(act, m, s, 0, m.w["f_n2"])
                act.wait_ge(s["gshift"], 1)
                act.activation(m.g16b[:], m.g16[:], ACT.Exp).then_inc(s["gexp"], 1)
                for n, (name, sources, w, at, func) in enumerate(HIDDEN):
                    act.wait_ge(s["hidden_sum"], n + 1)
                    act.activation(m.hid[:, n, :], m.ps[n % 6][:], func).then_inc(s["hidden"], 1)

            @block.vector
            def _(dve):
                rms_vector(dve, m, s)
                te = lambda x: x[:].rearrange("p (t e) -> p t e", e=4)
                over = lambda x: x.unsqueeze(2).to_broadcast([P, NT, 4])
                dve.wait_ge(s["gate_sum"], 1)
                dve.tensor_scalar(m.g16[:], m.ps[7][:, 0:16], FLOAT_MAX, -FLOAT_MAX, ALU.min, ALU.max
                                  ).then_inc(s["logits"], 1)
                dve.wait_ge(s["logits"], 1)
                dve.tensor_reduce(m.g4[:], te(m.g16), AX.X, ALU.max).then_inc(s["gmax"], 1)
                dve.wait_ge(s["gmax"], 1)
                dve.tensor_tensor(te(m.g16), te(m.g16), over(m.g4[:]), ALU.subtract
                                  ).then_inc(s["gshift"], 1)
                dve.wait_ge(s["gexp"], 1)
                dve.tensor_reduce(m.g4[:], te(m.g16b), AX.X, ALU.add).then_inc(s["gsum"], 1)
                dve.wait_ge(s["gsum"], 1)
                dve.reciprocal(m.g4b[:], m.g4[:]).then_inc(s["grec"], 1)
                dve.wait_ge(s["grec"], 1)
                dve.tensor_tensor(te(m.g16), te(m.g16b), over(m.g4b[:]), ALU.mult
                                  ).then_inc(s["probs"], 1)
                dve.wait_ge(s["probs"], 1)
                others = te(m.g16).unsqueeze(2).to_broadcast([P, NT, 4, 4])
                own = te(m.g16).unsqueeze(3).to_broadcast([P, NT, 4, 4])
                t44 = lambda x: x[:].rearrange("p (t e f) -> p t e f", t=NT, e=4)
                dve.tensor_tensor(t44(m.g64), others, own, ALU.is_gt).then_inc(s["gt"], 1)
                dve.tensor_tensor(t44(m.g64b), others, own, ALU.is_equal).then_inc(s["eq"], 1)
                dve.wait_ge(s["eq"], 1)
                low = m.t["lower4"].unsqueeze(1).to_broadcast([P, NT, 16])
                t16 = lambda x: x[:].rearrange("p (t e) -> p t e", t=NT)
                dve.tensor_tensor(t16(m.g64b), t16(m.g64b), low, ALU.mult).then_inc(s["eqlow"], 1)
                dve.wait_ge(s["eqlow"], 1)
                dve.wait_ge(s["gt"], 1)
                dve.tensor_tensor(m.g64[:], m.g64[:], m.g64b[:], ALU.add).then_inc(s["rank_terms"], 1)
                dve.wait_ge(s["rank_terms"], 1)
                dve.tensor_reduce(m.g16b[:], m.g64[:].rearrange("p (n f) -> p n f", f=4), AX.X,
                                  ALU.add).then_inc(s["rank"], 1)
                dve.wait_ge(s["rank"], 1)
                dve.scalar_tensor_tensor(m.top[:], m.g16b[:], 1.5, m.g16[:], ALU.is_lt, ALU.mult
                                         ).then_inc(s["kept"], 1)
                dve.wait_ge(s["kept"], 1)
                dve.tensor_reduce(m.g4[:], te(m.top), AX.X, ALU.add).then_inc(s["topsum"], 1)
                dve.wait_ge(s["topsum"], 1)
                dve.tensor_scalar(m.g4[:], m.g4[:], 1e-8, None, ALU.add).then_inc(s["topeps"], 1)
                dve.wait_ge(s["topeps"], 1)
                dve.reciprocal(m.g4b[:], m.g4[:]).then_inc(s["toprec"], 1)
                dve.wait_ge(s["toprec"], 1)
                dve.tensor_tensor(te(m.top), te(m.top), over(m.g4b[:]), ALU.mult
                                  ).then_inc(s["weights"], 1)
                dve.wait_ge(s["weights"], 1)
                for n, (_, e, _, _) in enumerate(EXPERT_OUT):
                    if e == 1:
                        for k in range(2):
                            dve.wait_ge(s["hidden"], TILE["e1v_1"] + 1)
                            dve.tensor_tensor(m.hid[:, TILE["e1g_0"] + k, :],
                                              m.hid[:, TILE["e1g_0"] + k, :],
                                              m.hid[:, TILE["e1v_0"] + k, :], ALU.mult
                                              ).then_inc(s["gated"], 1)
                    dve.wait_ge(s["out_sum"], n + 1)
                    for t in range(NT):
                        w = m.top[:, 4 * t + e:4 * t + e + 1]
                        o = m.ps[6 + n % 2][:, t * P + 32:(t + 1) * P]
                        if n:
                            dve.wait_ge(s["mixed"], 4 * (n - 1) + t + 1)
                        dve.scalar_tensor_tensor(m.Y[:, t, 32:P], o, w, m.Y[:, t, 32:P], ALU.mult,
                                                 ALU.add).then_inc(s["mixed"], 1)
                dve.wait_ge(s["mixed"], 16)
                dve.tensor_tensor(flat(m.X), flat(m.X), flat(m.Y), ALU.add).then_inc(s["residual"], 1)
        retire(m, ctx, used)


MLA_EPS = 1e-6
KEEP = 32
LATENT, SELECTED, WINDOW = 0, 1, 2
W_Q, W_WIN, W_SEL, W_LATENT = 0, 1, 2, 3
JOBS = [(g, x, j) for g in range(NG)
        for x, j in [(LATENT, j) for j in range(4)] + [(WINDOW, j) for j in range(4)] + [(SELECTED, 0)]]
PER_GROUP = 9


def key_item(k):
    g, x, j = JOBS[k]
    return (g, x, 0) if x == LATENT else JOBS[k]


def preparations():
    order, upto = [("q", 0, 0), JOBS[0], ("q", 0, 1), ("q", 0, 2), ("q", 0, 3)], []
    q_steps = {0: 0, 1: 1, 6: 2, 8: 3}
    for k in range(len(JOBS)):
        if k + 2 < len(JOBS) and key_item(k + 2) == JOBS[k + 2]:
            order.append(JOBS[k + 2])
        g, local = divmod(k, PER_GROUP)
        if local in q_steps and g + 1 < NG:
            order.append(("q", g + 1, q_steps[local]))
        upto.append(len(order))
    return order, upto


PREPS, PREPS_UPTO = preparations()
PREP_AT = {item: n for n, item in enumerate(PREPS)}
FIRST_PREPS, OWN_BANK = 5, 4
SWAPS_BEFORE = [sum(not (q[0] != "q" and q[1] == LATENT) for q in PREPS[:p]) for p in range(len(PREPS))]


def needed(k):
    g, x, j = JOBS[k]
    items = [("q", g, i) for i in (range(4) if x == SELECTED else [j])]
    return max(SWAPS_BEFORE[PREP_AT[i]] + 1 for i in items + [JOBS[k]] * (x != LATENT))


FIRST_TILES = [3, 2, 1, 0]
JOB_UNITS = [1 if x == SELECTED else 3 for _, x, _ in JOBS]
UNITS_BEFORE = [sum(JOB_UNITS[:k]) for k in range(len(JOBS) + 1)]
MAXES = [1 if x == SELECTED else NT for _, x, _ in JOBS]
MAXES_BEFORE = [sum(MAXES[:k]) for k in range(len(JOBS) + 1)]
def ends_kind(k):
    g, x, j = JOBS[k]
    return x == SELECTED or j == 3


KINDS_BEFORE = [sum(ends_kind(i) for i in range(k)) for k in range(len(JOBS) + 1)]
MAXED_ROWS = [sum(4 if x == SELECTED else 1 for _, x, _ in JOBS[:k]) for k in range(len(JOBS) + 1)]


def step_items(k):
    if k >= len(JOBS):
        return []
    return list(range(PREPS_UPTO[k - 1] if k else FIRST_PREPS, PREPS_UPTO[k]))


def mla_prepare(nc, m, mw):
    with ExitStack() as ctx:
        s, used = sems(nc, ctx, "mpre", LN_SEMS + "chain latent squares means roots normed turned laid "
                       "krope gate_sum gates_in gate_mean gmax gexp gates v1 imp before_sum "
                       "kept onehot picked picked_laid vs vs_read v1_read vw_read k_laid weights")
        with nc.Block() as block:

            @block.sync
            def _(sp):
                sp.dma_start(m.mw[:, 0:2, :], mw[0:2].rearrange("g p c -> p g c")
                             ).then_inc(s["weights"], 16)
                sp.wait_ge(s["weights"], 16)
                clear_stale(sp, m)

            @block.tensor
            def _(pe):
                ln_tensor(pe, m, s, 0)
                pe.wait_ge(s["ln_yt"], 1)
                cq = W_AT["m_cq"][0]
                for t in range(NT):
                    pe.matmul(m.ps[1][:, t * P:(t + 1) * P], m.YT[:, t * P:(t + 1) * P],
                              m.w_all[:, cq:cq + P], start=True, stop=True).then_inc(s["latent"], 1)
                pe.matmul(m.ps[2][:], m.w["m_imp"], m.YT[:], start=True, stop=True).then_inc(s["imp"], 1)
                pe.matmul(m.ps[3][0:64, :], m.w["m_krope"], m.YT[:], start=True, stop=True
                          ).then_inc(s["krope"], 1)
                for t in range(NT):
                    mm = pe.matmul(m.ps[5][:, 4 * t:4 * t + 3], m.YT[:, t * P:(t + 1) * P],
                                   m.w["m_gate"], start=True, stop=True)
                mm.then_inc(s["gate_sum"], 1)
                pe.wait_ge(s["gates_in"], 1)
                for t in range(NT):
                    mm = pe.matmul(m.ps[6][:, 0:3], m.ones[:], m.small[:, 4 * t:4 * t + 3],
                                   start=(t == 0), stop=(t == NT - 1))
                mm.then_inc(s["gate_mean"], 1)
                for t in range(NT):
                    pe.wait_ge(s["normed"], 2 * t + 2)
                    mm = pe.transpose(m.ps[7][:, t * P:(t + 1) * P], m.H[:, t, :], m.ident)
                mm.then_inc(s["turned"], 1)
                pe.wait_ge(s["laid"], 1)
                for n in range(2 * NT):
                    t, wide = n % NT, n // NT
                    if n == 0:
                        pe.wait_ge(s["v1_read"], 1)
                    if n >= 2:
                        pe.wait_ge(s["vw_read"], n - 1)
                    src = (m.YT if wide else m.NCT)[:, t * P:(t + 1) * P]
                    pe.matmul(m.ps[3 + n % 2][:], src, m.w["m_winv" if wide else "m_dv"],
                              start=True, stop=True).then_inc(s["v1"], 1)
                pe.wait_ge(s["kept"], 1)
                pe.matmul(m.ps[6][:, 8:12], m.t["before"], m.small[:, 20:24], start=True, stop=False,
                          skip_group_check=True)
                for t in range(1, NT):
                    mm = pe.matmul(m.ps[6][:, 8 + t:12], m.ones[:], m.small[:, 20:24 - t],
                                   start=False, stop=True, skip_group_check=True)
                mm.then_inc(s["before_sum"], 1)
                pe.wait_ge(s["onehot"], 4)
                for t in range(NT):
                    mm = pe.matmul(m.ps[5][:, 0:P], m.Y[:, t, :], m.onehot[:, t, :],
                                   start=(t == 0), stop=(t == NT - 1))
                mm.then_inc(s["picked"], 1)
                pe.wait_ge(s["picked_laid"], 1)
                pe.matmul(m.ps[0][:], m.SELT, m.w["m_selv"], start=True, stop=True
                          ).then_inc(s["vs"], 1)

            @block.scalar
            def _(act):
                ln_scalar(act, m, s)
                ln_copy(act, m, s, 0)
                act.wait_ge(s["latent"], NT)
                for t in range(NT):
                    act.activation(m.B1[:, t, 0:96], m.ps[1][:, t * P:t * P + 96], ACT.Square,
                                   accum_out=m.small[:, 24 + t:25 + t]).then_inc(s["squares"], 1)
                    act.activation(m.B1[:, t, 96:P], m.ps[1][:, t * P + 96:(t + 1) * P], ACT.Square,
                                   accum_out=m.small[:, 28 + t:29 + t]).then_inc(s["squares"], 1)
                act.wait_ge(s["means"], 1)
                act.activation(m.small[:, 40:48], m.small[:, 32:40], ACT.Sqrt).then_inc(s["roots"], 1)
                act.wait_ge(s["turned"], 1)
                act.activation(m.NCT, m.ps[7][:], ACT.Copy, scale=m.w["m_gqkv"]).then_inc(s["laid"], 1)
                act.wait_ge(s["gmax"], 1)
                act.activation(m.small[:, 52:55], m.small[:, 48:51], ACT.Exp,
                               bias=m.small[:, 51:52]).then_inc(s["gexp"], 1)
                act.wait_ge(s["gates"], 1)
                for n in range(2 * NT):
                    t, wide = n % NT, n // NT
                    act.wait_ge(s["v1"], n + 1)
                    act.activation((m.VW if wide else m.V1)[:, t, :, :].rearrange("p h d -> p (h d)"),
                                   m.ps[3 + n % 2][:], ACT.Copy,
                                   scale=m.gates[:, 2 * wide:2 * wide + 1]).then_inc(s["vw_read"], 1)
                act.wait_ge(s["picked"], 1)
                act.copy(m.SELT, m.ps[5][:, 0:P]).then_inc(s["picked_laid"], 1)

            @block.vector
            def _(dve):
                count = [0]

                def link(ins):
                    count[0] += 1
                    ins.then_inc(s["chain"], 1)
                    dve.wait_ge(s["chain"], count[0])

                dve.memset(m.NM[:, :, :, 8:P:32], 0.0)
                ln_vector(dve, m, s)
                dve.wait_ge(s["squares"], 8)
                link(dve.tensor_scalar(m.small[:, 32:36], m.small[:, 24:28], 1.0 / 96, MLA_EPS,
                                       ALU.mult, ALU.add))
                dve.tensor_scalar(m.small[:, 36:40], m.small[:, 28:32], 1.0 / 32, MLA_EPS,
                                  ALU.mult, ALU.add).then_inc(s["means"], 1)
                dve.wait_ge(s["roots"], 1)
                link(dve.reciprocal(m.small[:, 56:64], m.small[:, 40:48]))
                for t in range(NT):
                    dve.tensor_scalar(m.H[:, t, 0:96], m.ps[1][:, t * P:t * P + 96],
                                      m.small[:, 56 + t:57 + t], None, ALU.mult).then_inc(s["normed"], 1)
                    dve.tensor_scalar(m.H[:, t, 96:P], m.ps[1][:, t * P + 96:(t + 1) * P],
                                      m.small[:, 60 + t:61 + t], None, ALU.mult).then_inc(s["normed"], 1)
                dve.wait_ge(s["gate_sum"], 1)
                dve.tensor_copy(m.small[:, 0:16].rearrange("p (t e) -> p t e", e=4)[:, :, 0:3],
                                m.ps[5][:, 0:16].rearrange("p (t e) -> p t e", e=4)[:, :, 0:3]
                                ).then_inc(s["gates_in"], 1)
                dve.wait_ge(s["gate_mean"], 1)
                link(dve.tensor_scalar(m.small[:, 48:51], m.ps[6][:, 0:3], 1.0 / SEQ, None, ALU.mult))
                dve.tensor_reduce(m.small[:, 51:52], m.small[:, 48:51], AX.X, ALU.max, negate=True
                                  ).then_inc(s["gmax"], 1)
                dve.wait_ge(s["gexp"], 1)
                link(dve.tensor_reduce(m.small[:, 55:56], m.small[:, 52:55], AX.X, ALU.add))
                link(dve.reciprocal(m.small[:, 16:17], m.small[:, 55:56]))
                dve.tensor_scalar(m.gates[:], m.small[:, 52:55], m.small[:, 16:17], None, ALU.mult
                                  ).then_inc(s["gates"], 1)
                dve.wait_ge(s["krope"], 1)
                link(dve.scalar_tensor_tensor(m.R[0:64, :], m.ps[3][0:64, :], 1.0 / 16,
                                              m.t["rope_c"][0:64, :], ALU.mult, ALU.mult))
                for src, to in ((slice(32, 64), slice(0, 32)), (slice(0, 32), slice(32, 64))):
                    link(dve.scalar_tensor_tensor(m.A[to, :], m.ps[3][src, :], 1.0 / 16,
                                                  m.t["rope_s"][src, :], ALU.mult, ALU.mult))
                dve.tensor_tensor(m.Aall[0:64, 0, :], m.R[0:64, :], m.A[0:64, :], ALU.add
                                  ).then_inc(s["v1_read"], 1)
                dve.wait_ge(s["imp"], 1)
                link(dve.tensor_copy(m.imp, m.ps[2][:]))
                for t in range(NT):
                    link(dve.scalar_tensor_tensor(m.H2, m.imp[:, t * P:(t + 1) * P], 1.0, m.ident,
                                                  ALU.mult, ALU.mult, accum_out=m.own[:, t:t + 1]))
                for t in range(NT):
                    link(dve.tensor_scalar(m.R[:], m.imp, m.own[:, t:t + 1], 0.0, ALU.is_gt, ALU.add,
                                           accum_out=m.own[:, 4 + t:5 + t]))
                    if t:
                        link(dve.tensor_scalar(m.R[:, 0:t * P], m.imp[:, 0:t * P], m.own[:, t:t + 1], None,
                                               ALU.is_equal))
                    r = slice(t * P, (t + 1) * P)
                    link(dve.scalar_tensor_tensor(m.R[:, r], m.imp[:, r], m.own[:, t:t + 1],
                                                  m.t["below"], ALU.is_equal, ALU.mult))
                    link(dve.tensor_reduce(m.own[:, 8 + t:9 + t], m.R[:, 0:(t + 1) * P], AX.X, ALU.add))
                link(dve.tensor_tensor(m.own[:, 12:16], m.own[:, 4:8], m.own[:, 8:12], ALU.add))
                dve.tensor_scalar(m.small[:, 20:24], m.own[:, 12:16], KEEP - 0.5, None, ALU.is_lt
                                  ).then_inc(s["kept"], 1)
                dve.wait_ge(s["before_sum"], 1)
                link(dve.tensor_copy(m.own[:, 16:20], m.ps[6][:, 8:12]))
                for t in range(NT):
                    dve.tensor_scalar(m.onehot[:, t, :].rearrange("p (r k) -> p r k", k=KEEP),
                                      m.t["iota"].unsqueeze(1).to_broadcast([P, 4, KEEP]),
                                      m.own[:, 16 + t:17 + t], m.small[:, 20 + t:21 + t],
                                      ALU.is_equal, ALU.mult).then_inc(s["onehot"], 1)
                dve.wait_ge(s["vs"], 1)
                dve.scalar_tensor_tensor(
                    m.VS, m.ps[0][:].rearrange("p (g n) -> p g n", g=NG), m.gates[:, 1:2],
                    m.t["block"][:, 0:P].unsqueeze(1).to_broadcast([P, NG, P]), ALU.mult, ALU.mult
                    ).then_inc(s["vs_read"], 1)

            @block.gpsimd
            def _(pool):
                pool.wait_ge(s["v1_read"], 1)
                for k in range(4):
                    pool.tensor_copy(m.K1[0:64, k, :], m.Aall[0:64, 0, :])
                for k in range(4):
                    ins = pool.tensor_copy(m.K1B[0:64, k, :], m.Aall[0:64, 0, :])
                ins.then_inc(s["k_laid"], 1)
        retire(m, ctx, used)


def mla_heads(nc, m, mw):
    scale = 96 ** -0.5
    with ExitStack() as ctx:
        s, used = sems(nc, ctx, "mla", "weights_even weights_odd prep plain roped added small latent_small max_scores maxed "
                       "max_turned augmented scores probs numden num_out den_out rden part normed last out_sum residual")

        def landed(g):
            return (s["weights_even"], s["weights_odd"])[g % 2]

        def wt(g, part, j):
            at = 384 * part + 96 * j
            return m.mw[:, g % 2, at:at + 96]

        def prep_bank(p):
            return m.ps[[6, 7, 4, 5][p] if p < OWN_BANK else 6 + p % 2]

        def q_tile(g, j):
            return m.Q[:, (g % 2) * 4 + j, :]

        def k_tile(k):
            _, x, j = JOBS[k]
            return (m.K1[0:97, j, :] if x == LATENT else m.KW[0:97, j % 2, :])

        with nc.Block() as block:

            @block.sync
            def _(sp):
                for g in range(2, NG):
                    sp.wait_ge(s["prep"], PREP_AT[(g - 2, SELECTED, 0)] + 1)
                    sp.dma_start(m.mw[:, g % 2, :], mw[g]).then_inc(landed(g), 16)
                clear_stale(sp, m)

            @block.tensor
            def _(pe):
                def prepare(p):
                    kind, a, b = PREPS[p]
                    g = a if kind == "q" else kind
                    if g >= 2:
                        pe.wait_ge(landed(g), 16)
                    if p >= OWN_BANK:
                        pe.wait_ge(s["roped"], p - 1)
                    bank = prep_bank(p)
                    if kind != "q" and a == SELECTED:
                        for j in range(4):
                            mm = pe.matmul(bank[0:96, KEEP * j:KEEP * j + KEEP], wt(g, W_SEL, j),
                                           m.SELT[:, 0:KEEP], start=True, stop=True)
                    elif kind != "q" and a == LATENT:
                        at = 384 * W_LATENT
                        mm = pe.matmul(bank[:], m.mw[:, g % 2, at:at + P], m.NCT, start=True, stop=True)
                    else:
                        part, src = (W_Q, m.NCT) if kind == "q" else (W_WIN, m.YT[:])
                        mm = pe.matmul(bank[0:96, :], wt(g, part, b), src, start=True, stop=True)
                    mm.then_inc(s["prep"], 1)

                def first(k, places):
                    g, x, j = JOBS[k]
                    if 0 in places:
                        pe.wait_ge(s["small"], needed(k))
                        if x == LATENT:
                            pe.wait_ge(s["latent_small"], g + 1)
                        if k:
                            pe.wait_ge(s["augmented"], MAXED_ROWS[k])
                    if x == SELECTED:
                        if 0 not in places:
                            return
                        for t in range(NT):
                            for h in range(4):
                                c = t * P + KEEP * h
                                mm = pe.matmul(m.ps[0][:, c:c + KEEP],
                                               m.QB[0:96, 4 * (g % 2) + h, t * P:(t + 1) * P],
                                               m.KSB[0:96, KEEP * h:KEEP * h + KEEP],
                                               start=True, stop=True)
                        mm.then_inc(s["max_scores"], 1)
                    else:
                        def before(i):
                            if i >= 2:
                                pe.wait_ge(s["maxed"], MAXES_BEFORE[k] + i - 1)
                        score_max(pe, m, m.QB[0:96, 4 * (g % 2) + j, :],
                                  m.K1B[0:96, j, :] if x == LATENT else m.KWB[0:96, j % 2, :],
                                  before, s["max_scores"], FIRST_TILES, places)

                def turn_max(k, h):
                    for t in range(NT):
                        mm = pe.matmul(m.ps[h % 2][:, t * P:(t + 1) * P], m.NMm[:, h, t, :],
                                       m.identb[:], start=True, stop=True)
                    mm.then_inc(s["max_turned"], 1)

                def turn_maxes(k):
                    pe.wait_ge(s["maxed"], MAXES_BEFORE[k + 1])
                    for h in range(4 if JOBS[k][1] == SELECTED else 1):
                        if h >= 2:
                            pe.wait_ge(s["augmented"], MAXED_ROWS[k] + h - 1)
                        turn_max(k, h)

                def second(k):
                    g, x, j = JOBS[k]
                    pe.wait_ge(s["augmented"], MAXED_ROWS[k + 1])
                    pe.wait_ge(s["added"], needed(k))
                    for u in range(JOB_UNITS[k]):
                        n = UNITS_BEFORE[k] + u
                        if n >= 2:
                            pe.wait_ge(s["probs"], n - 1)
                        if x == SELECTED:
                            for h in range(4):
                                mm = pe.matmul(m.ps[2 + n % 2][32 * h:32 * h + 32, :],
                                               m.KS[0:97, KEEP * h:KEEP * h + KEEP],
                                               q_tile(g, h)[0:97, :], start=True, stop=True)
                            mm.then_inc(s["scores"], 1)
                        else:
                            score_unit(pe, m, q_tile(g, j)[0:97, :], k_tile(k), u, m.ps[2 + n % 2],
                                       s["scores"])

                def values(k, tiles):
                    g, x, j = JOBS[k]
                    if 0 not in tiles and x == SELECTED:
                        return
                    pe.wait_ge(s["probs"], UNITS_BEFORE[k + 1])
                    if (x == SELECTED or j == 0) and KINDS_BEFORE[k]:
                        pe.wait_ge(s["num_out"], KINDS_BEFORE[k])
                        pe.wait_ge(s["den_out"], KINDS_BEFORE[k])
                    if x == SELECTED:
                        pe.matmul(m.ps[4][:], m.VS[:, g, :], m.probs[:, k % 3, 0:SEQ], start=True,
                                  stop=True)
                        for to, at in ((0, 64), (64, 0)):
                            mm = pe.matmul(m.ps[5][to:to + 64, :], m.t["block"][:, at:at + 64],
                                           m.probs[:, k % 3, 0:SEQ], start=True, stop=True)
                    else:
                        v = m.V1 if x == LATENT else m.VW
                        mm = weigh_values(pe, m.probs[:, k % 3, :], lambda kt: v[:, kt, 4 * g + j, :],
                                          slice(32 * j, 32 * j + 32),
                                          slice(32 * ((j + 2) % 4), 32 * ((j + 2) % 4) + 32),
                                          m.ps[4], m.ps[5], m.ones[:, 0:32], tiles)
                    if ends_kind(k) and (x == SELECTED or NT - 1 in tiles):
                        mm.then_inc(s["numden"], 1)

                for p in range(OWN_BANK):
                    prepare(p)
                first(0, range(NT))
                for p in range(OWN_BANK, FIRST_PREPS):
                    prepare(p)
                turn_maxes(0)
                for k in range(len(JOBS) + 1):
                    items = step_items(k)
                    if k < len(JOBS):
                        second(k)
                    if k + 1 < len(JOBS):
                        first(k + 1, [0, 1])
                    for p in items[:1]:
                        prepare(p)
                    if k + 1 < len(JOBS):
                        first(k + 1, [2, 3])
                    if k:
                        values(k - 1, [0])
                    if k + 1 < len(JOBS):
                        turn_maxes(k + 1)
                    if k:
                        values(k - 1, [1, 2, 3])
                    for p in items[1:]:
                        prepare(p)
                for g in range(NG):
                    pe.wait_ge(s["normed"], min(3 * g + 3, 3 * NG - 1))
                    for t in range(NT):
                        pe.matmul(m.ps[0][:, t * P:(t + 1) * P], m.Aall[:, g, t * P:(t + 1) * P],
                                  m.w["m_proj"][:, g * P:(g + 1) * P], start=(g == 0 and t == 0),
                                  stop=False, skip_group_check=True)
                for t in range(NT):
                    if t % 2 == 0:
                        pe.wait_ge(s["last"], t // 2 + 1)
                    mm = pe.matmul(m.ps[0][:, t * P:(t + 1) * P], m.nums[1][:, t * P:(t + 1) * P],
                                   m.w["m_proj"][:, 3 * P:4 * P], start=False, stop=True,
                                   skip_group_check=True)
                mm.then_inc(s["out_sum"], 1)

            @block.scalar
            def _(act):
                def augment(k):
                    g, x, j = JOBS[k]
                    for h in range(4 if x == SELECTED else 1):
                        act.wait_ge(s["max_turned"], MAXED_ROWS[k] + h + 1)
                        act.copy(q_tile(g, h if x == SELECTED else j)[96:97, :],
                                 m.ps[h % 2][96:97, :]
                                 ).then_inc(s["augmented"], 1)

                def take_num(k):
                    n = KINDS_BEFORE[k]
                    act.wait_ge(s["numden"], n + 1)
                    if n >= 2:
                        act.wait_ge(s["normed"], n - 1)
                    act.copy(m.nums[n % 2], m.ps[4][:]).then_inc(s["num_out"], 1)

                def latent_small(k):
                    act.wait_ge(s["roped"], PREP_AT[JOBS[k]] + 1)
                    for j in range(4):
                        ins = act.copy(m.K1B[64:96, j, :], m.K1[64:96, j, :])
                    ins.then_inc(s["latent_small"], 1)

                latent_small(0)
                augment(0)
                for k in range(len(JOBS)):
                    for u in range(JOB_UNITS[k]):
                        n = UNITS_BEFORE[k] + u
                        cols = SEQ if JOBS[k][1] == SELECTED else unit_cols(u)
                        act.wait_ge(s["scores"], n + 1)
                        act.activation(m.probs[:, k % 3, UNIT_AT[u]:UNIT_AT[u] + cols],
                                       m.ps[2 + n % 2][:, 0:cols], ACT.Exp, scale=scale
                                       ).then_inc(s["probs"], 1)
                    if k + 1 < len(JOBS):
                        augment(k + 1)
                    if k + 2 < len(JOBS) and JOBS[k + 2][1:] == (LATENT, 0):
                        latent_small(k + 2)
                    if k and ends_kind(k - 1):
                        take_num(k - 1)
                take_num(len(JOBS) - 1)

            @block.vector
            def _(dve):
                def rope(p):
                    kind, a, b = PREPS[p]
                    dve.wait_ge(s["prep"], p + 1)
                    bank = prep_bank(p)
                    if kind != "q" and a == LATENT:
                        for j in range(4):
                            ins = dve.tensor_copy(m.K1[64:96, j, :], bank[32 * j:32 * j + 32, :])
                        ins.then_inc(s["roped"], 1)
                        return
                    n = SWAPS_BEFORE[p]
                    if kind != "q" and a == SELECTED:
                        heads = lambda x: x.rearrange("p (h k) -> p h k", k=KEEP)
                        A = heads(bank[0:96, 0:P])
                        C, S = (m.t[c][:, 0:KEEP].unsqueeze(1).to_broadcast([rows, 4, KEEP])
                                for c, rows in (("rope_c", 96), ("rope_s", 64)))
                        to, tmp = heads(m.KS[0:96, :]), heads(m.R2[n % 2][0:96, 0:P])
                    else:
                        A, C, S = bank[0:96, :], m.t["rope_c"], m.t["rope_s"]
                        to = q_tile(a, b)[0:96, :] if kind == "q" else m.KW[0:96, b % 2, :]
                        tmp = m.R2[n % 2][0:96, :]
                    dve.tensor_tensor(to, A, C, ALU.mult).then_inc(s["plain"], 1)
                    if n >= 2:
                        dve.wait_ge(s["added"], n - 1)
                    dve.tensor_tensor(tmp[0:32], A[32:64], S[32:64], ALU.mult)
                    dve.tensor_tensor(tmp[32:64], A[0:32], S[0:32], ALU.mult).then_inc(s["roped"], 1)

                def largest(k):
                    g, x, j = JOBS[k]
                    if x == SELECTED:
                        dve.wait_ge(s["max_scores"], MAXES_BEFORE[k] + 1)
                        dve.tensor_reduce(m.NMm[:, :, :, 96:97].rearrange("p h t o -> p t (h o)"),
                                          m.ps[0][:].rearrange("p (t h k) -> p t h k", t=NT, h=4),
                                          AX.X, ALU.max, negate=True).then_inc(s["maxed"], 1)
                        return
                    for place, i in enumerate(FIRST_TILES):
                        dve.wait_ge(s["max_scores"], MAXES_BEFORE[k] + place + 1)
                        dve.tensor_reduce(m.NMm[:, 0, i, 96:97], m.ps[place % 2][:, 0:(i + 1) * P], AX.X,
                                          ALU.max, negate=True).then_inc(s["maxed"], 1)

                def take_den(k):
                    n = KINDS_BEFORE[k]
                    dve.wait_ge(s["numden"], n + 1)
                    if n >= 2:
                        dve.wait_ge(s["normed"], n - 1)
                    take_swapped(dve, m.dens[n % 2], m.ps[5], s["den_out"])

                def invert(k, half):
                    n = KINDS_BEFORE[k]
                    dve.wait_ge(s["den_out"], n + 1)
                    r = slice(256 * half, 256 * half + 256)
                    dve.reciprocal(m.dens[n % 2][:, r], m.dens[n % 2][:, r]).then_inc(s["rden"], 1)

                for tmp in m.R2:
                    dve.memset(tmp[64:96, :], 0.0)
                for p in range(FIRST_PREPS):
                    if p == 3:
                        largest(0)
                    rope(p)
                for k in range(len(JOBS)):
                    items = step_items(k)
                    if k + 1 < len(JOBS):
                        largest(k + 1)
                    for p in items[:1]:
                        rope(p)
                    if k >= 2 and ends_kind(k - 2):
                        invert(k - 2, 1)
                    if k and ends_kind(k - 1):
                        take_den(k - 1)
                        invert(k - 1, 0)
                    for p in items[1:]:
                        rope(p)
                invert(len(JOBS) - 2, 1)
                take_den(len(JOBS) - 1)
                dve.wait_ge(s["num_out"], 3 * NG)
                for half in range(2):
                    invert(len(JOBS) - 1, half)
                    r = slice(256 * half, 256 * half + 256)
                    dve.wait_ge(s["rden"], 6 * NG - 1 + half)
                    dve.tensor_tensor(m.nums[1][:, r], m.nums[1][:, r], m.dens[1][:, r], ALU.mult
                                      ).then_inc(s["last"], 1)
                dve.wait_ge(s["out_sum"], 1)
                dve.tensor_tensor(flat(m.X), flat(m.X), m.ps[0][:], ALU.add).then_inc(s["residual"], 1)

            @block.gpsimd
            def _(pool):
                def norm(k):
                    g, x, j = JOBS[k]
                    n = KINDS_BEFORE[k]
                    num, den = m.nums[n % 2], m.dens[n % 2]
                    pool.wait_ge(s["rden"], 2 * n + 2)
                    pool.wait_ge(s["num_out"], n + 1)
                    if x == LATENT:
                        pool.tensor_tensor(m.Aall[:, g, :], num, den, ALU.mult
                                           ).then_inc(s["normed"], 1)
                    else:
                        pool.tensor_tensor(num, num, den, ALU.mult).then_inc(s["part"], 1)
                        pool.wait_ge(s["part"], n - g)
                        pool.tensor_tensor(m.Aall[:, g, :], m.Aall[:, g, :], num, ALU.add
                                           ).then_inc(s["normed"], 1)
                    pool.wait_ge(s["normed"], n + 1)

                steps = [(step_items(k)[0] + 1) if step_items(k) else PREPS_UPTO[min(k, len(JOBS) - 1)]
                         for k in range(len(JOBS) + 1)]
                for p, (kind, a, b) in enumerate(PREPS):
                    while steps and steps[0] <= p:
                        k = len(PREPS_UPTO) + 1 - len(steps)
                        steps.pop(0)
                        if k >= 2 and ends_kind(k - 2):
                            pool.wait_ge(s["small"], SWAPS_BEFORE[p])
                            pool.wait_ge(s["added"], SWAPS_BEFORE[p])
                            norm(k - 2)
                    if kind != "q" and a == LATENT:
                        continue
                    pool.wait_ge(s["roped"], p + 1)
                    if kind == "q":
                        to, src = m.QB[0:96, 4 * (a % 2) + b, :], q_tile(a, b)[0:96, :]
                    elif a == WINDOW:
                        to, src = m.KWB[0:96, b % 2, :], m.KW[0:96, b % 2, :]
                    else:
                        to, src = m.KSB[0:96, :], m.KS[0:96, :]
                    n = SWAPS_BEFORE[p]
                    tmp = m.R2[n % 2][0:96, 0:src.shape[-1]]
                    pool.wait_ge(s["plain"], n + 1)
                    pool.tensor_tensor(to, src, tmp, ALU.add).then_inc(s["small"], 1)
                    pool.tensor_tensor(src, src, tmp, ALU.add).then_inc(s["added"], 1)
                pool.wait_ge(s["small"], SWAPS_BEFORE[-1] + 1)
                pool.wait_ge(s["added"], SWAPS_BEFORE[-1] + 1)
                for k in range(len(PREPS_UPTO) + 1 - len(steps), len(JOBS) + 1):
                    if ends_kind(k - 2):
                        norm(k - 2)
        retire(m, ctx, used)


def gated_attention(nc, m):
    b = Named()
    b.qT, b.kT = m.Q[:, 0, :], m.Q[:, 1, :]
    b.k, b.v, b.vbeta, b.vmean = (m.Q[:, 2 + n, :].rearrange("p (t c) -> p t c", t=NT) for n in range(4))
    b.logits, b.abs = m.B1, m.B2
    b.beta, b.logalpha = (m.PT[:, n, :].rearrange("p (t c) -> p t c", t=NT) for n in range(2))
    b.rep = m.hid[:, 0:2, :].rearrange("p n c -> p (n c)").rearrange("p (n c) -> p n c", n=8)
    b.decay, b.attn = m.hid[:, 2:4, :], m.hid[:, 4:6, :]
    b.state = m.PT[:, 2, 0:256].rearrange("p (c v) -> p c v", c=NT)
    scale = 64 ** -0.5
    with ExitStack() as ctx:
        s, used = sems(nc, ctx, "gla", LN_SEMS + "bcol heads heads_laid proj clipped copied absed exps logs "
                       "chain alpha_mean cum cum_laid curves rep decay_sum decay scores attn vbeta vmean "
                       "delta state intra_sum mem_sum residual")
        with nc.Block() as block:

            @block.sync
            def _(sp):
                clear_stale(sp, m)

            @block.tensor
            def _(pe):
                for t in range(NT):
                    pe.matmul(m.ps[3 + t][:], m.ones[0:1, 0:P], m.w["g_brow"], start=True, stop=False,
                              skip_group_check=True)
                ln_tensor(pe, m, s, 0)
                pe.wait_ge(s["ln_yt"], 1)
                for t in range(NT):
                    pe.matmul(m.ps[3 + t][:], m.YT[:, t * P:(t + 1) * P], m.w["g_wkvab"],
                              start=False, stop=True, skip_group_check=True).then_inc(s["proj"], 1)
                for k in range(2):
                    pe.matmul(m.ps[1 + k][:], m.w["g_wqk"][:, k * P:(k + 1) * P], m.YT[:],
                              start=True, stop=True).then_inc(s["heads"], 1)
                pe.wait_ge(s["alpha_mean"], 1)
                pe.matmul(m.ps[7][:, 0:8], m.t["upto"], m.own[:, 0:8], start=True, stop=True)
                pe.matmul(m.ps[7][:, 8:16], m.ones[:], m.own[:, 0:8], start=True, stop=True
                          ).then_inc(s["cum"], 1)
                pe.wait_ge(s["heads_laid"], 2)
                for h in range(2):
                    for c in range(NT):
                        r = slice(c * P, (c + 1) * P)
                        mm = pe.matmul(m.ps[1 + h][:, r], b.kT[64 * h:64 * h + 64, r],
                                       b.qT[64 * h:64 * h + 64, r], start=True, stop=True)
                    mm.then_inc(s["scores"], 1)
                pe.wait_ge(s["rep"], 1)
                pe.wait_ge(s["copied"], 2 * NT)
                for h in range(2):
                    for c in range(NT):
                        r = slice(c * P, (c + 1) * P)
                        pe.matmul(m.ps[3 + h][:, r], b.rep[:, 2 * c + h, :], m.t["upto"],
                                  start=(c == 0), stop=False, skip_group_check=True)
                        mm = pe.matmul(m.ps[3 + h][:, r], m.identb[:], m.mask_kq[:], start=False,
                                       stop=True, skip_group_check=True)
                    mm.then_inc(s["decay_sum"], 1)
                pe.wait_ge(s["vmean"], 1)
                for c in range(NT - 1):
                    mm = pe.matmul(m.ps[5][:, c * P:(c + 1) * P], b.k[:, c, :], b.vmean[:, c, :],
                                   start=True, stop=True)
                mm.then_inc(s["delta"], 1)
                pe.wait_ge(s["vbeta"], 1)
                pe.wait_ge(s["attn"], 2)
                for c in range(NT):
                    for h in range(2):
                        mm = pe.matmul(m.ps[6][:, c * P + 64 * h:c * P + 64 * h + 64],
                                       b.attn[:, h, c * P:(c + 1) * P],
                                       b.vbeta[:, c, 64 * h:64 * h + 64], start=True, stop=True)
                mm.then_inc(s["intra_sum"], 1)
                for c in range(1, NT):
                    pe.wait_ge(s["state"], 2 * c)
                    for h in range(2):
                        q = slice(64 * h, 64 * h + 64)
                        mm = pe.matmul(m.ps[7 * h][:, c * P + 64 * h:c * P + 64 * h + 64],
                                       b.qT[q, c * P:(c + 1) * P], b.state[q, c, :],
                                       start=True, stop=True)
                mm.then_inc(s["mem_sum"], 1)

            @block.scalar
            def _(act):
                ln_scalar(act, m, s)
                ln_copy(act, m, s, 0)
                act.wait_ge(s["clipped"], 2 * NT)
                act.activation(b.abs, b.logits, ACT.Abs).then_inc(s["absed"], 1)
                act.wait_ge(s["absed"], 1)
                act.activation(b.abs, b.abs, ACT.Exp, scale=-1.0).then_inc(s["exps"], 1)
                act.wait_ge(s["exps"], 1)
                act.activation(b.abs, b.abs, ACT.Ln, bias=1.0).then_inc(s["logs"], 1)
                for t in range(NT):
                    act.activation(b.k[:, t, :], m.ps[3 + t][:, 0:P], ACT.Copy, scale=scale
                                   ).then_inc(s["copied"], 1)
                    act.copy(b.v[:, t, :], m.ps[3 + t][:, P:256]).then_inc(s["copied"], 1)
                act.wait_ge(s["bcol"], 1)
                for k, to in enumerate((b.qT, b.kT)):
                    act.wait_ge(s["heads"], k + 1)
                    act.activation(to, m.ps[1 + k][:], ACT.Identity, scale=scale,
                                   bias=m.small[:, k:k + 1]).then_inc(s["heads_laid"], 1)
                act.wait_ge(s["cum_laid"], 1)
                act.activation(m.small[:, 32:48], m.small[:, 16:32], ACT.Exp).then_inc(s["curves"], 1)
                for h in range(2):
                    act.wait_ge(s["decay_sum"], h + 1)
                    for c in range(NT):
                        n = 2 * c + h
                        act.activation(b.decay[:, h, c * P:(c + 1) * P],
                                       m.ps[3 + h][:, c * P:(c + 1) * P], ACT.Exp,
                                       bias=m.small[:, 48 + n:49 + n]).then_inc(s["decay"], 1)

            @block.vector
            def _(dve):
                count = [0]

                def link(ins):
                    count[0] += 1
                    ins.then_inc(s["chain"], 1)
                    dve.wait_ge(s["chain"], count[0])

                dve.tensor_scalar(m.small[:, 0:2], m.w["g_bcol"], scale, None, ALU.mult
                                  ).then_inc(s["bcol"], 1)
                ln_vector(dve, m, s)
                for t in range(NT):
                    dve.wait_ge(s["proj"], t + 1)
                    dve.tensor_copy(b.logits[:, t, 0:P], m.ps[3 + t][:, 256:384]).then_inc(s["clipped"], 1)
                    dve.tensor_scalar(b.logits[:, t, P:256], m.ps[3 + t][:, 384:512], -10.0, 10.0,
                                      ALU.max, ALU.min).then_inc(s["clipped"], 1)
                dve.wait_ge(s["logs"], 1)
                link(dve.scalar_tensor_tensor(b.logalpha, b.logits[:, :, P:256], 0.0, b.abs[:, :, P:256],
                                              ALU.min, ALU.subtract))
                per_head = lambda x: x.rearrange("p t (h d) -> p t h d", h=2)
                sums = lambda x: x.rearrange("p (t h) -> p t h", h=2)
                link(dve.tensor_reduce(sums(m.own[:, 8:16]), per_head(b.logalpha), AX.X, ALU.add))
                dve.tensor_scalar(m.own[:, 0:8], m.own[:, 8:16], 1.0 / 64, None, ALU.mult
                                  ).then_inc(s["alpha_mean"], 1)
                dve.wait_ge(s["alpha_mean"], 1)
                dve.tensor_copy(b.rep, m.own[:, 0:8].unsqueeze(2).to_broadcast([P, 8, P])
                                ).then_inc(s["rep"], 1)
                link(dve.scalar_tensor_tensor(b.beta, b.logits[:, :, 0:P], 0.0, b.abs[:, :, 0:P],
                                              ALU.max, ALU.add))
                dve.wait_ge(s["cum"], 1)
                link(dve.tensor_copy(m.small[:, 16:32], m.ps[7][:, 0:16]))
                dve.tensor_scalar(m.small[:, 48:56], m.small[:, 16:24], -1.0, None, ALU.mult
                                  ).then_inc(s["cum_laid"], 1)
                link(dve.tensor_reduce(sums(m.own[:, 8:16]), per_head(b.beta), AX.X, ALU.add))
                link(dve.tensor_scalar(m.small[:, 8:16], m.own[:, 8:16], 1.0 / 64, None, ALU.mult))
                dve.wait_ge(s["copied"], 2 * NT)
                dve.tensor_tensor(per_head(b.vmean), per_head(b.v),
                                  sums(m.small[:, 8:16]).unsqueeze(3).to_broadcast([P, NT, 2, 64]),
                                  ALU.mult).then_inc(s["vmean"], 1)
                dve.tensor_tensor(b.vbeta, b.v, b.beta, ALU.mult).then_inc(s["vbeta"], 1)
                for h in range(2):
                    dve.wait_ge(s["decay"], NT * (h + 1))
                    dve.wait_ge(s["scores"], h + 1)
                    dve.tensor_tensor(b.attn[:, h, :], m.ps[1 + h][:], b.decay[:, h, :], ALU.mult
                                      ).then_inc(s["attn"], 1)
                dve.wait_ge(s["delta"], 1)
                dve.wait_ge(s["curves"], 1)
                for c in range(NT - 1):
                    for h in range(2):
                        q = slice(64 * h, 64 * h + 64)
                        new = m.ps[5][q, c * P + 64 * h:c * P + 64 * h + 64]
                        n = 2 * c + h
                        if c == 0:
                            dve.tensor_copy(b.state[q, 1, :], new).then_inc(s["state"], 1)
                        else:
                            dve.wait_ge(s["state"], n - 1)
                            dve.scalar_tensor_tensor(b.state[q, c + 1, :], b.state[q, c, :],
                                                     m.small[q, 40 + n:41 + n], new, ALU.mult, ALU.add
                                                     ).then_inc(s["state"], 1)
                dve.wait_ge(s["intra_sum"], 1)
                link(dve.tensor_tensor(flat(m.X), flat(m.X), m.ps[6][:], ALU.add))
                dve.wait_ge(s["mem_sum"], 1)
                for c in range(1, NT):
                    for h in range(2):
                        n, q = 2 * c + h, slice(64 * h, 64 * h + 64)
                        dve.scalar_tensor_tensor(m.X[:, c, q],
                                                 m.ps[7 * h][:, c * P + 64 * h:c * P + 64 * h + 64],
                                                 m.small[:, 32 + n:33 + n], m.X[:, c, q], ALU.mult,
                                                 ALU.add).then_inc(s["residual"], 1)
        retire(m, ctx, used)


ROUND = 12582912.0


def quantize(dve, link, src, dst, tmp, scales, columns):
    n = columns // 32
    blocks = lambda x: x.rearrange("p (n k) -> p n k", k=32)
    over = lambda x: x.unsqueeze(2).to_broadcast([P, n, 32])
    value, step, a, c = (t[:, 0:columns] for t in tmp)
    scale, inverse = scales[:, 0:n], scales[:, 16:16 + n]
    link(dve.tensor_reduce(scale, blocks(src), AX.X, ALU.max, apply_absolute_value=True))
    link(dve.tensor_scalar(scale, scale, 1.0 / 7.5, 1e-30, ALU.mult, ALU.max))
    link(dve.reciprocal(inverse, scale))
    link(dve.tensor_tensor(blocks(value), blocks(src), over(inverse), ALU.mult))
    link(dve.scalar_tensor_tensor(c, value, -1.0, value, ALU.mult, ALU.max))
    link(dve.tensor_scalar(step, c, 2.0, 0.125, ALU.is_ge, ALU.mult))
    link(dve.tensor_scalar(a, c, 4.0, 0.25, ALU.is_ge, ALU.mult))
    link(dve.scalar_tensor_tensor(step, a, 0.125, step, ALU.add, ALU.add))
    link(dve.scalar_tensor_tensor(a, step, ROUND, value, ALU.mult, ALU.add))
    link(dve.scalar_tensor_tensor(a, step, -ROUND, a, ALU.mult, ALU.add))
    link(dve.tensor_tensor(c, a, value, ALU.subtract))
    link(dve.scalar_tensor_tensor(c, step, 0.5, c, ALU.mult, ALU.is_le))
    link(dve.tensor_tensor(c, c, step, ALU.mult))
    link(dve.tensor_tensor(a, a, c, ALU.subtract))
    return dve.tensor_tensor(blocks(dst), blocks(a), over(scale), ALU.mult)


def quantize_weight(nc, m):
    with ExitStack() as ctx:
        s, used = sems(nc, ctx, "qw", "chain ready turned laid")
        with nc.Block() as block:

            @block.sync
            def _(sp):
                clear_stale(sp, m)

            @block.vector
            def _(dve):
                count = [0]

                def link(ins):
                    count[0] += 1
                    ins.then_inc(s["chain"], 1)
                    dve.wait_ge(s["chain"], count[0])

                quantize(dve, link, m.w["q_w"], m.R[:, 0:P], [m.PT[:, n, :] for n in range(4)],
                         m.small, P).then_inc(s["ready"], 1)

            @block.tensor
            def _(pe):
                pe.wait_ge(s["ready"], 1)
                pe.transpose(m.ps[0][:, 0:P], m.R[:, 0:P], m.ident).then_inc(s["turned"], 1)

            @block.scalar
            def _(act):
                act.wait_ge(s["turned"], 1)
                act.copy(m.WQT[:], m.ps[0][:, 0:P]).then_inc(s["laid"], 1)
        retire(m, ctx, used)


def quantized_linear(nc, m, sw=None, out_row=None):
    with ExitStack() as ctx:
        s, used = sems(nc, ctx, "fp6", LN_SEMS + "weights zeros chain ready turned laid out_sum residual x_out")
        with nc.Block() as block:

            @block.sync
            def _(sp):
                clear_stale(sp, m)
                if out_row is not None:
                    sp.wait_ge(s["residual"], 1)
                    sp.dma_start(out_row, m.X[:]).then_inc(s["x_out"], 16)
                    sp.wait_ge(s["x_out"], 16)
                if sw is not None:
                    sp.dma_start(m.big[:, 0:8 * 512], sw).then_inc(s["weights"], 16)
                    sp.wait_ge(s["weights"], 16)

            @block.gpsimd
            def _(pool):
                for j in range(2 if sw is not None else 0):
                    pool.memset(m.hid[64 - 64 * j:P - 64 * j, 8 + j:12:2, :], 0.0
                                ).then_inc(s["zeros"], 1)
                    pool.wait_ge(s["zeros"], j + 1)

            @block.vector
            def _(dve):
                count = [0]

                def link(ins):
                    count[0] += 1
                    ins.then_inc(s["chain"], 1)
                    dve.wait_ge(s["chain"], count[0])

                ln_vector(dve, m, s)
                dve.wait_ge(s["ln_y"], NT)
                quantize(dve, link, flat(m.Y), m.H.rearrange("p t d -> p (t d)"), [m.PT[:, n, :] for n in range(4)], m.small,
                         SEQ).then_inc(s["ready"], 1)
                dve.wait_ge(s["out_sum"], 1)
                dve.tensor_tensor(flat(m.X), flat(m.X), m.ps[1][:], ALU.add).then_inc(s["residual"], 1)

            @block.tensor
            def _(pe):
                for t in range(NT):
                    pe.matmul(m.ps[1][:, t * P:(t + 1) * P], m.ones[0:1, 0:P], m.w["q_brow"],
                              start=(t == 0), stop=False, skip_group_check=True)
                pe.wait_ge(s["ready"], 1)
                for t in range(NT):
                    mm = pe.transpose(m.ps[0][:, t * P:(t + 1) * P], m.H[:, t, :], m.ident)
                mm.then_inc(s["turned"], 1)
                pe.wait_ge(s["laid"], 1)
                for t in range(NT):
                    r = slice(t * P, (t + 1) * P)
                    mm = pe.matmul(m.ps[1][:, r], m.YT[:, r], m.WQT[:], start=False, stop=True,
                                   skip_group_check=True)
                mm.then_inc(s["out_sum"], 1)

            @block.scalar
            def _(act):
                ln_scalar(act, m, s)
                act.wait_ge(s["turned"], 1)
                act.copy(m.YT[:], m.ps[0][:]).then_inc(s["laid"], 1)
        retire(m, ctx, used)


SOFTCAP = 50.0
CAP_BANKS = [2, 3, 6, 7]


def capped_attention(nc, m):
    b = Named()
    b.w = m.hid[:, 0:8, :]
    b.q = [m.B1[:, t:t + 2, :].rearrange("p t c -> p (t c)") for t in (0, 2)]
    b.k = m.hid[:, 8:12, :]
    b.v = [m.PT[:, n, :].rearrange("p (t c) -> p t c", t=NT) for n in range(2)]
    b.gate = [m.PT[:, 2 + n, :] for n in range(2)]
    scale = 64 ** -0.5
    with ExitStack() as ctx:
        s, used = sems(nc, ctx, "cap", LN_SEMS + "qk qk_laid vg v_laid gate_laid scores tanhs probs "
                       "masked numden num_out den_out den rden normed out_sum residual")
        with nc.Block() as block:

            @block.sync
            def _(sp):
                clear_stale(sp, m)

            @block.tensor
            def _(pe):
                ln_tensor(pe, m, s, 2)
                pe.wait_ge(s["ln_yt"], 1)

                def project_qk(g):
                    if g:
                        pe.wait_ge(s["v_laid"], g)
                        pe.wait_ge(s["gate_laid"], g)
                    for k in range(2):
                        mm = pe.matmul(m.ps[k][:], b.w[:, g, k * P:(k + 1) * P], m.YT[:], start=True,
                                       stop=True)
                    mm.then_inc(s["qk"], 1)

                def project_vg(g):
                    pe.wait_ge(s["qk_laid"], 3 * g + 3)
                    for t in range(NT):
                        pe.matmul(m.ps[0][:, t * P:(t + 1) * P], m.YT[:, t * P:(t + 1) * P],
                                  b.w[:, g, 256:384], start=True, stop=True)
                    pe.matmul(m.ps[1][:], b.w[:, g, 384:512], m.YT[:], start=True, stop=True
                              ).then_inc(s["vg"], 1)

                def scores(n):
                    g = n // 2
                    for u in range(3):
                        if 3 * n + u >= 4:
                            pe.wait_ge(s["tanhs"], 3 * n + u - 3)
                        bank = m.ps[CAP_BANKS[(3 * n + u) % 4]]
                        for kt, at in UNITS[u]:
                            mm = pe.matmul(bank[:, at:at + WIDTH[kt]], b.k[:, n % 4, kt * P:(kt + 1) * P],
                                           b.q[g % 2][:, kt * P:SEQ], start=True, stop=True)
                        mm.then_inc(s["scores"], 1)

                def values(n):
                    g, j = divmod(n, 2)
                    pe.wait_ge(s["masked"], 2 * n + 2)
                    if j == 0 and g:
                        pe.wait_ge(s["num_out"], g)
                        pe.wait_ge(s["den_out"], g)
                    cols, others = slice(64 * j, 64 * j + 64), slice(64 - 64 * j, P - 64 * j)
                    mm = weigh_values(pe, m.probs[:, n % 3, :], lambda kt: b.v[g % 2][:, kt, cols],
                                      cols, others, m.ps[4], m.ps[5], m.ones[:, 0:64])
                    if j:
                        mm.then_inc(s["numden"], 1)

                project_qk(0)
                project_vg(0)
                for n in range(18):
                    if n < 16:
                        scores(n)
                    if n >= 2:
                        values(n - 2)
                    if n % 2 == 0 and n // 2 + 1 < 8:
                        project_qk(n // 2 + 1)
                    if n % 2 == 1 and n // 2 + 1 < 8:
                        project_vg(n // 2 + 1)
                for g in range(8):
                    pe.wait_ge(s["normed"], g + 1)
                    for t in range(NT):
                        mm = pe.matmul(m.ps[2][:, t * P:(t + 1) * P], m.Q[:, g, t * P:(t + 1) * P],
                                       m.w["s_wout"][:, g * P:(g + 1) * P], start=(g == 0 and t == 0),
                                       stop=(g == 7), skip_group_check=True)
                mm.then_inc(s["out_sum"], 1)

            @block.scalar
            def _(act):
                ln_scalar(act, m, s)
                ln_copy(act, m, s, 2)

                def gate(g):
                    act.wait_ge(s["vg"], g + 1)
                    if g >= 2:
                        act.wait_ge(s["den"], g - 1)
                    act.activation(b.gate[g % 2], m.ps[1][:], ACT.Exp, scale=-1.0
                                   ).then_inc(s["gate_laid"], 1)

                def exps(n):
                    act.wait_ge(s["tanhs"], 3 * n + 3)
                    act.activation(m.probs[:, n % 3, :], m.probs[:, n % 3, :], ACT.Exp, scale=SOFTCAP
                                   ).then_inc(s["probs"], 1)

                def take_num(g):
                    act.wait_ge(s["numden"], g + 1)
                    act.copy(m.Q[:, g, :], m.ps[4][:]).then_inc(s["num_out"], 1)

                for n in range(16):
                    if n % 2 == 0:
                        gate(n // 2)
                    for u in range(3):
                        act.wait_ge(s["scores"], 3 * n + u + 1)
                        act.activation(m.probs[:, n % 3, UNIT_AT[u]:UNIT_AT[u] + unit_cols(u)],
                                       m.ps[CAP_BANKS[(3 * n + u) % 4]][:, 0:unit_cols(u)], ACT.Tanh,
                                       scale=scale / SOFTCAP).then_inc(s["tanhs"], 1)
                    if n:
                        exps(n - 1)
                    if n >= 3 and n % 2:
                        take_num(n // 2 - 1)
                exps(15)
                take_num(7)

            @block.vector
            def _(dve):
                ln_vector(dve, m, s)

                def lay_qk(g):
                    dve.wait_ge(s["qk"], g + 1)
                    dve.tensor_copy(b.q[g % 2], m.ps[0][:]).then_inc(s["qk_laid"], 1)
                    for j in range(2):
                        r = slice(64 * j, 64 * j + 64)
                        dve.tensor_copy(b.k[r, 2 * (g % 2) + j, :], m.ps[1][r, :]).then_inc(s["qk_laid"], 1)

                def lay_v(g):
                    dve.wait_ge(s["vg"], g + 1)
                    dve.tensor_copy(b.v[g % 2].rearrange("p t c -> p (t c)"), m.ps[0][:]
                                    ).then_inc(s["v_laid"], 1)

                def mask(n):
                    dve.wait_ge(s["probs"], n + 1)
                    p = m.probs[:, n % 3, :]
                    three = m.probs_wide[:, n % 3, 0:3, 0:P]
                    upto = m.t["upto"]
                    dve.tensor_tensor(three, three, upto.unsqueeze(1).to_broadcast([P, 3, P]), ALU.mult
                                      ).then_inc(s["masked"], 1)
                    last = p[:, KEYS_AT[3]:KEYS_AT[3] + P]
                    dve.tensor_tensor(last, last, upto, ALU.mult).then_inc(s["masked"], 1)

                def take_den(g):
                    dve.wait_ge(s["numden"], g + 1)
                    take_swapped(dve, m.R, m.ps[5], s["den_out"])
                    dve.wait_ge(s["gate_laid"], g + 1)
                    dve.wait_ge(s["den_out"], g + 1)
                    dve.scalar_tensor_tensor(m.A[:], b.gate[g % 2], 1.0, m.R[:], ALU.add, ALU.mult
                                             ).then_inc(s["den"], 1)

                def norm(g):
                    dve.wait_ge(s["den"], g + 1)
                    dve.reciprocal(m.A[:], m.A[:]).then_inc(s["rden"], 1)
                    dve.wait_ge(s["rden"], g + 1)
                    dve.wait_ge(s["num_out"], g + 1)
                    dve.tensor_tensor(m.Q[:, g, :], m.Q[:, g, :], m.A[:], ALU.mult).then_inc(s["normed"], 1)

                lay_qk(0)
                lay_v(0)
                for n in range(19):
                    if 1 <= n <= 16:
                        mask(n - 1)
                    if n % 2 == 0 and n // 2 + 1 < 8:
                        lay_qk(n // 2 + 1)
                    if n >= 4 and n % 2 == 0:
                        norm(n // 2 - 2)
                    if n % 2 == 1 and n // 2 + 1 < 8:
                        lay_v(n // 2 + 1)
                    if n >= 3 and n % 2:
                        take_den(n // 2 - 1)
                dve.wait_ge(s["out_sum"], 1)
                dve.tensor_tensor(flat(m.X), flat(m.X), m.ps[2][:], ALU.add).then_inc(s["residual"], 1)
        retire(m, ctx, used)


def ffn(nc, m):
    ffn_attention(nc, m)
    experts(nc, m)


def batch_row(nc, m, x_row, out_row, m_weights, s_weights):
    linear_attention(nc, m, x_row)
    ffn(nc, m)
    mla_prepare(nc, m, m_weights)
    mla_heads(nc, m, m_weights)
    ffn(nc, m)
    gated_attention(nc, m)
    quantized_linear(nc, m, sw=s_weights)
    capped_attention(nc, m)
    quantized_linear(nc, m, out_row=out_row)
    clear(nc, m.to_clear)
    m.stale.close()


def more_memory(sb, m, b12):
    m.H = b12[:, 0:NT * P].rearrange("p (t c) -> p t c", t=NT)
    m.sq = sb("sq", [P, NT])
    m.hsum, m.hmean, m.hstd = sb("hsum", [P, NT, 32]), sb("hmean", [P, 128]), sb("hstd", [P, 128])
    m.QB = sb("QB", [P, 8, SEQ], BF16)
    m.KB = m.QB[:, NG:2 * NG, :]
    wide = sb("probs", [P, 3, 3, SEQ])
    m.probs_wide = wide
    m.probs = wide[:].rearrange("p h u c -> p h (u c)")[:, :, 0:HEAD_COLS]
    m.S = m.probs[:, 0, 0:768].rearrange("p (g c n) -> p g c n", g=2, c=3)
    m.Aall = sb("Aall", [P, NG, SEQ])
    m.g16, m.g16b, m.top = (sb(n, [P, 16]) for n in ("g16", "g16b", "top"))
    m.g64, m.g64b = (sb(n, [P, 64]) for n in ("g64", "g64b"))
    m.g4, m.g4b = (sb(n, [P, 4]) for n in ("g4", "g4b"))
    big = sb("big", [P, 15 * SEQ])
    m.big = big
    m.WQT = sb("WQT", [P, P])
    m.hid = big[:].rearrange("p (n c) -> p n c", c=SEQ)
    m.mw = big[:, 0:2 * M_COLS].rearrange("p (n c) -> p n c", c=M_COLS)
    m.K1, m.KW = sb("K1", [P, 4, SEQ]), sb("KW", [P, 2, SEQ])
    m.K1B, m.KWB = sb("K1B", [P, 4, SEQ], BF16), sb("KWB", [P, 2, SEQ], BF16)
    m.KS, m.KSB = sb("KS", [P, P]), sb("KSB", [P, P], BF16)
    m.V1 = b12[:].rearrange("p (t h d) -> p t h d", t=NT, h=16)
    m.VW = m.PT[:].rearrange("p j n -> p (j n)").rearrange("p (t h d) -> p t h d", t=NT, h=16)
    spare = 2 * M_COLS
    m.VS = big[:, spare:spare + 512].rearrange("p (g n) -> p g n", g=NG)
    m.NCT, m.imp, r2 = (big[:, spare + 512 * n:spare + 512 * n + 512] for n in (1, 2, 3))
    m.R2 = [r2, m.imp]
    m.nums, m.dens = ([own[:], big[:, spare + 512 * n:spare + 512 * n + 512]] for n, own in ((4, m.A), (5, m.R)))
    m.NMm = sb("NMm", [P, 4, NT, P], BF16)
    m.NM = m.NMm[:, 0:2, :, :]
    m.small, m.own, m.gates = sb("small", [P, 64]), sb("own", [P, 20]), sb("gates", [P, 3])
    m.SELT = wide[:, 2, 2, HEAD_COLS - 1024:HEAD_COLS - 1024 + P]
    m.H2, m.onehot = m.A[:, 0:P], m.Aall[:, 1, :].rearrange("p (t c) -> p t c", t=NT)


def program(nc, x, weights, tables, m_weights, s_weights, out):
    with ExitStack() as ctx:
        def sb(name, shape, dt=F32):
            return ctx.enter_context(nc.sbuf_tensor(name, shape, dt))

        m = Named()
        m.stale, m.to_clear = ExitStack(), []
        m.other_weights = ctx.enter_context(nc.semaphore("other_weights"))
        m.ps = [ctx.enter_context(nc.psum_tensor(f"bank{i}", [P, 512], F32)) for i in range(8)]
        m.w_all = sb("weights_sb", [P, W_COLS])
        m.t_all = sb("tables_sb", [P, T_COLS])
        m.w = {n: m.w_all[0:r, a:a + c] for n, (a, r, c) in W_AT.items()}
        m.t = {n: m.t_all[0:r, a:a + c] for n, (a, r, c) in T_AT.items()}
        m.ident = m.t["ident"]
        m.identb, m.mask_qk, m.mask_kq = (sb(n, [P, P], BF16) for n in ("identb", "maskqkb", "maskkqb"))
        m.ones = sb("ones", [P, P])
        m.X, m.Y = sb("X", [P, NT, P]), sb("Y", [P, NT, P])
        m.YT = sb("YT", [P, SEQ])
        m.stats, m.mv = sb("stats", [P, NT, 6]), sb("mv", [P, NT, 2])
        m.var, m.std, m.rstd = (sb(n, [P, NT]) for n in ("var", "std", "rstd"))
        m.Qp, m.Kp, m.Vp = (sb(n, [P, NT, 16, 32]) for n in ("Qp", "Kp", "Vp"))
        m.Q = sb("Q", [P, 2 * NG, SEQ])
        m.QTall, m.KTall = m.Q[:, 0:NG, :], m.Q[:, NG:2 * NG, :]
        b12 = sb("B12", [P, 2 * NT * 256])
        m.B1, m.B2 = (b12[:, 1024 * n:1024 * n + 1024].rearrange("p (t c) -> p t c", t=NT) for n in range(2))
        m.PT = sb("PT", [P, 4, SEQ])
        m.R, m.A = sb("R", [P, SEQ]), sb("A", [P, SEQ])
        more_memory(sb, m, b12)
        x_dram = x.rearrange("b (t p) d -> b p t d", p=P)
        out_dram = out.rearrange("b (t p) d -> b p t d", p=P)

        with ExitStack() as start:
            s, used = sems(nc, start, "load", "loaded set")
            with nc.Block() as block:

                @block.sync
                def _(sp):
                    sp.dma_start(m.w_all[:, 0:FIRST_COLS], weights[:, 0:FIRST_COLS]
                                 ).then_inc(s["loaded"], 16)
                    sp.dma_start(m.t_all[:], tables).then_inc(s["loaded"], 16)
                    sp.dma_start(m.w_all[:, FIRST_COLS:W_COLS], weights[:, FIRST_COLS:W_COLS]
                                 ).then_inc(m.other_weights, 16)

                @block.vector
                def _(dve):
                    dve.memset(m.Qp[:], 0.0)
                    dve.memset(m.Kp[:], 0.0)
                    dve.memset(m.Vp[:, :, :, 0:8], 0.0)
                    dve.memset(m.Vp[:, :, :, 8:9], 1.0)
                    dve.memset(m.Vp[:, :, :, 9:32], 0.0)
                    dve.memset(m.NMm[:], 0.0)
                    dve.memset(m.K1[96:97, :, :], 1.0)
                    dve.memset(m.KW[96:97, :, :], 1.0)
                    dve.memset(m.KS[96:97, :], 1.0)
                    dve.memset(m.ones[:], 1.0).then_inc(s["set"], 1)
                    dve.wait_ge(s["loaded"], 32)
                    dve.tensor_copy(m.identb[:], m.t["ident"])
                    dve.tensor_copy(m.mask_qk[:], m.t["mask_qk"])
                    dve.tensor_copy(m.mask_kq[:], m.t["mask_kq"]).then_inc(s["set"], 1)
            clear(nc, used)
        quantize_weight(nc, m)
        clear(nc, m.to_clear)
        m.stale.close()
        m.to_clear = []

        with nc.Fori(0, BATCH) as b:
            batch_row(nc, m, x_dram[bass.ds(b, 1)].rearrange("o p t d -> p (o t) d"),
                      out_dram[bass.ds(b, 1)].rearrange("o p t d -> p (o t) d"), m_weights, s_weights)


def pack(table, parts):
    at, cols = offsets(table)
    packed = np.zeros((P, cols), np.float32)
    for name, part in parts.items():
        off, r, c = at[name]
        packed[0:r, off:off + c] = part.reshape(r, c)
    return packed


def head_rows(w):
    out = np.zeros((NG, P, w.shape[1]), np.float32)
    for g in range(NG):
        for j in range(4):
            out[g, 32 * j:32 * j + 8] = w[8 * (4 * g + j):8 * (4 * g + j) + 8]
    return out.transpose(1, 0, 2).reshape(P, -1)


def halves(w):
    return np.concatenate([w[:P], w[P:]], axis=1)


def rope_order(w, heads):
    w = w.reshape(w.shape[0], heads, 96)
    return np.concatenate([w[:, :, 32:96], w[:, :, 0:32]], axis=2)


def column8(v):
    out = np.zeros((P, 1), np.float32)
    for j in range(4):
        out[32 * j:32 * j + 8, 0] = v
    return out


def tables():
    i = np.arange(P)
    k, q = i[:, None], i[None, :]
    angle = np.outer(np.arange(SEQ, dtype=np.float32),
                     (1.0 / np.float32(10000.0) ** (np.arange(0, 64, 2, dtype=np.float32) / np.float32(64)))
                     .astype(np.float32)).astype(np.float32)
    cos, sin = np.cos(angle).T, np.sin(angle).T
    one = np.ones((32, SEQ), np.float32)
    e = np.arange(4)
    return pack(TABLES, {
        "ident": np.eye(P), "mask_qk": np.where(q > k, NEG, 0.0), "mask_kq": np.where(q < k, NEG, 0.0),
        "upto": k <= q, "before": k < q, "block": (k // 32) == (q // 32),
        "spread8": k == 32 * (q // 32) + 8,
        "rope_c": np.concatenate([cos, cos, one]), "rope_s": np.concatenate([sin, -sin]),
        "below": q < k,
        "iota": np.tile(np.arange(32), (P, 1)),
        "lower4": np.tile((e[None, :] < e[:, None]).reshape(1, 16), (P, 1)),
        "aug8": i % 32 == 8, "aug3": i[:, None] - 96 == np.arange(3)[None, :],
    })


def kernel(**inputs):
    import concourse.bacc as bacc
    from concourse.bass_utils import run_bass_kernel_spmd

    nc = bacc.Bacc("TRN2", target_bir_lowering=False, num_devices=1)
    arrays, args = {}, []
    for name, a in host_arrays(**inputs).items():
        arrays[name] = np.ascontiguousarray(a)
        args.append(nc.dram_tensor(name, a.shape, F32, kind="ExternalInput").ap())
    args.append(nc.dram_tensor("out", (BATCH, SEQ, D), F32, kind="ExternalOutput").ap())
    program(nc, *args)
    return run_bass_kernel_spmd(nc, [arrays], core_ids=[0]).results[0]["out"]


def host_arrays(**inputs):
    v = {n: np.asarray(a) for n, a in inputs.items()}
    a = {n[len("L0_attn_a_"):]: x for n, x in v.items() if n.startswith("L0_attn_a_")}
    f = {n[len("L0_ffn_"):]: x for n, x in v.items() if n.startswith("L0_ffn_")}
    b = {n[len("L0_attn_b_"):]: x for n, x in v.items() if n.startswith("L0_attn_b_")}
    g = {n[len("L1_attn_a_"):]: x for n, x in v.items() if n.startswith("L1_attn_a_")}
    h = {n[len("L1_attn_b_"):]: x for n, x in v.items() if n.startswith("L1_attn_b_")}
    side = lambda *ws: np.concatenate(ws, axis=1)
    weights = pack(WEIGHTS, {
        "a_wqkv": side(a["Wq"].T, a["Wk"].T, a["Wv"].T), "a_wo": head_rows(a["Wo"].T),
        "a_brow": np.concatenate([a["bq"], a["bk"], a["bv"], a["bo"]]),
        "f_wqkv": side(f["wq"].T, f["wk"].T, f["wv"].T), "f_wo": head_rows(f["wo"].T),
        "f_n1": f["n1_w"], "f_n2": f["n2_w"], "f_qn": column8(f["qn_w"]), "f_kn": column8(f["kn_w"]),
        "f_gate": f["gate_w"].T, "f_e0_up": f["e0_up"].T, "f_e0_dn": halves(f["e0_down"].T),
        "f_e1_w1": f["e1_w1"].T, "f_e1_w2": f["e1_w2"].T, "f_e1_dn": halves(f["e1_down"].T),
        "f_e2_l1": f["e2_l1"].T, "f_e2_l2": halves(f["e2_l2"].T), "f_e2_l3": halves(f["e2_l3"].T),
        "f_e2_l4": halves(f["e2_l4"].T), "f_e3_dn": f["e3_down"].T, "f_e3_up": f["e3_up"].T,
        "f_e3_out": halves(f["e3_out"].T),
        "m_cq": b["w_cq"], "m_ckv": b["w_ckv"], "m_krope": b["w_krope"],
        "m_imp": np.tile(b["w_imp"], (1, P)), "m_gate": b["w_gate"], "m_gqkv": np.concatenate([b["g_qnorm"], b["g_kvnorm"]]),
        "m_dv": np.concatenate([np.zeros((96, 512), np.float32), b["w_dv"]]), "m_selv": b["w_selv"], "m_winv": b["w_winv"],
        "m_proj": b["w_proj"].reshape(NG, P, D).transpose(1, 0, 2),
        "g_wqk": side(g["Wq"].T, g["Wk"].T),
        "g_wkvab": side(g["Wk"].T, g["Wv"].T, g["Wbeta"].T, g["Walpha"].T),
        "g_bcol": np.stack([g["bq"], g["bk"]], axis=1),
        "g_brow": np.concatenate([g["bk"], g["bv"], g["bbeta"], g["balpha"]]),
        "s_wout": h["w_out"].reshape(8, P, D).transpose(1, 0, 2),
        "q_w": v["L1_ffn_weight"], "q_brow": v["L1_ffn_bias"],
    })
    m_weights = np.zeros((NG, P, M_COLS), np.float32)
    nope = np.concatenate([b["w_dq_rope"].reshape(96, 16, 64), b["w_dq_nope"].reshape(96, 16, 32)], axis=2)
    win, sel = rope_order(b["w_wink"], 16), rope_order(b["w_selk"], 16)
    for grp in range(NG):
        hs = slice(4 * grp, 4 * grp + 4)
        m_weights[grp, 96:P, 3 * 384:] = b["w_dk_nope"][:, 128 * grp:128 * grp + 128]
        for n, w in enumerate((nope, win, sel)):
            m_weights[grp, 0:w.shape[0], 384 * n:384 * n + 384] = w[:, hs].reshape(w.shape[0], 384)
    qkv = np.concatenate([h["w_qkv"].reshape(P, 3, 8, P),
                          np.repeat(h["w_gates"], 64, axis=1).reshape(P, 1, 8, P)], axis=1)
    s_weights = qkv.transpose(0, 2, 1, 3).reshape(P, 8 * 512)
    return {"x": v["L0_attn_a_x"], "weights": weights, "tables": tables(), "m_weights": m_weights,
            "s_weights": s_weights}
```
